# Optimizing a Trainium2 kernel written in Bass

```python
import numpy as np
import jax
import jax.numpy as jnp

def _softmax(x, axis=-1):
    return jax.nn.softmax(x, axis=axis)

def _gelu(x):
    return jax.nn.gelu(x, approximate=True)

def _silu(x):
    return jax.nn.silu(x)

def _sigmoid(x):
    return jax.nn.sigmoid(x)

def _layernorm(x, axis=-1, eps=1e-05):
    m = jnp.mean(x, axis=axis, keepdims=True)
    v = jnp.var(x, axis=axis, keepdims=True)
    return (x - m) / jnp.sqrt(v + eps)

def _scatter_add(tgt, idx, src, axis=0):
    return tgt.at[idx].add(src)

def _segment_sum(src, seg, n):
    return jax.ops.segment_sum(src, seg, n)
kernel_name = 'mk_seq_postln_d2_jaxref_r8_4b488f'

def setup_inputs(seed: int=0):
    np.random.seed(seed)
    _w = jnp.asarray

    def _L0_attn_setup():
        import jax, jax.numpy as jnp
        import numpy as np
        B, N, D = (4, 512, 128)
        H, DH = (16, 64)
        EPS = 1e-06
        key = jax.random.key(seed)
        ks = jax.random.split(key, 6)
        s = 1.0 / np.sqrt(D)
        return {'x': jax.random.normal(ks[0], (B, N, D), dtype=jnp.float32), 'Wq': jax.random.normal(ks[1], (D, H * DH), dtype=jnp.float32) * s, 'Wk': jax.random.normal(ks[2], (D, H * DH), dtype=jnp.float32) * s, 'Wv': jax.random.normal(ks[3], (D, H * DH), dtype=jnp.float32) * s, 'Wo': jax.random.normal(ks[4], (H * DH, D), dtype=jnp.float32) * s, 'bo': jnp.zeros((D,), dtype=jnp.float32)}
    _L0_attn_in = _L0_attn_setup()

    def _L0_ffn_setup():
        import jax, jax.numpy as jnp
        import numpy as np
        B, T, D, H, E, K = (2, 128, 128, 16, 8, 2)
        HS = D // H
        FF = 4 * D

        def layernorm(x, g, b, eps=1e-05):
            m = jnp.mean(x, axis=-1, keepdims=True)
            v = jnp.mean((x - m) ** 2, axis=-1, keepdims=True)
            return (x - m) * jax.lax.rsqrt(v + eps) * g + b
        key = jax.random.key(seed)
        ks = jax.random.split(key, 10)
        s = 0.02
        return {'x': jax.random.normal(ks[0], (B, T, D), jnp.float32), 'Wq': jax.random.normal(ks[1], (H, D, HS), jnp.float32) * s, 'Wk': jax.random.normal(ks[2], (H, D, HS), jnp.float32) * s, 'Wv': jax.random.normal(ks[3], (H, D, HS), jnp.float32) * s, 'gate_W': jax.random.normal(ks[4], (D, E), jnp.float32) * s, 'W1': jax.random.normal(ks[5], (E, D, FF), jnp.float32) * s, 'b1': jnp.zeros((E, FF), jnp.float32), 'W2': jax.random.normal(ks[6], (E, FF, D), jnp.float32) * s, 'b2': jnp.zeros((E, D), jnp.float32), 'ln1_g': jnp.ones((D,), jnp.float32), 'ln1_b': jnp.zeros((D,), jnp.float32), 'ln2_g': jnp.ones((D,), jnp.float32), 'ln2_b': jnp.zeros((D,), jnp.float32)}
    _L0_ffn_in = _L0_ffn_setup()

    def _L1_attn_setup():
        import jax, jax.numpy as jnp
        import numpy as np
        B, T, DIM = (2, 128, 128)
        H, D = (16, 64)
        key = jax.random.key(seed)
        k1, k2, k3, k4 = jax.random.split(key, 4)
        s = DIM ** (-0.5)
        return {'x': jax.random.normal(k1, (B, T, DIM), jnp.float32), 'w_qkv': jax.random.normal(k2, (DIM, 3 * H * D), jnp.float32) * s, 'w_gate': jax.random.normal(k3, (DIM, H * D), jnp.float32) * s, 'w_out': jax.random.normal(k4, (H * D, DIM), jnp.float32) * s}
    _L1_attn_in = _L1_attn_setup()

    def _L1_ffn_setup():
        import jax, jax.numpy as jnp
        import numpy as np
        EMB = 128
        FF = 4 * EMB

        def _ternary(w):
            scale = jnp.maximum(jnp.mean(jnp.abs(w)), 1e-08)
            w_t = jnp.clip(jnp.round(w / scale), -1.0, 1.0)
            return w + jax.lax.stop_gradient(w_t - w)
        key = jax.random.key(seed)
        kx, k1, k2, kb1, kb2 = jax.random.split(key, 5)
        x = jax.random.normal(kx, (4, 256, EMB), dtype=jnp.float32)
        lim1 = 1.0 / np.sqrt(EMB)
        lim2 = 1.0 / np.sqrt(FF)
        W1 = jax.random.uniform(k1, (FF, EMB), jnp.float32, -lim1, lim1)
        b1 = jax.random.uniform(kb1, (FF,), jnp.float32, -lim1, lim1)
        W2 = jax.random.uniform(k2, (EMB, FF), jnp.float32, -lim2, lim2)
        b2 = jax.random.uniform(kb2, (EMB,), jnp.float32, -lim2, lim2)
        return {'x': x, 'W1': W1, 'b1': b1, 'W2': W2, 'b2': b2}
    _L1_ffn_in = _L1_ffn_setup()
    _d = {'L0_attn_x': _L0_attn_in['x'], 'L0_attn_Wq': _L0_attn_in['Wq'], 'L0_attn_Wk': _L0_attn_in['Wk'], 'L0_attn_Wv': _L0_attn_in['Wv'], 'L0_attn_Wo': _L0_attn_in['Wo'], 'L0_attn_bo': _L0_attn_in['bo'], 'L0_ffn_Wq': _L0_ffn_in['Wq'], 'L0_ffn_Wk': _L0_ffn_in['Wk'], 'L0_ffn_Wv': _L0_ffn_in['Wv'], 'L0_ffn_gate_W': _L0_ffn_in['gate_W'], 'L0_ffn_W1': _L0_ffn_in['W1'], 'L0_ffn_b1': _L0_ffn_in['b1'], 'L0_ffn_W2': _L0_ffn_in['W2'], 'L0_ffn_b2': _L0_ffn_in['b2'], 'L0_ffn_ln1_g': _L0_ffn_in['ln1_g'], 'L0_ffn_ln1_b': _L0_ffn_in['ln1_b'], 'L0_ffn_ln2_g': _L0_ffn_in['ln2_g'], 'L0_ffn_ln2_b': _L0_ffn_in['ln2_b'], 'L1_attn_w_qkv': _L1_attn_in['w_qkv'], 'L1_attn_w_gate': _L1_attn_in['w_gate'], 'L1_attn_w_out': _L1_attn_in['w_out'], 'L1_ffn_W1': _L1_ffn_in['W1'], 'L1_ffn_b1': _L1_ffn_in['b1'], 'L1_ffn_W2': _L1_ffn_in['W2'], 'L1_ffn_b2': _L1_ffn_in['b2']}
    _x0 = _d['L0_attn_x']
    _d['L0_attn_x'] = jax.random.normal(jax.random.fold_in(jax.random.key(seed), 1), (16, 256, 128), dtype=_x0.dtype)
    del _x0
    return _d

def reference(L0_attn_x, L0_attn_Wq, L0_attn_Wk, L0_attn_Wv, L0_attn_Wo, L0_attn_bo, L0_ffn_Wq, L0_ffn_Wk, L0_ffn_Wv, L0_ffn_gate_W, L0_ffn_W1, L0_ffn_b1, L0_ffn_W2, L0_ffn_b2, L0_ffn_ln1_g, L0_ffn_ln1_b, L0_ffn_ln2_g, L0_ffn_ln2_b, L1_attn_w_qkv, L1_attn_w_gate, L1_attn_w_out, L1_ffn_W1, L1_ffn_b1, L1_ffn_W2, L1_ffn_b2):

    def _L0_attn_ref(x, Wq, Wk, Wv, Wo, bo):
        import jax, jax.numpy as jnp
        import numpy as np
        B, N, D = (4, 512, 128)
        H, DH = (16, 64)
        EPS = 1e-06

        def split_heads(t):
            b, n, _ = t.shape
            return t.reshape(b, n, H, DH).transpose(0, 2, 1, 3)
        q = split_heads(x @ Wq)
        k = split_heads(x @ Wk)
        v = split_heads(x @ Wv)
        q = jax.nn.elu(q) + 1.0
        k = jax.nn.elu(k) + 1.0
        k_sum = k.sum(axis=2)
        z = jnp.einsum('bhnd,bhd->bhn', q, k_sum)[..., None] + EPS
        kv = jnp.einsum('bhnd,bhne->bhde', k, v)
        out = jnp.einsum('bhnd,bhde->bhne', q, kv) / z
        out = out.transpose(0, 2, 1, 3).reshape(x.shape[0], x.shape[1], H * DH)
        return out @ Wo + bo

    def _L0_ffn_ref(x, Wq, Wk, Wv, gate_W, W1, b1, W2, b2, ln1_g, ln1_b, ln2_g, ln2_b):
        import jax, jax.numpy as jnp
        import numpy as np
        B, T, D, H, E, K = (2, 128, 128, 16, 8, 2)
        HS = D // H
        FF = 4 * D

        def layernorm(x, g, b, eps=1e-05):
            m = jnp.mean(x, axis=-1, keepdims=True)
            v = jnp.mean((x - m) ** 2, axis=-1, keepdims=True)
            return (x - m) * jax.lax.rsqrt(v + eps) * g + b
        b, t, d = x.shape
        q = jnp.einsum('btd,hdf->bhtf', x, Wq)
        k = jnp.einsum('btd,hdf->bhtf', x, Wk)
        v = jnp.einsum('btd,hdf->bhtf', x, Wv)
        wei = jnp.einsum('bhtf,bhsf->bhts', q, k) * d ** (-0.5)
        mask = jnp.tril(jnp.ones((t, t), bool))
        wei = jnp.where(mask, wei, -jnp.inf)
        wei = jax.nn.softmax(wei, axis=-1)
        attn = jnp.einsum('bhts,bhsf->bhtf', wei, v)
        attn = attn.transpose(0, 2, 1, 3).reshape(b, t, d)
        y = x + layernorm(attn, ln1_g, ln1_b)
        flat = y.reshape(-1, d)
        logits = flat @ gate_W
        topv, topi = jax.lax.top_k(logits, K)
        w = jax.nn.softmax(topv, axis=-1)
        combine = jnp.sum(jax.nn.one_hot(topi, E, dtype=flat.dtype) * w[..., None], axis=1)
        h = jax.nn.relu(jnp.einsum('nd,edf->enf', flat, W1) + b1[:, None, :])
        eo = jnp.einsum('enf,efd->end', h, W2) + b2[:, None, :]
        moe = jnp.einsum('ne,end->nd', combine, eo)
        out = y + layernorm(moe.reshape(b, t, d), ln2_g, ln2_b)
        return out

    def _L1_attn_ref(x, w_qkv, w_gate, w_out):
        import jax, jax.numpy as jnp
        import numpy as np
        B, T, DIM = (2, 128, 128)
        H, D = (16, 64)
        b, t, c = x.shape
        qkv = (x @ w_qkv).reshape(b, t, 3, H, D)
        q, k, v = (qkv[:, :, 0], qkv[:, :, 1], qkv[:, :, 2])
        gate = jax.nn.sigmoid((x @ w_gate).reshape(b, t, H, D))
        q = jax.nn.elu(q) + 1.0
        k = jax.nn.elu(k) + 1.0
        k_cum = jnp.cumsum(k, axis=1)
        kv = jnp.cumsum(k[..., None, :] * v[..., :, None], axis=1)
        numerator = jnp.einsum('bthj,bthij->bthi', q, kv)
        denominator = jnp.einsum('bthj,bthj->bth', q, k_cum)
        out = numerator / (denominator[..., None] + 1e-06)
        out = out * gate
        return out.reshape(b, t, H * D) @ w_out

    def _L1_ffn_ref(x, W1, b1, W2, b2):
        import jax, jax.numpy as jnp
        import numpy as np
        EMB = 128
        FF = 4 * EMB

        def _ternary(w):
            scale = jnp.maximum(jnp.mean(jnp.abs(w)), 1e-08)
            w_t = jnp.clip(jnp.round(w / scale), -1.0, 1.0)
            return w + jax.lax.stop_gradient(w_t - w)
        h = jnp.einsum('bsd,fd->bsf', x, _ternary(W1)) + b1
        h = jax.nn.gelu(h, approximate=False)
        out = jnp.einsum('bsf,df->bsd', h, _ternary(W2)) + b2
        return out
    x = L0_attn_x
    x = _layernorm(x + _L0_attn_ref(x, L0_attn_Wq, L0_attn_Wk, L0_attn_Wv, L0_attn_Wo, L0_attn_bo), axis=-1)
    x = _layernorm(x + _L0_ffn_ref(x, L0_ffn_Wq, L0_ffn_Wk, L0_ffn_Wv, L0_ffn_gate_W, L0_ffn_W1, L0_ffn_b1, L0_ffn_W2, L0_ffn_b2, L0_ffn_ln1_g, L0_ffn_ln1_b, L0_ffn_ln2_g, L0_ffn_ln2_b), axis=-1)
    x = _layernorm(x + _L1_attn_ref(x, L1_attn_w_qkv, L1_attn_w_gate, L1_attn_w_out), axis=-1)
    x = _layernorm(x + _L1_ffn_ref(x, L1_ffn_W1, L1_ffn_b1, L1_ffn_W2, L1_ffn_b2), axis=-1)
    return x

_drawn_inputs = setup_inputs


def setup_inputs(seed=0):
    import zlib

    import numpy as np

    out = dict(_drawn_inputs(seed))
    spreads = {'L0_attn_bo': (0.0, 0.1),
     'L0_ffn_b1': (0.0, 0.1),
     'L0_ffn_b2': (0.0, 0.1),
     'L0_ffn_ln1_g': (1.0, 0.2),
     'L0_ffn_ln1_b': (0.0, 0.1),
     'L0_ffn_ln2_g': (1.0, 0.2),
     'L0_ffn_ln2_b': (0.0, 0.1)}
    factors = {'L0_ffn_Wq': 2.832, 'L1_ffn_b1': 8.0, 'L1_ffn_b2': 200.0}
    for name, (base, spread) in spreads.items():
        noise = np.random.default_rng([zlib.crc32(name.encode()), seed]).standard_normal(out[name].shape)
        drawn = base * np.exp(spread * noise) if base else spread * noise
        out[name] = jnp.asarray(drawn.astype(out[name].dtype))
    for name, factor in factors.items():
        out[name] = (out[name] * factor).astype(out[name].dtype)
    return out
```

```python
from contextlib import ExitStack

import concourse.bass as bass
from concourse import mybir

F32 = mybir.dt.float32
BF16 = mybir.dt.bfloat16
U32 = mybir.dt.uint32
ALU = mybir.AluOpType
ACT = mybir.ActivationFunctionType
AX_X = mybir.AxisListType.X
ds = bass.ds

P = 128
BANK = 512
B, N, D = 16, 256, 128
TT = N // P
TILES = B * TT
H, DH = 16, 64
PAIRS = H // 2
HD = H * DH
LN_EPS = 1e-5


class Count:

    def __init__(self, turn, per_turn):
        self.base, self.per_turn, self.n = turn * per_turn, per_turn, 0

    def next(self):
        self.n += 1
        return self.base + self.n

    def close(self):
        assert self.n == self.per_turn, (self.n, self.per_turn)


class Chip:

    def __init__(self, nc, stack):
        self.nc, self.stack = nc, stack

    def sb(self, name, shape, dt=F32):
        return self.stack.enter_context(self.nc.sbuf_tensor(name, shape, dt))

    def ps(self, name, shape, dt=F32):
        return self.stack.enter_context(self.nc.psum_tensor(name, shape, dt))

    def sem(self, name):
        return self.stack.enter_context(self.nc.semaphore(name))



def layernorm_rows(dve, nc, steps, dve_step, rows, stats, mv, rstd, var_ready, rstd_ready, rounds, out, tiles):
    for t in range(tiles):
        nc.vector.bn_stats(stats[:, t, :], rows[:, t, :])
    dve.drain()
    for t in range(tiles):
        ins = nc.vector.bn_aggr(mv[:, t, :], stats[:, t, :])
    ins.then_inc(dve_step, 1)
    dve.wait_ge(dve_step, steps.next())
    nc.vector.tensor_scalar(mv[:, :, 1], mv[:, :, 1], LN_EPS, None, ALU.add).then_inc(var_ready, 1)
    dve.wait_ge(rstd_ready, rounds)
    for t in range(tiles):
        last = nc.vector.tensor_scalar(out(t), rows[:, t, :], mv[:, t, 0:1], rstd[:, t:t + 1],
                                       ALU.subtract, ALU.mult)
    return last


def stage_a(nc, c, x_dram, x_all, w, ident, ones_row, mhalf, consts_ready):
    VB = 2 * DH + 2
    RING = 3
    PROJ = 2 * TT * (HD // BANK) + PAIRS // 2
    FEAT = PROJ - TT * (HD // BANK)
    KVG = [(0, 2), (2, 4), (4, 6), (6, 8)]
    APG = [(0, 3), (3, 6), (6, 8)]
    MIX = len(KVG) + TT * len(APG)
    TPU = TT + 2 * TT
    assert PROJ % RING == 0 and MIX % 2 == 0 and TPU % 2 == 0

    x_in = c.sb("a_x_in", [P, TT, D])
    xT = c.sb("a_xT", [P, N])
    k = c.sb("a_k", [P, TT, HD])
    v = c.sb("a_v", [P, TT, PAIRS, VB])
    qT = c.sb("a_qT", [P, PAIRS, N])
    kv = c.sb("a_kv", [P, PAIRS, VB])
    ex = c.sb("a_exp", [P, 2, BANK])
    re = c.sb("a_relu", [P, 2, BANK])
    den = c.sb("a_den", [P, MIX, 6])
    rden = c.sb("a_rden", [P, MIX, 6])
    on = c.sb("a_on", [P, TT, HD])
    onT = c.sb("a_onT", [P, TT, PAIRS, P])
    rows = c.sb("a_rows", [P, TT, D])
    stats = c.sb("a_stats", [P, TT, 6])
    mv = c.sb("a_mv", [P, TT, 2])
    rstd = c.sb("a_rstd", [P, TT])
    ps_proj = [c.ps(f"a_ps_proj{j}", [P, BANK]) for j in range(RING)]
    ps_mix = [c.ps(f"a_ps_mix{j}", [P, BANK]) for j in range(2)]
    ps_tp = [c.ps(f"a_ps_tp{j}", [P, BANK]) for j in range(2)]
    ps_out = c.ps("a_ps_out", [P, TT, D])

    x_in_ready = c.sem("a_x_in_ready")
    x_turned = c.sem("a_x_turned")
    x_all_ready = c.sem("a_x_all_ready")
    slots_set = c.sem("a_slots_set")
    proj_ready = c.sem("a_proj_ready")
    proj_free = c.sem("a_proj_free")
    feat_free = c.sem("a_feat_free")
    mix_ready = c.sem("a_mix_ready")
    mix_free = c.sem("a_mix_free")
    tp_ready = c.sem("a_tp_ready")
    tp_free = c.sem("a_tp_free")
    out_ready = c.sem("a_out_ready")
    out_used = c.sem("a_out_used")
    dve_step = c.sem("a_dve_step")
    var_ready = c.sem("a_var_ready")
    rstd_ready = c.sem("a_rstd_ready")

    with nc.Block() as block:

        @block.sync
        def _(sp):
            sp.dma_start(x_all[:, :, :], x_dram.rearrange("(t p) d -> p t d", p=P)).then_inc(x_all_ready, 16)
            with sp.Fori(0, B) as i:
                sp.wait_ge(x_turned, i + 1)
                sp.dma_start(x_in[:, :, :], x_dram[ds(i * N, N), :].rearrange("(t p) d -> p t d", p=P))\
                  .then_inc(x_in_ready, 16)

        @block.gpsimd
        def _(pool):
            nc.gpsimd.memset(kv[:, :, :], 0.0).then_inc(slots_set, 1)
            nc.gpsimd.memset(v[:, :, :, 0:1], 1.0).then_inc(slots_set, 1)
            nc.gpsimd.memset(v[:, :, :, VB - 1:VB], 1.0).then_inc(slots_set, 1)
            with pool.Fori(0, B) as i:
                pool.wait_ge(var_ready, i + 1)
                nc.gpsimd.tensor_tensor(rstd[:, :], mv[:, :, 1], mhalf[:, 0:TT], ALU.pow).then_inc(rstd_ready, 1)

        @block.tensor
        def _(pe):
            pe.wait_ge(consts_ready, CONSTS)
            pe.wait_ge(slots_set, 3)
            pe.sem_inc(x_turned, 1)
            with pe.Fori(0, B) as i:
                def tp_unit(n):
                    pe.wait_ge(tp_free, i * TPU + n + 1)
                    return ps_tp[n % 2]

                pe.wait_ge(x_in_ready, i * 16 + 16)
                for t in range(TT):
                    last = nc.tensor.transpose(tp_unit(t)[:, 0:P], x_in[:, t, :], ident[:, :])
                    last.then_inc(tp_ready, 1)
                pe.wait_ge(tp_ready, i * TPU + TT)
                pe.sem_inc(x_turned, 1)
                pe.wait_ge(tp_free, 2 + i * TPU + TT)
                n = 0
                for name in ("k", "v"):
                    if name == "k":
                        pe.wait_ge(w["A_ready"], 16 * 5)
                    for t in range(TT):
                        for h in range(HD // BANK):
                            pe.wait_ge(proj_free, i * PROJ + n + 1)
                            nc.tensor.matmul(ps_proj[n % RING][:, :], xT[:, t * P:(t + 1) * P],
                                             w["A_" + name][:, h * BANK:(h + 1) * BANK],
                                             start=True, stop=True).then_inc(proj_ready, 1)
                            n += 1
                for g in range(PAIRS // 2):
                    pe.wait_ge(proj_free, i * PROJ + n + 1)
                    for s in range(2):
                        m = 2 * g + s
                        last = nc.tensor.matmul(ps_proj[n % RING][:, s * N:(s + 1) * N],
                                                w["A_q"][:, m * P:(m + 1) * P], xT[:, :], start=True, stop=True)
                    last.then_inc(proj_ready, 1)
                    n += 1
                pe.wait_ge(feat_free, 2 + i * FEAT + TT * (HD // BANK))
                pe.wait_ge(proj_free, RING + i * PROJ + 2 * TT * (HD // BANK))
                for n, (m0, m1) in enumerate(KVG):
                    pe.wait_ge(mix_free, i * MIX + n + 1)
                    for m in range(m0, m1):
                        for t in range(TT):
                            last = nc.tensor.matmul(ps_mix[n % 2][:, (m - m0) * VB:(m - m0 + 1) * VB],
                                                    k[:, t, m * P:(m + 1) * P], v[:, t, m, :],
                                                    start=(t == 0), stop=(t == TT - 1))
                    last.then_inc(mix_ready, 1)
                pe.wait_ge(feat_free, 2 + i * FEAT + FEAT)
                n = len(KVG)
                for t in range(TT):
                    for m0, m1 in APG:
                        pe.wait_ge(mix_free, i * MIX + n + 1)
                        pe.wait_ge(mix_free, 2 + i * MIX + min((m1 + 1) // 2, len(KVG)))
                        for m in range(m0, m1):
                            last = nc.tensor.matmul(ps_mix[n % 2][:, (m - m0) * VB:(m - m0 + 1) * VB],
                                                    qT[:, m, t * P:(t + 1) * P], kv[:, m, :],
                                                    start=True, stop=True)
                        last.then_inc(mix_ready, 1)
                        n += 1

                def turn(t, half):
                    tile = tp_unit(TT + 2 * t + half)
                    for j in range(4):
                        m = 4 * half + j
                        last = nc.tensor.transpose(tile[:, j * P:(j + 1) * P], on[:, t, m * P:(m + 1) * P],
                                                   ident[:, :])
                    last.then_inc(tp_ready, 1)

                def project(t, half):
                    pe.wait_ge(tp_free, 2 + i * TPU + TT + 2 * t + half + 1)
                    for j in range(4):
                        m = 4 * half + j
                        nc.tensor.matmul(ps_out[:, t, :], onT[:, t, m, :], w["A_o"][:, m, :],
                                         start=(m == 0), stop=False)

                pe.wait_ge(mix_free, 2 + i * MIX + len(KVG) + len(APG))
                turn(0, 0)
                turn(0, 1)
                pe.wait_ge(out_used, i + 1)
                project(0, 0)
                pe.wait_ge(mix_free, 2 + i * MIX + MIX)
                turn(1, 0)
                project(0, 1)
                nc.tensor.matmul(ps_out[:, 0, :], ones_row[:, :], w["A_bo"][:, :], start=False, stop=True)
                turn(1, 1)
                project(1, 0)
                project(1, 1)
                nc.tensor.matmul(ps_out[:, 1, :], ones_row[:, :], w["A_bo"][:, :], start=False, stop=True)\
                    .then_inc(out_ready, 1)

        @block.scalar
        def _(act):
            act.sem_inc(proj_free, RING)
            act.sem_inc(tp_free, 2)
            act.wait_ge(consts_ready, CONSTS)
            nc.scalar.activation(re[:, 0, 0:1], ident[:, 0:1], ACT.Exp)
            with act.Fori(0, B) as i:
                for t in range(TT):
                    act.wait_ge(tp_ready, i * TPU + t + 1)
                    nc.scalar.copy(xT[:, t * P:(t + 1) * P], ps_tp[t % 2][:, 0:P]).then_inc(tp_free, 1)
                f = 0
                for n in range(PROJ):
                    bank = ps_proj[n % RING]
                    act.wait_ge(proj_ready, i * PROJ + n + 1)
                    kind, r = divmod(n, TT * (HD // BANK))
                    if kind == 1:
                        t, h = divmod(r, HD // BANK)
                        nc.scalar.copy(v[:, t, 4 * h:4 * h + 4, 1:1 + P],
                                       bank[:, :].rearrange("p (m e) -> p m e", e=P)).then_inc(proj_free, 1)
                    else:
                        act.wait_ge(feat_free, i * FEAT + f + 1)
                        nc.scalar.activation(ex[:, f % 2, :], bank[:, :], ACT.Exp)
                        nc.scalar.activation(re[:, f % 2, :], bank[:, :], ACT.Relu).then_inc(proj_free, 1)
                        f += 1
                for t in range(TT):
                    for half in range(2):
                        n = TT + 2 * t + half
                        act.wait_ge(tp_ready, i * TPU + n + 1)
                        nc.scalar.copy(onT[:, t, 4 * half:4 * half + 4, :],
                                       ps_tp[n % 2][:, :].rearrange("p (m q) -> p m q", q=P)).then_inc(tp_free, 1)

        @block.vector
        def _(dve):
            dve.sem_inc(feat_free, 2)
            dve.sem_inc(mix_free, 2)
            dve.sem_inc(out_used, 1)
            dve.wait_ge(x_all_ready, 16)
            dve.wait_ge(slots_set, 3)
            with dve.Fori(0, B) as i:
                steps = Count(i, 2 * TT * len(APG) + 1 + 1)
                for f in range(FEAT):
                    r = f % (TT * (HD // BANK))
                    if f < TT * (HD // BANK):
                        t, h = divmod(r, HD // BANK)
                        out = k[:, t, h * BANK:(h + 1) * BANK]
                    else:
                        out = qT[:, 2 * r:2 * r + 2, :].rearrange("p m q -> p (m q)")
                    n = f if f < TT * (HD // BANK) else f + TT * (HD // BANK)
                    dve.wait_ge(proj_free, RING + i * PROJ + n + 1)
                    nc.vector.scalar_tensor_tensor(out, ex[:, f % 2, :], 1.0, re[:, f % 2, :], ALU.min, ALU.add)\
                        .then_inc(feat_free, 1)
                for n, (m0, m1) in enumerate(KVG):
                    dve.wait_ge(mix_ready, i * MIX + n + 1)
                    src = ps_mix[n % 2][:, 0:(m1 - m0) * VB].rearrange("p (m e) -> p m e", e=VB)
                    nc.vector.tensor_copy(kv[0:DH, m0:m1, 0:DH + 1], src[0:DH, :, 0:DH + 1])
                    nc.vector.tensor_copy(kv[DH:P, m0:m1, DH + 1:VB], src[DH:P, :, DH + 1:VB])\
                        .then_inc(mix_free, 1)
                n = len(KVG)
                for t in range(TT):
                    for m0, m1 in APG:
                        dve.wait_ge(mix_ready, i * MIX + n + 1)
                        ms = m1 - m0
                        src = ps_mix[n % 2][:, 0:ms * VB].rearrange("p (m e) -> p m e", e=VB)
                        d = den[:, n, 0:2 * ms].rearrange("p (m s) -> p m s", s=2)
                        r = rden[:, n, 0:2 * ms].rearrange("p (m s) -> p m s", s=2)
                        nc.vector.tensor_scalar(d, src[:, :, 0:VB:VB - 1], 1e-6, None, ALU.add)\
                            .then_inc(dve_step, 1)
                        dve.wait_ge(dve_step, steps.next())
                        nc.vector.reciprocal(r, d).then_inc(dve_step, 1)
                        dve.wait_ge(dve_step, steps.next())
                        nc.vector.tensor_tensor(
                            on[:, t, m0 * P:m1 * P].rearrange("p (m s e) -> p m s e", s=2, e=DH),
                            src[:, :, 1:1 + P].rearrange("p m (s e) -> p m s e", s=2),
                            r.unsqueeze(3).broadcast_to([P, ms, 2, DH]), ALU.mult).then_inc(mix_free, 1)
                        n += 1
                dve.wait_ge(out_ready, i + 1)
                nc.vector.tensor_tensor(rows[:, :, :], ps_out[:, :, :], x_all[:, ds(i * TT, TT), :], ALU.add)\
                    .then_inc(out_used, 1)
                dve.wait_ge(out_used, i + 2)
                layernorm_rows(dve, nc, steps, dve_step, rows, stats, mv, rstd, var_ready, rstd_ready, i + 1,
                               lambda t: x_all[:, ds(i * TT + t, 1), :].squeeze(1), TT).then_inc(dve_step, 1)
                dve.wait_ge(dve_step, steps.next())
                steps.close()


def stage_b_attention(nc, c, x_all, y_all, w, ident, consts_ready, mhalf, lnrow):
    G, HH, F = 4, 4, 8
    VB = F + 1
    SC = 3 * P
    SCALE = float(D) ** -0.5

    x_in = c.sb("b_x_in", [P, TT, D])
    xT = c.sb("b_xT", [P, N])
    qT = c.sb("b_qT", [P, G, N])
    qTm = c.sb("b_qTm", [P, G, N])
    kT = c.sb("b_kT", [P, G, N])
    v = c.sb("b_v", [P, TT, G * HH, VB])
    negmax = c.sb("b_negmax", [P, TT, G, HH, 32])
    probs = c.sb("b_probs", [P, 2, HH, SC])
    rsum = c.sb("b_rsum", [P, TT, G * HH])
    attn = c.sb("b_attn", [P, TT, D])
    z = c.sb("b_z", [P, TT, D])
    zg = c.sb("b_zg", [P, TT, D])
    xb = c.sb("b_xb", [P, TT, D])
    stats = c.sb("b_stats", [P, TT, 6])
    mv = c.sb("b_mv", [P, TT, 2])
    rstd = c.sb("b_rstd", [P, TT])
    k_one = c.sb("b_k_one", [P, 1])
    mask = c.sb("b_mask", [P, 3, P], BF16)
    identb = c.sb("b_identb", [P, P], BF16)
    turn_mark = c.sb("b_turn_mark", [P, 2])
    ps_sc = c.ps("b_ps_sc", [P, HH, BANK])
    ps_st = [c.ps(f"b_ps_st{j}", [P, BANK]) for j in range(2)]
    ps_misc = c.ps("b_ps_misc", [P, BANK])
    ps_att = c.ps("b_ps_att", [P, TT, G * HH, VB])

    x_in_ready = c.sem("b_x_in_ready")
    x_turned = c.sem("b_x_turned")
    xb_ready = c.sem("b_xb_ready")
    set_step = c.sem("b_set_step")
    slots_set = c.sem("b_slots_set")
    xT_ready = c.sem("b_xT_ready")
    proj_ready = c.sem("b_proj_ready")
    qk_ready = c.sem("b_qk_ready")
    v_made = c.sem("b_v_made")
    v_ready = c.sem("b_v_ready")
    scores_ready = c.sem("b_scores_ready")
    max_turned = c.sem("b_max_turned")
    max_ready = c.sem("b_max_ready")
    qTm_ready = c.sem("b_qTm_ready")
    st_ready = c.sem("b_st_ready")
    st_free = c.sem("b_st_free")
    masked = c.sem("b_masked")
    probs_free = c.sem("b_probs_free")
    att_ready = c.sem("b_att_ready")
    att_free = c.sem("b_att_free")
    dve_step = c.sem("b_dve_step")
    var_ready = c.sem("b_var_ready")
    rstd_ready = c.sem("b_rstd_ready")
    z_ready = c.sem("b_z_ready")
    zg_ready = c.sem("b_zg_ready")
    y_ready = c.sem("b_y_ready")

    with nc.Block() as block:

        @block.sync
        def _(sp):
            with sp.Fori(0, B) as i:
                sp.wait_ge(x_turned, i + 1)
                sp.wait_ge(xb_ready, i + 1)
                sp.dma_start(x_in[:, :, :], x_all[:, ds(i * TT, TT), :]).then_inc(x_in_ready, 16)

        @block.gpsimd
        def _(pool):
            nc.gpsimd.memset(negmax[:, :, :, :, :], 0.0).then_inc(slots_set, 1)
            nc.gpsimd.memset(v[:, :, :, F:VB], 1.0).then_inc(slots_set, 1)
            nc.gpsimd.memset(turn_mark[:, :], 1.0).then_inc(set_step, 1)
            nc.gpsimd.memset(mask[:, :, :], 0.0).then_inc(set_step, 1)
            nc.gpsimd.memset(identb[:, :], 0.0).then_inc(set_step, 1)
            nc.gpsimd.memset(k_one[:, :], 0.0).then_inc(set_step, 1)
            pool.wait_ge(set_step, 4)
            for j in (0, 2):
                nc.gpsimd.affine_select(out=mask[:, j, :], in_=mask[:, j, :], compare_op=ALU.is_ge, fill=-1e30,
                                        base=0, pattern=[[-1, P]], channel_multiplier=1).then_inc(slots_set, 1)
            nc.gpsimd.affine_select(out=identb[:, :], in_=identb[:, :], compare_op=ALU.not_equal, fill=1.0,
                                    base=0, pattern=[[-1, P]], channel_multiplier=1).then_inc(slots_set, 1)
            for hh in range(HH):
                nc.gpsimd.affine_select(out=k_one[:, :], in_=k_one[:, :], compare_op=ALU.not_equal, fill=1.0,
                                        base=-(32 * hh + F), pattern=[[0, 1]], channel_multiplier=1)\
                    .then_inc(set_step, 1)
                pool.wait_ge(set_step, 5 + hh)
            pool.sem_inc(slots_set, 1)
            pool.sem_inc(xb_ready, 1)
            pool.sem_inc(y_ready, 1)
            with pool.Fori(0, B) as i:
                pool.wait_ge(y_ready, i + 1)
                pool.wait_ge(x_in_ready, i * 16 + 16)
                nc.gpsimd.tensor_tensor(xb[:, :, :], x_in[:, :, :],
                                        lnrow[:, 1, :].unsqueeze(1).broadcast_to([P, TT, D]), ALU.add)\
                    .then_inc(xb_ready, 1)
                for g in range(G):
                    pool.wait_ge(st_free, 2 + i * G * HH + (g + 1) * HH)
                    nc.gpsimd.tensor_tensor(turn_mark[:, 1:2], turn_mark[:, 0:1], turn_mark[:, 0:1], ALU.mult)
                    diag = probs[:, g % 2, :, 0:2 * P]
                    nc.gpsimd.affine_select(out=diag, in_=diag, compare_op=ALU.is_ge, fill=0.0, base=0,
                                            pattern=[[0, HH], [0, 2], [1, P]], channel_multiplier=-1)\
                        .then_inc(masked, 1)
                pool.wait_ge(var_ready, i + 1)
                nc.gpsimd.tensor_tensor(rstd[:, :], mv[:, :, 1], mhalf[:, 0:TT], ALU.pow).then_inc(rstd_ready, 1)
                pool.wait_ge(z_ready, i + 1)
                nc.gpsimd.tensor_tensor(zg[:, :, :], z[:, :, :],
                                        lnrow[:, 0, :].unsqueeze(1).broadcast_to([P, TT, D]), ALU.mult)\
                    .then_inc(zg_ready, 1)
                pool.wait_ge(xb_ready, i + 2)
                pool.wait_ge(zg_ready, i + 1)
                nc.gpsimd.tensor_tensor(y_all[:, ds(i * TT, TT), :], zg[:, :, :], xb[:, :, :], ALU.add)\
                    .then_inc(y_ready, 1)

        @block.tensor
        def _(pe):
            pe.wait_ge(consts_ready, CONSTS)
            pe.wait_ge(w["B_ready"], W_B)
            pe.wait_ge(slots_set, 6)
            pe.sem_inc(x_turned, 1)
            with pe.Fori(0, B) as i:
                pe.wait_ge(x_in_ready, i * 16 + 16)
                pe.wait_ge(qTm_ready, i * G + 1)
                for t in range(TT):
                    last = nc.tensor.transpose(ps_misc[:, t * P:(t + 1) * P], x_in[:, t, :], ident[:, :])
                last.then_inc(x_turned, 1)
                pe.wait_ge(xT_ready, i + 1)
                pe.wait_ge(max_ready, i * G + 1)
                for j, name in ((0, "B_q"), (2, "B_k")):
                    for g in range(G):
                        last = nc.tensor.matmul(ps_sc[:, j + g // 2, (g % 2) * N:(g % 2 + 1) * N],
                                                w[name][:, g, :, :].rearrange("p h f -> p (h f)"), xT[:, :],
                                                start=True, stop=True)
                last.then_inc(proj_ready, 1)
                for t in range(TT):
                    last = nc.tensor.matmul(ps_misc[:, t * P:(t + 1) * P], xT[:, t * P:(t + 1) * P], w["B_v"][:, :],
                                            start=True, stop=True)
                last.then_inc(v_made, 1)

                def scores(g):
                    if g == 0:
                        pe.wait_ge(qk_ready, i + 1)
                    else:
                        pe.wait_ge(max_ready, 1 + i * G + g)
                    for hh in range(HH):
                        nc.tensor.matmul(ps_sc[:, hh, 0:SC], identb[:, :], mask[:, :, :].rearrange("p j s -> p (j s)"),
                                         start=True, stop=True, skip_group_check=True)
                    for t, (c0, c1) in enumerate(((0, P), (P, SC))):
                        for hh in range(HH):
                            r0 = 32 * hh
                            last = nc.tensor.matmul(ps_sc[:, hh, c0:c1], qT[r0:r0 + 32, g, t * P:(t + 1) * P],
                                                    kT[r0:r0 + 32, g, 0:c1 - c0], start=False, stop=True,
                                                    skip_group_check=True)
                    last.then_inc(scores_ready, 1)

                def maxima(g):
                    pe.wait_ge(max_ready, 1 + i * G + g + 1)
                    if g == 0:
                        pe.wait_ge(v_ready, i + 1)
                    else:
                        pe.wait_ge(qTm_ready, 1 + i * G + g)
                    for t in range(TT):
                        last = nc.tensor.transpose(ps_misc[:, t * P:(t + 1) * P],
                                                   negmax[:, t, g, :, :].rearrange("p h f -> p (h f)"), ident[:, :])
                    last.then_inc(max_turned, 1)

                def scores_t(g):
                    pe.wait_ge(qTm_ready, 1 + i * G + g + 1)
                    for hh in range(HH):
                        r0, bank = 32 * hh, ps_st[hh % 2]
                        pe.wait_ge(st_free, i * G * HH + g * HH + hh + 1)
                        nc.tensor.matmul(bank[:, 0:SC].rearrange("p (j t) -> p j t", t=P)[:, 0:3:2, :],
                                         kT[r0:r0 + 32, g, 0:P], qTm[r0:r0 + 32, g, :], start=True, stop=True)
                        nc.tensor.matmul(bank[:, P:N], kT[r0:r0 + 32, g, P:N], qTm[r0:r0 + 32, g, P:N],
                                         start=True, stop=True).then_inc(st_ready, 1)

                def attend(g):
                    pe.wait_ge(masked, i * G + g + 1)
                    for hh in range(HH):
                        pr, h = probs[:, g % 2, hh, :], g * HH + hh
                        nc.tensor.matmul(ps_att[:, 0, h, :], pr[:, 0:P], v[:, 0, h, :], start=True, stop=True)
                        nc.tensor.matmul(ps_att[:, 1, h, :], pr[:, N:SC], v[:, 0, h, :], start=True, stop=False)
                        last = nc.tensor.matmul(ps_att[:, 1, h, :], pr[:, P:N], v[:, 1, h, :],
                                                start=False, stop=True)
                    last.then_inc(probs_free, 1)

                scores(0)
                maxima(0)
                scores(1)
                scores_t(0)
                maxima(1)
                scores(2)
                pe.wait_ge(att_free, i + 1)
                attend(0)
                scores_t(1)
                maxima(2)
                scores(3)
                attend(1)
                scores_t(2)
                maxima(3)
                attend(2)
                scores_t(3)
                attend(3)

        @block.scalar
        def _(act):
            act.sem_inc(st_free, 2)
            act.wait_ge(slots_set, 6)
            with act.Fori(0, B) as i:
                act.wait_ge(x_turned, i + 2)
                nc.scalar.copy(xT[:, :], ps_misc[:, 0:N]).then_inc(xT_ready, 1)
                act.wait_ge(proj_ready, i + 1)
                for j in range(2):
                    nc.scalar.copy(qT[:, 2 * j:2 * j + 2, :], ps_sc[:, j, :].rearrange("p (g n) -> p g n", g=2))
                for j in range(2):
                    last = nc.scalar.activation(kT[:, 2 * j:2 * j + 2, :],
                                                ps_sc[:, 2 + j, :].rearrange("p (g n) -> p g n", g=2),
                                                ACT.Identity, bias=k_one[:, :])
                last.then_inc(qk_ready, 1)
                act.wait_ge(v_made, i + 1)
                nc.scalar.copy(v[:, :, :, 0:F], ps_misc[:, 0:N].rearrange("p (t h f) -> p t h f", t=TT, f=F))\
                    .then_inc(v_ready, 1)
                for g in range(G):
                    act.wait_ge(probs_free, i * G + g + 1)
                    for hh in range(HH):
                        act.wait_ge(st_ready, i * G * HH + g * HH + hh + 1)
                        nc.scalar.activation(probs[:, g % 2, hh, :], ps_st[hh % 2][:, 0:SC], ACT.Exp, scale=SCALE)\
                            .then_inc(st_free, 1)

        @block.vector
        def _(dve):
            dve.sem_inc(probs_free, 2)
            dve.sem_inc(max_ready, 1)
            dve.sem_inc(qTm_ready, 1)
            dve.sem_inc(att_free, 1)
            dve.wait_ge(slots_set, 6)
            with dve.Fori(0, B) as i:
                steps = Count(i, 1 + 1)

                def row_max(g):
                    dve.wait_ge(scores_ready, i * G + g + 1)
                    for t, (c0, c1) in enumerate(((0, P), (P, SC))):
                        last = nc.vector.tensor_reduce(negmax[:, t, g, :, F:F + 1], ps_sc[:, :, c0:c1], AX_X, ALU.max,
                                                       negate=True)
                    last.then_inc(max_ready, 1)

                def add_max(g):
                    dve.wait_ge(max_turned, i * G + g + 1)
                    nc.vector.tensor_tensor(qTm[:, g, :], ps_misc[:, 0:N], qT[:, g, :], ALU.add).then_inc(qTm_ready, 1)
                for g in range(G):
                    row_max(g)
                    add_max(g)
                dve.wait_ge(probs_free, 2 + i * G + G)
                nc.vector.reciprocal(rsum[:, :, :], ps_att[:, :, :, F]).then_inc(dve_step, 1)
                dve.wait_ge(dve_step, steps.next())
                nc.vector.tensor_tensor(attn[:, :, :].rearrange("p t (h f) -> p t h f", f=F), ps_att[:, :, :, 0:F],
                                        rsum[:, :, :].unsqueeze(3).broadcast_to([P, TT, G * HH, F]), ALU.mult)\
                    .then_inc(att_free, 1)
                dve.wait_ge(att_free, i + 2)
                dve.wait_ge(y_ready, i + 1)
                layernorm_rows(dve, nc, steps, dve_step, attn, stats, mv, rstd, var_ready, rstd_ready, i + 1,
                               lambda t: z[:, t, :], TT).then_inc(z_ready, 1)
                steps.close()


def stage_b_experts(nc, c, x_all, y_all, w, ident, consts_ready, mhalf, lnrow):
    E, FF = 8, 4 * D
    TM = BANK // P
    TURNS = TILES // TM
    C = FF // P
    MISC = 4

    y_in = c.sb("m_y_in", [P, TM, D])
    xy = c.sb("m_xy", [P, TM, D])
    yT = c.sb("m_yT", [P, BANK])
    lg = c.sb("m_lg", [P, TM, E])
    mx = c.sb("m_mx", [P, TM, 8])
    ix = c.sb("m_ix", [P, TM, 8], U32)
    ixf = c.sb("m_ixf", [P, TM, 2])
    gap = c.sb("m_gap", [P, TM])
    eg = c.sb("m_eg", [P, TM])
    wsum = c.sb("m_wsum", [P, TM])
    wt = c.sb("m_wt", [P, 2, TM])
    pick = c.sb("m_pick", [P, 2, TM, E])
    comb = c.sb("m_comb", [P, TM, E])
    combT = c.sb("m_combT", [E, BANK])
    experts = c.sb("m_experts", [P, E])
    h = c.sb("m_h", [P, 2, C, BANK])
    acc = c.sb("m_acc", [P, TM, D])
    z = c.sb("m_z", [P, TM, D])
    zg = c.sb("m_zg", [P, TM, D])
    rows = c.sb("m_rows", [P, TM, D])
    stats = c.sb("m_stats", [P, TM, 6])
    mv = c.sb("m_mv", [P, TM, 2])
    rstd = c.sb("m_rstd", [P, TM])
    ps_h = [c.ps(f"m_ps_h{j}", [P, BANK]) for j in range(4)]
    ps_eo = [c.ps(f"m_ps_eo{j}", [P, BANK]) for j in range(2)]
    ps_misc = [c.ps(f"m_ps_misc{j}", [P, BANK]) for j in range(2)]

    y_in_ready = c.sem("m_y_in_ready")
    y_in_free = c.sem("m_y_in_free")
    iota_ready = c.sem("m_iota_ready")
    misc_ready = c.sem("m_misc_ready")
    misc_free = c.sem("m_misc_free")
    gap_ready = c.sem("m_gap_ready")
    eg_ready = c.sem("m_eg_ready")
    comb_ready = c.sem("m_comb_ready")
    h_ready = c.sem("m_h_ready")
    h_free = c.sem("m_h_free")
    eo_ready = c.sem("m_eo_ready")
    eo_free = c.sem("m_eo_free")
    dve_step = c.sem("m_dve_step")
    var_ready = c.sem("m_var_ready")
    rstd_ready = c.sem("m_rstd_ready")
    z_ready = c.sem("m_z_ready")
    pool_step = c.sem("m_pool_step")
    rows_ready = c.sem("m_rows_ready")

    with nc.Block() as block:

        @block.sync
        def _(sp):
            with sp.Fori(0, TURNS) as i:
                sp.wait_ge(y_in_free, i + 1)
                sp.dma_start(y_in[:, :, :], y_all[:, ds(i * TM, TM), :]).then_inc(y_in_ready, 16)

        @block.gpsimd
        def _(pool):
            nc.gpsimd.iota(experts[:, :], pattern=[[1, E]], base=0, channel_multiplier=0,
                           allow_small_or_imprecise_dtypes=True).then_inc(iota_ready, 1)
            pool.sem_inc(y_in_free, 1)
            pool.sem_inc(rows_ready, 1)
            with pool.Fori(0, TURNS) as i:
                pool.wait_ge(rows_ready, i + 1)
                pool.wait_ge(y_in_ready, i * 16 + 16)
                nc.gpsimd.tensor_tensor(xy[:, :, :], x_all[:, ds(i * TM, TM), :], y_in[:, :, :], ALU.add)\
                    .then_inc(pool_step, 1)
                pool.wait_ge(pool_step, i * 3 + 1)
                nc.gpsimd.tensor_tensor(xy[:, :, :], xy[:, :, :],
                                        lnrow[:, 3, :].unsqueeze(1).broadcast_to([P, TM, D]), ALU.add)\
                    .then_inc(pool_step, 1)
                pool.wait_ge(misc_ready, i * MISC + 1)
                pool.wait_ge(pool_step, i * 3 + 2)
                pool.sem_inc(y_in_free, 1)
                pool.wait_ge(var_ready, 2 * i + 1)
                nc.gpsimd.tensor_tensor(rstd[:, :], mv[:, :, 1], mhalf[:, 0:TM], ALU.pow).then_inc(rstd_ready, 1)
                pool.wait_ge(z_ready, i + 2)
                nc.gpsimd.tensor_tensor(zg[:, :, :], z[:, :, :],
                                        lnrow[:, 2, :].unsqueeze(1).broadcast_to([P, TM, D]), ALU.mult)\
                    .then_inc(pool_step, 1)
                pool.wait_ge(pool_step, i * 3 + 3)
                nc.gpsimd.tensor_tensor(rows[:, :, :], zg[:, :, :], xy[:, :, :], ALU.add).then_inc(rows_ready, 1)
                pool.wait_ge(var_ready, 2 * i + 2)
                nc.gpsimd.tensor_tensor(rstd[:, :], mv[:, :, 1], mhalf[:, 0:TM], ALU.pow).then_inc(rstd_ready, 1)

        @block.tensor
        def _(pe):
            pe.wait_ge(w["B_ready"], W_B)
            pe.wait_ge(consts_ready, CONSTS)
            with pe.Fori(0, TURNS) as i:
                pe.wait_ge(y_in_ready, i * 16 + 16)
                pe.wait_ge(misc_free, i * MISC + 1)
                for t in range(TM):
                    last = nc.tensor.transpose(ps_misc[0][:, t * P:(t + 1) * P], y_in[:, t, :], ident[:, :])
                last.then_inc(misc_ready, 1)
                pe.wait_ge(misc_free, i * MISC + 2)
                pe.wait_ge(misc_free, 2 + i * MISC + 1)
                for t in range(TM):
                    last = nc.tensor.matmul(ps_misc[1][:, t * E:(t + 1) * E], yT[:, t * P:(t + 1) * P],
                                            w["B_gate"][:, :], start=True, stop=True)
                last.then_inc(misc_ready, 1)

                def hidden(e):
                    for j in range(C):
                        n = e * C + j
                        pe.wait_ge(h_free, i * E * C + n + 1)
                        nc.tensor.matmul(ps_h[n % 4][:, :], w["B_W1"][:, e, j * P:(j + 1) * P], yT[:, :],
                                         start=True, stop=True).then_inc(h_ready, 1)

                def outputs(e):
                    pe.wait_ge(eo_free, i * E + e + 1)
                    pe.wait_ge(h_free, 4 + i * E * C + (e + 1) * C)
                    for t in range(TM):
                        for j in range(C):
                            last = nc.tensor.matmul(ps_eo[e % 2][:, t * P:(t + 1) * P],
                                                    h[:, e % 2, j, t * P:(t + 1) * P], w["B_W2"][:, e * C + j, :],
                                                    start=(j == 0), stop=(j == C - 1))
                    last.then_inc(eo_ready, 1)

                hidden(0)
                pe.wait_ge(comb_ready, i + 1)
                pe.wait_ge(misc_free, i * MISC + 3)
                for t in range(TM):
                    last = nc.tensor.transpose(ps_misc[0][0:E, t * P:(t + 1) * P], comb[:, t, :], ident[:, :])
                last.then_inc(misc_ready, 1)
                hidden(1)
                pe.wait_ge(misc_free, 2 + i * MISC + 3)
                for t in range(TM):
                    last = nc.tensor.matmul(ps_misc[1][:, t * P:(t + 1) * P], combT[:, t * P:(t + 1) * P],
                                            w["B_b2"][:, :], start=True, stop=True)
                last.then_inc(misc_ready, 1)
                for e in range(E):
                    outputs(e)
                    if e + 2 < E:
                        hidden(e + 2)

        @block.scalar
        def _(act):
            act.sem_inc(misc_free, 2)
            act.sem_inc(h_free, 4)
            act.wait_ge(w["B_ready"], W_B)
            with act.Fori(0, TURNS) as i:
                act.wait_ge(misc_ready, i * MISC + 1)
                nc.scalar.copy(yT[:, :], ps_misc[0][:, :]).then_inc(misc_free, 1)

                def relu(e):
                    if e >= 2:
                        act.wait_ge(eo_ready, i * E + e - 1)
                    for j in range(C):
                        n = e * C + j
                        act.wait_ge(h_ready, i * E * C + n + 1)
                        nc.scalar.activation(h[:, e % 2, j, :], ps_h[n % 4][:, :], ACT.Relu,
                                             bias=w["B_b1"][:, n:n + 1]).then_inc(h_free, 1)

                act.wait_ge(gap_ready, i + 1)
                nc.scalar.activation(eg[:, :], gap[:, :], ACT.Exp).then_inc(eg_ready, 1)
                relu(0)
                act.wait_ge(misc_ready, i * MISC + 3)
                nc.scalar.copy(combT[:, :], ps_misc[0][0:E, :]).then_inc(misc_free, 1)
                relu(1)
                act.wait_ge(misc_ready, i * MISC + 4)
                act.wait_ge(z_ready, i + 1)
                nc.scalar.copy(acc[:, :, :].rearrange("p t d -> p (t d)"), ps_misc[1][:, :]).then_inc(misc_free, 1)
                for e in range(2, E):
                    relu(e)

        @block.vector
        def _(dve):
            dve.sem_inc(eo_free, 2)
            dve.sem_inc(z_ready, 1)
            dve.wait_ge(iota_ready, 1)
            with dve.Fori(0, TURNS) as i:
                steps = Count(i, 4 + 2 + 1)
                dve.wait_ge(misc_ready, i * MISC + 2)
                dve.wait_ge(misc_free, 2 + i * MISC + 1)
                nc.vector.tensor_copy(lg[:, :, :].rearrange("p t e -> p (t e)"), ps_misc[1][:, 0:TM * E])\
                    .then_inc(misc_free, 1)
                dve.drain()
                for t in range(TM):
                    nc.vector.max(mx[:, t, :], lg[:, t, :])
                dve.drain()
                for t in range(TM):
                    nc.vector.max_index(ix[:, t, :], mx[:, t, :], lg[:, t, :])
                nc.vector.tensor_tensor(gap[:, :], mx[:, :, 1], mx[:, :, 0], ALU.subtract).then_inc(gap_ready, 1)
                dve.drain()
                nc.vector.tensor_copy(ixf[:, :, :], ix[:, :, 0:2])
                dve.wait_ge(eg_ready, i + 1)
                nc.vector.tensor_scalar(wsum[:, :], eg[:, :], 1.0, None, ALU.add).then_inc(dve_step, 1)
                dve.wait_ge(dve_step, steps.next())
                nc.vector.reciprocal(wt[:, 0, :], wsum[:, :]).then_inc(dve_step, 1)
                dve.wait_ge(dve_step, steps.next())
                nc.vector.tensor_tensor(wt[:, 1, :], eg[:, :], wt[:, 0, :], ALU.mult).then_inc(dve_step, 1)
                dve.wait_ge(dve_step, steps.next())
                for s in range(2):
                    for t in range(TM):
                        last = nc.vector.tensor_scalar(pick[:, s, t, :], experts[:, :], ixf[:, t, s:s + 1],
                                                       wt[:, s, t:t + 1], ALU.is_equal, ALU.mult)
                last.then_inc(dve_step, 1)
                dve.wait_ge(dve_step, steps.next())
                nc.vector.tensor_tensor(comb[:, :, :], pick[:, 0, :, :], pick[:, 1, :, :], ALU.add)\
                    .then_inc(comb_ready, 1)
                dve.wait_ge(comb_ready, i + 1)
                dve.wait_ge(misc_free, 2 + i * MISC + MISC)
                for e in range(E):
                    dve.wait_ge(eo_ready, i * E + e + 1)
                    for t in range(TM):
                        last = nc.vector.scalar_tensor_tensor(acc[:, t, :], ps_eo[e % 2][:, t * P:(t + 1) * P],
                                                              comb[:, t, e:e + 1], acc[:, t, :], ALU.mult, ALU.add)
                    last.then_inc(eo_free, 1)
                    dve.wait_ge(eo_free, 2 + i * E + e + 1)
                layernorm_rows(dve, nc, steps, dve_step, acc, stats, mv, rstd, var_ready, rstd_ready, 2 * i + 1,
                               lambda t: z[:, t, :], TM).then_inc(z_ready, 1)
                dve.wait_ge(rows_ready, i + 2)
                layernorm_rows(dve, nc, steps, dve_step, rows, stats, mv, rstd, var_ready, rstd_ready, 2 * i + 2,
                               lambda t: x_all[:, ds(i * TM + t, 1), :].squeeze(1), TM).then_inc(dve_step, 1)
                dve.wait_ge(dve_step, steps.next())
                steps.close()


def stage_c(nc, c, x_all, w, ident, consts_ready, mhalf):
    VB = DH + 1
    SC = 3 * P
    RING = 2
    PROJ = 2 * (PAIRS // 2) + 2 * TT * (HD // BANK)
    FEAT = 2 * (PAIRS // 2)
    TPU = TT + 2 * TT
    assert PROJ % RING == 0 and TPU % 2 == 0

    x_in = c.sb("c_x_in", [P, TT, D])
    xT = c.sb("c_xT", [P, N])
    qT = c.sb("c_qT", [P, PAIRS, N])
    kT = c.sb("c_kT", [P, PAIRS, N])
    v = c.sb("c_v", [P, TT, H, VB])
    gate = c.sb("c_gate", [P, TT, HD])
    ex = c.sb("c_exp", [P, 2, BANK])
    re = c.sb("c_relu", [P, 2, BANK])
    mask = c.sb("c_mask", [P, SC])
    sc = c.sb("c_sc", [P, 2, 2, SC])
    den = c.sb("c_den", [P, PAIRS, TT * 2])
    rden = c.sb("c_rden", [P, PAIRS, TT * 2])
    o = c.sb("c_o", [P, TT, HD])
    og = c.sb("c_og", [P, TT, HD])
    oT = c.sb("c_oT", [P, TT, PAIRS, P])
    rows = c.sb("c_rows", [P, TT, D])
    stats = c.sb("c_stats", [P, TT, 6])
    mv = c.sb("c_mv", [P, TT, 2])
    rstd = c.sb("c_rstd", [P, TT])
    ps_proj = [c.ps(f"c_ps_proj{j}", [P, BANK]) for j in range(RING)]
    ps_sc = [c.ps(f"c_ps_sc{j}", [P, 2, BANK]) for j in range(2)]
    ps_att = c.ps("c_ps_att", [P, BANK])
    ps_out = c.ps("c_ps_out", [P, TT, D])

    x_in_ready = c.sem("c_x_in_ready")
    x_turned = c.sem("c_x_turned")
    set_step = c.sem("c_set_step")
    slots_set = c.sem("c_slots_set")
    xT_ready = c.sem("c_xT_ready")
    proj_ready = c.sem("c_proj_ready")
    proj_free = c.sem("c_proj_free")
    feat_free = c.sem("c_feat_free")
    sc_ready = c.sem("c_sc_ready")
    sc_masked = c.sem("c_sc_masked")
    att_ready = c.sem("c_att_ready")
    att_free = c.sem("c_att_free")
    gated = c.sem("c_gated")
    o_turned = c.sem("c_o_turned")
    oT_ready = c.sem("c_oT_ready")
    out_ready = c.sem("c_out_ready")
    out_used = c.sem("c_out_used")
    dve_step = c.sem("c_dve_step")
    var_ready = c.sem("c_var_ready")
    rstd_ready = c.sem("c_rstd_ready")

    with nc.Block() as block:

        @block.sync
        def _(sp):
            with sp.Fori(0, B) as i:
                sp.wait_ge(x_turned, i + 1)
                sp.dma_start(x_in[:, :, :], x_all[:, ds(i * TT, TT), :]).then_inc(x_in_ready, 16)

        @block.gpsimd
        def _(pool):
            nc.gpsimd.memset(v[:, :, :, DH:VB], 1.0).then_inc(slots_set, 1)
            nc.gpsimd.memset(mask[:, :], 1.0).then_inc(set_step, 1)
            pool.wait_ge(set_step, 1)
            diag = mask[:, 0:2 * P].rearrange("p (j t) -> p j t", t=P)
            nc.gpsimd.affine_select(out=diag, in_=diag, compare_op=ALU.is_ge, fill=0.0, base=0,
                                    pattern=[[0, 2], [1, P]], channel_multiplier=-1).then_inc(slots_set, 1)
            with pool.Fori(0, B) as i:
                pool.wait_ge(var_ready, i + 1)
                nc.gpsimd.tensor_tensor(rstd[:, :], mv[:, :, 1], mhalf[:, 0:TT], ALU.pow).then_inc(rstd_ready, 1)

        @block.tensor
        def _(pe):
            pe.wait_ge(consts_ready, CONSTS)
            pe.wait_ge(w["C_ready"], W_C)
            pe.wait_ge(slots_set, 2)
            pe.sem_inc(x_turned, 1)
            with pe.Fori(0, B) as i:
                pe.wait_ge(x_in_ready, i * 16 + 16)
                pe.wait_ge(att_free, i * PAIRS + 1)
                for t in range(TT):
                    last = nc.tensor.transpose(ps_att[:, t * P:(t + 1) * P], x_in[:, t, :], ident[:, :])
                last.then_inc(x_turned, 1)
                pe.wait_ge(xT_ready, i + 1)
                n = 0
                for g in range(PAIRS // 2):
                    for j in range(2):
                        pe.wait_ge(proj_free, i * PROJ + n + 1)
                        for s in range(2):
                            c0 = j * HD + (2 * g + s) * P
                            last = nc.tensor.matmul(ps_proj[n % RING][:, s * N:(s + 1) * N], w["C_qkv"][:, c0:c0 + P],
                                                    xT[:, :], start=True, stop=True)
                        last.then_inc(proj_ready, 1)
                        n += 1
                for mat, c0 in (("C_qkv", 2 * HD), ("C_gate", 0)):
                    for t in range(TT):
                        for h in range(HD // BANK):
                            pe.wait_ge(proj_free, i * PROJ + n + 1)
                            nc.tensor.matmul(ps_proj[n % RING][:, :], xT[:, t * P:(t + 1) * P],
                                             w[mat][:, c0 + h * BANK:c0 + (h + 1) * BANK],
                                             start=True, stop=True).then_inc(proj_ready, 1)
                            n += 1

                def scores(m):
                    if m < 2:
                        pe.wait_ge(sc_masked, i * PAIRS + m + 1)
                    else:
                        pe.wait_ge(sc_masked, 2 + i * PAIRS + m - 1)
                    for s in range(2):
                        r0 = DH * s
                        bank = ps_sc[m % 2][:, s, :]
                        nc.tensor.matmul(bank[:, 0:SC].rearrange("p (j t) -> p j t", t=P)[:, 0:3:2, :],
                                         kT[r0:r0 + DH, m, 0:P], qT[r0:r0 + DH, m, :], start=True, stop=True)
                        last = nc.tensor.matmul(bank[:, P:N], kT[r0:r0 + DH, m, P:N], qT[r0:r0 + DH, m, P:N],
                                                start=True, stop=True)
                    last.then_inc(sc_ready, 1)

                def attend(m):
                    pe.wait_ge(sc_masked, 2 + i * PAIRS + m + 1)
                    pe.wait_ge(att_free, i * PAIRS + m + 1)
                    for s in range(2):
                        hd, a = 2 * m + s, sc[:, m % 2, s, :]
                        o0 = ps_att[:, s * VB:(s + 1) * VB]
                        o1 = ps_att[:, (2 + s) * VB:(3 + s) * VB]
                        nc.tensor.matmul(o0, a[:, 0:P], v[:, 0, hd, :], start=True, stop=True)
                        nc.tensor.matmul(o1, a[:, N:SC], v[:, 0, hd, :], start=True, stop=False)
                        last = nc.tensor.matmul(o1, a[:, P:N], v[:, 1, hd, :], start=False, stop=True)
                    last.then_inc(att_ready, 1)

                pe.wait_ge(feat_free, 2 + i * FEAT + FEAT)
                scores(0)
                scores(1)
                pe.wait_ge(proj_free, RING + i * PROJ + FEAT + TT * (HD // BANK))
                for m in range(PAIRS):
                    attend(m)
                    if m + 2 < PAIRS:
                        scores(m + 2)
                def turn(t):
                    if t == 0:
                        pe.wait_ge(sc_masked, 2 + i * PAIRS + PAIRS)
                    pe.wait_ge(gated, i * TT + t + 1)
                    for m in range(PAIRS):
                        last = nc.tensor.transpose(ps_sc[t][:, m // 4, (m % 4) * P:(m % 4 + 1) * P],
                                                   og[:, t, m * P:(m + 1) * P], ident[:, :])
                    last.then_inc(o_turned, 1)

                def project(t):
                    pe.wait_ge(oT_ready, 1 + i * TT + t + 1)
                    for m in range(PAIRS):
                        last = nc.tensor.matmul(ps_out[:, t, :], oT[:, t, m, :], w["C_out"][:, m, :],
                                                start=(m == 0), stop=(m == PAIRS - 1))
                    return last

                turn(0)
                turn(1)
                pe.wait_ge(out_used, i + 1)
                project(0)
                project(1).then_inc(out_ready, 1)
                pe.wait_ge(oT_ready, 1 + i * TT + TT)

        @block.scalar
        def _(act):
            act.sem_inc(proj_free, RING)
            act.sem_inc(oT_ready, 1)
            with act.Fori(0, B) as i:
                act.wait_ge(x_turned, i + 2)
                nc.scalar.copy(xT[:, :], ps_att[:, 0:N]).then_inc(xT_ready, 1)
                for n in range(FEAT):
                    act.wait_ge(proj_ready, i * PROJ + n + 1)
                    act.wait_ge(feat_free, i * FEAT + n + 1)
                    nc.scalar.activation(ex[:, n % 2, :], ps_proj[n % RING][:, :], ACT.Exp)
                    nc.scalar.activation(re[:, n % 2, :], ps_proj[n % RING][:, :], ACT.Relu).then_inc(proj_free, 1)
                for n in range(FEAT, PROJ):
                    kind, r = divmod(n - FEAT, TT * (HD // BANK))
                    t, h = divmod(r, HD // BANK)
                    bank = ps_proj[n % RING]
                    act.wait_ge(proj_ready, i * PROJ + n + 1)
                    if kind == 0:
                        nc.scalar.copy(v[:, t, 8 * h:8 * h + 8, 0:DH],
                                       bank[:, :].rearrange("p (m e) -> p m e", e=DH)).then_inc(proj_free, 1)
                    else:
                        nc.scalar.activation(gate[:, t, h * BANK:(h + 1) * BANK], bank[:, :], ACT.Tanh, scale=0.5)\
                            .then_inc(proj_free, 1)
                for t in range(TT):
                    act.wait_ge(o_turned, i * TT + t + 1)
                    for j in range(2):
                        last = nc.scalar.copy(oT[:, t, 4 * j:4 * j + 4, :],
                                              ps_sc[t][:, j, :].rearrange("p (m q) -> p m q", q=P))
                    last.then_inc(oT_ready, 1)

        @block.vector
        def _(dve):
            dve.sem_inc(feat_free, 2)
            dve.sem_inc(sc_masked, 2)
            dve.sem_inc(att_free, 1)
            dve.sem_inc(out_used, 1)
            dve.wait_ge(slots_set, 2)
            with dve.Fori(0, B) as i:
                steps = Count(i, 2 * PAIRS + 1 + 1)
                for n in range(FEAT):
                    out = (qT, kT)[n % 2][:, 2 * (n // 2):2 * (n // 2) + 2, :].rearrange("p m q -> p (m q)")
                    dve.wait_ge(proj_free, RING + i * PROJ + n + 1)
                    nc.vector.scalar_tensor_tensor(out, ex[:, n % 2, :], 1.0, re[:, n % 2, :], ALU.min, ALU.add)\
                        .then_inc(feat_free, 1)

                def mask_scores(m):
                    dve.wait_ge(sc_ready, i * PAIRS + m + 1)
                    if m >= 2:
                        dve.wait_ge(att_ready, i * PAIRS + m - 1)
                    nc.vector.tensor_tensor(sc[:, m % 2, :, :], ps_sc[m % 2][:, :, 0:SC],
                                            mask[:, :].unsqueeze(1).broadcast_to([P, 2, SC]), ALU.mult)\
                        .then_inc(sc_masked, 1)

                def divide(m):
                    dve.wait_ge(att_ready, i * PAIRS + m + 1)
                    src = ps_att[:, 0:4 * VB].rearrange("p (g e) -> p g e", e=VB)
                    nc.vector.tensor_scalar(den[:, m, :], src[:, :, DH], 1e-6, 2.0, ALU.add, ALU.mult)\
                        .then_inc(dve_step, 1)
                    dve.wait_ge(dve_step, steps.next())
                    nc.vector.reciprocal(rden[:, m, :], den[:, m, :]).then_inc(dve_step, 1)
                    dve.wait_ge(dve_step, steps.next())
                    nc.vector.tensor_tensor(
                        o[:, :, m * P:(m + 1) * P].rearrange("p t (s e) -> p t s e", s=2),
                        src[:, :, 0:DH].rearrange("p (t s) e -> p t s e", t=TT),
                        rden[:, m, :].rearrange("p (t s) -> p t s", t=TT).unsqueeze(3).broadcast_to([P, TT, 2, DH]),
                        ALU.mult).then_inc(att_free, 1)

                mask_scores(0)
                mask_scores(1)
                for m in range(PAIRS):
                    divide(m)
                    if m + 2 < PAIRS:
                        mask_scores(m + 2)
                dve.wait_ge(att_free, 1 + i * PAIRS + PAIRS)
                dve.wait_ge(proj_free, RING + i * PROJ + PROJ)
                for t in range(TT):
                    nc.vector.scalar_tensor_tensor(og[:, t, :], gate[:, t, :], 1.0, o[:, t, :], ALU.add, ALU.mult)\
                        .then_inc(gated, 1)
                dve.wait_ge(out_ready, i + 1)
                nc.vector.tensor_tensor(rows[:, :, :], ps_out[:, :, :], x_all[:, ds(i * TT, TT), :], ALU.add)\
                    .then_inc(out_used, 1)
                dve.wait_ge(out_used, i + 2)
                layernorm_rows(dve, nc, steps, dve_step, rows, stats, mv, rstd, var_ready, rstd_ready, i + 1,
                               lambda t: x_all[:, ds(i * TT + t, 1), :].squeeze(1), TT).then_inc(dve_step, 1)
                dve.wait_ge(dve_step, steps.next())
                steps.close()


def stage_d(nc, c, x_all, out, w, ident, ones_row, consts_ready, mhalf, stored):
    TM = BANK // P
    TURNS = TILES // TM
    C = 4
    MAGIC = 1.5 * 2.0 ** 23

    x_in = c.sb("d_x_in", [P, TM, D])
    xT = c.sb("d_xT", [P, BANK])
    h = c.sb("d_h", [P, C, BANK])
    rows = c.sb("d_rows", [P, TM, D])
    final = c.sb("d_final", [P, TM, D])
    stats = c.sb("d_stats", [P, TM, 6])
    mv = c.sb("d_mv", [P, TM, 2])
    rstd = c.sb("d_rstd", [P, TM])
    total = c.sb("d_total", [P, 2])
    scale = c.sb("d_scale", [P, 2])
    rscale = c.sb("d_rscale", [P, 2])
    ones = c.sb("d_ones", [P, P])
    tern = c.sb("d_tern", [P, 2, BANK])
    wt = [c.sb(f"d_wt{j}", [P, BANK]) for j in range(2)]
    ps_x = c.ps("d_ps_x", [P, BANK])
    ps_h = [c.ps(f"d_ps_h{j}", [P, BANK]) for j in range(4)]
    ps_out = c.ps("d_ps_out", [P, TM, D])
    ps_sum = c.ps("d_ps_sum", [P, 2])

    x_in_ready = c.sem("d_x_in_ready")
    x_turned = c.sem("d_x_turned")
    xT_ready = c.sem("d_xT_ready")
    ones_set = c.sem("d_ones_set")
    total_ready = c.sem("d_total_ready")
    sum_ready = c.sem("d_sum_ready")
    tern_step = c.sem("d_tern_step")
    wt_ready = c.sem("d_wt_ready")
    h_made = c.sem("d_h_made")
    h_ready = c.sem("d_h_ready")
    out_ready = c.sem("d_out_ready")
    out_used = c.sem("d_out_used")
    dve_step = c.sem("d_dve_step")
    var_ready = c.sem("d_var_ready")
    rstd_ready = c.sem("d_rstd_ready")
    final_free = c.sem("d_final_free")
    final_ready = c.sem("d_final_ready")

    with nc.Block() as block:

        @block.sync
        def _(sp):
            with sp.Fori(0, TURNS) as i:
                sp.wait_ge(x_turned, i + 1)
                sp.dma_start(x_in[:, :, :], x_all[:, ds(i * TM, TM), :]).then_inc(x_in_ready, 16)

        @block.gpsimd
        def _(pool):
            nc.gpsimd.memset(ones[:, :], 1.0).then_inc(ones_set, 1)
            out_rows = out.rearrange("b n d -> (b n) d")
            pool.sem_inc(final_free, 1)
            with pool.Fori(0, TURNS) as i:
                pool.wait_ge(var_ready, i + 1)
                nc.gpsimd.tensor_tensor(rstd[:, :], mv[:, :, 1], mhalf[:, 0:TM], ALU.pow).then_inc(rstd_ready, 1)
                pool.wait_ge(final_ready, i + 1)
                pool.dma_start(out_rows[ds(i * BANK, BANK), :].rearrange("(t p) d -> p t d", p=P), final[:, :, :])\
                    .then_inc(stored, 16)
                pool.wait_ge(stored, i * 16 + 16)
                pool.sem_inc(final_free, 1)

        @block.tensor
        def _(pe):
            pe.sem_inc(x_turned, 1)
            pe.wait_ge(consts_ready, CONSTS)
            pe.wait_ge(ones_set, 1)
            pe.wait_ge(total_ready, 1)
            nc.tensor.matmul(ps_sum[:, :], ones[:, :], total[:, :], start=True, stop=True).then_inc(sum_ready, 1)
            pe.wait_ge(wt_ready, 2)
            pe.wait_ge(w["D_ready"], W_D)
            with pe.Fori(0, TURNS) as i:
                pe.wait_ge(x_in_ready, i * 16 + 16)
                for t in range(TM):
                    last = nc.tensor.transpose(ps_x[:, t * P:(t + 1) * P], x_in[:, t, :], ident[:, :])
                last.then_inc(x_turned, 1)
                pe.wait_ge(xT_ready, i + 1)
                for j in range(C):
                    pe.wait_ge(h_ready, i * C + j + 1)
                    nc.tensor.matmul(ps_h[j][:, :], wt[0][:, j * P:(j + 1) * P], xT[:, :], start=True, stop=True)\
                        .then_inc(h_made, 1)
                pe.wait_ge(out_used, i + 1)
                pe.wait_ge(h_ready, C + i * C + C)
                for t in range(TM):
                    for j in range(C):
                        nc.tensor.matmul(ps_out[:, t, :], h[:, j, t * P:(t + 1) * P], wt[1][:, j * P:(j + 1) * P],
                                         start=(j == 0), stop=False)
                    last = nc.tensor.matmul(ps_out[:, t, :], ones_row[:, :], w["D_b2"][:, :], start=False, stop=True)
                last.then_inc(out_ready, 1)

        @block.scalar
        def _(act):
            act.sem_inc(h_ready, C)
            act.wait_ge(w["D_ready"], W_D)
            with act.Fori(0, TURNS) as i:
                act.wait_ge(x_turned, i + 2)
                nc.scalar.copy(xT[:, :], ps_x[:, :]).then_inc(xT_ready, 1)
                for j in range(C):
                    act.wait_ge(h_made, i * C + j + 1)
                    nc.scalar.activation(h[:, j, :], ps_h[j][:, :], ACT.Gelu, bias=w["D_b1"][:, j:j + 1])\
                        .then_inc(h_ready, 1)

        @block.vector
        def _(dve):
            dve.wait_ge(w["D_ready"], W_D)
            for j in range(2):
                last = nc.vector.tensor_reduce(total[:, j:j + 1], w[f"D_W{j + 1}"][:, :], AX_X, ALU.add,
                                               apply_absolute_value=True)
            last.then_inc(total_ready, 1)
            dve.wait_ge(sum_ready, 1)
            n = 0

            def step(ins):
                nonlocal n
                n += 1
                ins.then_inc(tern_step, 1)
                dve.wait_ge(tern_step, n)

            step(nc.vector.tensor_scalar(scale[:, :], ps_sum[:, :], 1.0 / (4 * D * D), 1e-8, ALU.mult, ALU.max))
            step(nc.vector.reciprocal(rscale[:, :], scale[:, :]))
            for j in range(2):
                src, t = w[f"D_W{j + 1}"][:, :], tern[:, j, :]
                step(nc.vector.tensor_scalar(t, src, rscale[:, j:j + 1], None, ALU.mult))
                step(nc.vector.tensor_scalar(t, t, MAGIC, None, ALU.add))
                step(nc.vector.tensor_scalar(t, t, -MAGIC, None, ALU.add))
                step(nc.vector.tensor_scalar(t, t, -1.0, 1.0, ALU.max, ALU.min))
                step(nc.vector.tensor_tensor(t, t, src, ALU.subtract))
                nc.vector.tensor_tensor(wt[j][:, :], src, t, ALU.add).then_inc(wt_ready, 1)
            dve.sem_inc(out_used, 1)
            with dve.Fori(0, TURNS) as i:
                steps = Count(i, 1)
                dve.wait_ge(out_ready, i + 1)
                nc.vector.tensor_tensor(rows[:, :, :], ps_out[:, :, :], x_all[:, ds(i * TM, TM), :], ALU.add)\
                    .then_inc(out_used, 1)
                dve.wait_ge(out_used, i + 2)
                dve.wait_ge(final_free, i + 1)
                layernorm_rows(dve, nc, steps, dve_step, rows, stats, mv, rstd, var_ready, rstd_ready, i + 1,
                               lambda t: final[:, t, :], TM).then_inc(final_ready, 1)
                dve.wait_ge(final_ready, i + 1)
                steps.close()


CONSTS = 4
W_B = 16 * 12
W_C = 16 * 3
W_D = 16 * 4


def two_blocks(nc, a, out, stages="ABCD"):
    with ExitStack() as stack:
        c = Chip(nc, stack)
        x_all = c.sb("x_all", [P, TILES, D])
        ident = c.sb("ident", [P, P])
        ones_row = c.sb("ones_row", [1, P])
        mhalf = c.sb("mhalf", [P, 8])
        consts_ready = c.sem("consts_ready")
        consts_step = c.sem("consts_step")
        x_dram = a["L0_attn_x"].rearrange("b n d -> (b n) d")

        w = {}
        w["A_ready"] = c.sem("A_ready")
        for n in "qkv":
            w["A_" + n] = c.sb("A_w" + n, [P, HD])
        w["A_o"] = c.sb("A_wo", [P, PAIRS, D])
        w["A_bo"] = c.sb("A_bo", [1, D])

        w["B_ready"] = c.sem("B_ready")
        for n in "qk":
            w["B_" + n] = c.sb("B_w" + n, [P, 4, 4, 32])
        w["B_v"] = c.sb("B_wv", [P, D])
        w["B_gate"] = c.sb("B_gate", [P, 8])
        w["B_W1"] = c.sb("B_W1", [P, 8, 4 * D])
        w["B_W2"] = c.sb("B_W2", [P, 32, D])
        w["B_b1"] = c.sb("B_b1", [P, 32])
        w["B_b2"] = c.sb("B_b2", [8, D])
        lnrow = c.sb("B_lnrow", [P, 4, D])
        w["C_ready"] = c.sem("C_ready")
        w["C_qkv"] = c.sb("C_qkv", [P, 3 * HD])
        w["C_gate"] = c.sb("C_gate", [P, HD])
        w["C_out"] = c.sb("C_out", [P, PAIRS, D])
        w["D_ready"] = c.sem("D_ready")
        w["D_W1"] = c.sb("D_W1", [P, 4 * D])
        w["D_W2"] = c.sb("D_W2", [P, 4 * D])
        w["D_b1"] = c.sb("D_b1", [P, 4])
        w["D_b2"] = c.sb("D_b2", [1, D])
        y_all = c.sb("y_all", [P, TILES, D])

        with nc.Block() as block:

            @block.sync
            def _(sp):
                for n in "kvq":
                    sp.dma_start(w["A_" + n][:, :], a["L0_attn_W" + n]).then_inc(w["A_ready"], 16)
                sp.dma_start(w["A_o"][:, :, :], a["L0_attn_Wo"].rearrange("(m p) n -> p m n", p=P))\
                    .then_inc(w["A_ready"], 16)
                sp.dma_start(w["A_bo"][:, :], a["L0_attn_bo"].rearrange("(a n) -> a n", a=1))\
                    .then_inc(w["A_ready"], 16)

                sp.dma_start(w["C_qkv"][:, :], a["L1_attn_w_qkv"]).then_inc(w["C_ready"], 16)
                sp.dma_start(w["C_gate"][:, :], a["L1_attn_w_gate"]).then_inc(w["C_ready"], 16)
                sp.dma_start(w["C_out"][:, :, :], a["L1_attn_w_out"].rearrange("(m p) n -> p m n", p=P))\
                    .then_inc(w["C_ready"], 16)
                sp.dma_start(w["D_W1"][:, :], a["L1_ffn_W1"]).then_inc(w["D_ready"], 16)
                sp.dma_start(w["D_W2"][:, :].rearrange("p (j d) -> p j d", d=D),
                             a["L1_ffn_W2"].rearrange("(j p) d -> p j d", p=P)).then_inc(w["D_ready"], 16)
                sp.dma_start(w["D_b1"][:, :], a["L1_ffn_b1"]).then_inc(w["D_ready"], 16)
                sp.dma_start(w["D_b2"][:, :], a["L1_ffn_b2"].rearrange("(a n) -> a n", a=1))\
                    .then_inc(w["D_ready"], 16)

            @block.scalar
            def _(act):
                act.wait_ge(consts_step, 2)
                for n in "qk":
                    act.dma_start(w["B_" + n][:, :, :, 0:8].rearrange("p g h f -> p (g h) f"), a["L0_ffn_W" + n],
                                  allow_slow_non_contiguous=True).then_inc(w["B_ready"], 16)
                act.dma_start(w["B_v"][:, :], a["L0_ffn_Wv"].rearrange("p h f -> p (h f)")).then_inc(w["B_ready"], 16)
                act.dma_start(w["B_gate"][:, :], a["L0_ffn_gate_W"]).then_inc(w["B_ready"], 16)
                for j, n in enumerate(("ln1_g", "ln1_b", "ln2_g", "ln2_b")):
                    act.dma_start(lnrow[:, j, :], a["L0_ffn_" + n].partition_broadcast(P)).then_inc(w["B_ready"], 16)
                act.dma_start(w["B_b1"][:, :], a["L0_ffn_b1"]).then_inc(w["B_ready"], 16)
                act.dma_start(w["B_b2"][:, :], a["L0_ffn_b2"]).then_inc(w["B_ready"], 16)
                act.dma_start(w["B_W1"][:, :, :], a["L0_ffn_W1"].rearrange("e p f -> p e f")).then_inc(w["B_ready"], 16)
                act.dma_start(w["B_W2"][:, :, :], a["L0_ffn_W2"].rearrange("e (j p) d -> p (e j) d", p=P))\
                    .then_inc(w["B_ready"], 16)

            @block.gpsimd
            def _(pool):
                for n in "qk":
                    nc.gpsimd.memset(w["B_" + n][:, :, :, :], 0.0).then_inc(consts_step, 1)
                nc.gpsimd.memset(ident[:, :], 0.0).then_inc(consts_step, 1)
                nc.gpsimd.memset(ones_row[:, :], 1.0).then_inc(consts_ready, 1)
                nc.gpsimd.memset(mhalf[:, :], -0.5).then_inc(consts_ready, 1)
                pool.wait_ge(consts_step, 3)
                nc.gpsimd.affine_select(out=ident[:, :], in_=ident[:, :], compare_op=ALU.not_equal, fill=1.0,
                                        base=0, pattern=[[-1, P]], channel_multiplier=1).then_inc(consts_ready, 2)

        def stage(f, *args):
            with ExitStack() as inner:
                f(nc, Chip(nc, inner), *args)

        if "A" in stages:
            stage(stage_a, x_dram, x_all, w, ident, ones_row, mhalf, consts_ready)
        if "b" in stages:
            stage(stage_b_attention, x_all, y_all, w, ident, consts_ready, mhalf, lnrow)
        if "B" in stages:
            stage(stage_b_experts, x_all, y_all, w, ident, consts_ready, mhalf, lnrow)
        if "C" in stages:
            stage(stage_c, x_all, w, ident, consts_ready, mhalf)
        stored = c.sem("stored")
        if "D" in stages:
            stage(stage_d, x_all, out, w, ident, ones_row, consts_ready, mhalf, stored)
            n_stored = 16 * (TILES // 4)
        else:
            n_stored = 16
        with nc.Block() as block:
            @block.sync
            def _(sp):
                if "D" not in stages:
                    sp.dma_start(out.rearrange("b (t p) d -> p (b t) d", p=P), x_all[:, :, :]).then_inc(stored, 16)
                sp.wait_ge(stored, n_stored)


_INS = ['L0_attn_x', 'L0_attn_Wq', 'L0_attn_Wk', 'L0_attn_Wv', 'L0_attn_Wo', 'L0_attn_bo',
        'L0_ffn_Wq', 'L0_ffn_Wk', 'L0_ffn_Wv', 'L0_ffn_gate_W', 'L0_ffn_W1', 'L0_ffn_b1', 'L0_ffn_W2', 'L0_ffn_b2',
        'L0_ffn_ln1_g', 'L0_ffn_ln1_b', 'L0_ffn_ln2_g', 'L0_ffn_ln2_b',
        'L1_attn_w_qkv', 'L1_attn_w_gate', 'L1_attn_w_out', 'L1_ffn_W1', 'L1_ffn_b1', 'L1_ffn_W2', 'L1_ffn_b2']
_OUTS = [((B, N, D), 'float32')]


def kernel(**inputs):
    import numpy as _np
    import concourse.bacc as _bacc
    from concourse import mybir as _mybir
    from concourse.bass_utils import run_bass_kernel_spmd as _run

    nc = _bacc.Bacc("TRN2", target_bir_lowering=False, num_devices=1)
    arrays, args = {}, {}
    for name in _INS:
        a = _np.asarray(inputs[name])
        if name in ('L0_ffn_Wq', 'L0_ffn_Wk', 'L0_ffn_Wv'):
            a = a.transpose(1, 0, 2)
        if name in ('L1_ffn_W1', 'L1_ffn_W2'):
            a = a.T
        if name in ('L0_ffn_b1', 'L1_ffn_b1'):
            a = a.reshape(-1, 128).T
        a = _np.ascontiguousarray(a)
        arrays[f"in_{name}_dram"] = a
        args[name] = nc.dram_tensor(f"in_{name}_dram", a.shape, _mybir.dt.from_np(a.dtype), kind="ExternalInput").ap()
    shape, dtype = _OUTS[0]
    out = nc.dram_tensor("out_0_dram", shape, _mybir.dt.from_np(_np.dtype(dtype)), kind="ExternalOutput").ap()
    two_blocks(nc, args, out, "AbBCD")
    r = _run(nc, [arrays], core_ids=[0])
    return r.results[0]["out_0_dram"]
```

```python
from contextlib import ExitStack

import concourse.bass as bass
from concourse import mybir

F32 = mybir.dt.float32
BF16 = mybir.dt.bfloat16
F16 = mybir.dt.float16
U32 = mybir.dt.uint32
ALU = mybir.AluOpType
ACT = mybir.ActivationFunctionType
AX_X = mybir.AxisListType.X
ds = bass.ds

P = 128
BANK = 512
B, N, D = 16, 256, 128
TT = N // P
TILES = B * TT
H, DH = 16, 64
PAIRS = H // 2
HD = H * DH
LN_EPS = 1e-5


class Count:

    def __init__(self, turn, per_turn):
        self.base, self.per_turn, self.n = turn * per_turn, per_turn, 0

    def next(self):
        self.n += 1
        return self.base + self.n

    def close(self):
        assert self.n == self.per_turn, (self.n, self.per_turn)


class Chip:

    def __init__(self, nc, stack):
        self.nc, self.stack = nc, stack

    def sb(self, name, shape, dt=F32):
        return self.stack.enter_context(self.nc.sbuf_tensor(name, shape, dt))

    def ps(self, name, shape, dt=F32):
        return self.stack.enter_context(self.nc.psum_tensor(name, shape, dt))

    def sem(self, name):
        return self.stack.enter_context(self.nc.semaphore(name))



def layernorm_rows(dve, nc, steps, dve_step, rows, stats, mv, rstd, var_ready, rstd_ready, rounds, out, tiles):
    for t in range(tiles):
        nc.vector.bn_stats(stats[:, t, :], rows[:, t, :])
    dve.drain()
    for t in range(tiles):
        ins = nc.vector.bn_aggr(mv[:, t, :], stats[:, t, :])
    ins.then_inc(dve_step, 1)
    dve.wait_ge(dve_step, steps.next())
    nc.vector.tensor_scalar(mv[:, :, 1], mv[:, :, 1], LN_EPS, None, ALU.add).then_inc(var_ready, 1)
    dve.wait_ge(rstd_ready, rounds)
    for t in range(tiles):
        last = nc.vector.tensor_scalar(out(t), rows[:, t, :], mv[:, t, 0:1], rstd[:, t:t + 1],
                                       ALU.subtract, ALU.mult)
    return last


def each_batch(eng, body):
    for b in range(2):
        body(b, b, b == 0, True, True)
    with eng.Fori(1, B // 2 - 1) as i:
        for p in range(2):
            body(2 * i + p, p, False, True, True)
    for p in range(2):
        b = B - 2 + p
        body(b, p, False, b + 1 < B, b + 2 < B)


def zero(b):
    return isinstance(b, int) and b == 0


def row_variance(dve, nc, rows, stats, mv, tiles, step, value, var_ready):
    for t in range(tiles):
        nc.vector.bn_stats(stats[:, t, :], rows[:, t, :])
    dve.drain()
    for t in range(tiles):
        ins = nc.vector.bn_aggr(mv[:, t, :], stats[:, t, :])
    ins.then_inc(step, 1)
    dve.wait_ge(step, value)
    nc.vector.tensor_scalar(mv[:, :, 1], mv[:, :, 1], LN_EPS, None, ALU.add).then_inc(var_ready, 1)


def row_normalise(nc, rows, mv, rstd, tiles, out):
    for t in range(tiles):
        last = nc.vector.tensor_scalar(out(t), rows[:, t, :], mv[:, t, 0:1], rstd[:, t:t + 1],
                                       ALU.subtract, ALU.mult)
    return last


def stage_a(nc, c, a, x_all, w, wa, ident, ones_row, mhalf, consts_ready):
    VB = 2 * DH + 2
    RING = 3
    UNIT = TT * (HD // BANK)
    PROJ = 3 * UNIT
    FEAT = 2 * UNIT
    KVG = [(0, 2), (2, 4), (4, 6), (6, 8)]
    APG = [(0, 3), (3, 6), (6, 8)]
    MIX = len(KVG) + TT * len(APG)
    SCALE = 1.0 / 64
    assert PROJ % RING == 0 and MIX % 2 == 0 and MIX <= PROJ

    x_in = c.sb("a_x_in", [P, 2, TT, D])
    w_full = c.sb("a_w_full", [P, 3, HD])
    wh = c.sb("a_wh", [P, 3, HD], F16)
    wl = c.sb("a_wl", [P, 3, HD], F16)
    xTh = c.sb("a_xTh", [P, 2, N], F16)
    xTl = c.sb("a_xTl", [P, 2, N], F16)
    k = c.sb("a_k", [P, 2, TT, HD])
    v = c.sb("a_v", [P, 2, TT, PAIRS, VB])
    qT = c.sb("a_qT", [P, 2, PAIRS, N])
    kv = c.sb("a_kv", [P, PAIRS, VB])
    ex = c.sb("a_exp", [P, 2, BANK])
    re = c.sb("a_relu", [P, 2, BANK])
    den = c.sb("a_den", [P, MIX, 6])
    rden = c.sb("a_rden", [P, MIX, 6])
    on = c.sb("a_on", [P, TT, HD])
    onT = c.sb("a_onT", [P, TT, PAIRS, P])
    rows = c.sb("a_rows", [P, TT, D])
    stats = c.sb("a_stats", [P, TT, 6])
    mv = c.sb("a_mv", [P, TT, 2])
    rstd = c.sb("a_rstd", [P, TT])
    piece = c.sb("a_piece", [P, 2, PIECE])
    qkv = c.sb("a_B_qkv", [P, 3 * D])
    PEELED = 2
    assert PIECES == B - 2 * PEELED
    ps_proj = [c.ps(f"a_ps_proj{j}", [P, BANK]) for j in range(RING)]
    ps_mix = [c.ps(f"a_ps_mix{j}", [P, BANK]) for j in range(2)]
    ps_turn = [c.ps(f"a_ps_turn{j}", [P, BANK]) for j in range(2)]
    ps_out = c.ps("a_ps_out", [P, TT, D])

    x_in_ready = [c.sem(f"a_x_in_ready{j}") for j in range(2)]
    x_all_ready = c.sem("a_x_all_ready")
    w_ready = [c.sem(f"a_w_ready{j}") for j in range(3)]
    wh_ready = c.sem("a_wh_ready")
    wl_ready = c.sem("a_wl_ready")
    x_turned = c.sem("a_x_turned")
    xTh_ready = c.sem("a_xTh_ready")
    xTl_ready = c.sem("a_xTl_ready")
    slots_set = c.sem("a_slots_set")
    proj_ready = c.sem("a_proj_ready")
    proj_free = c.sem("a_proj_free")
    feat_free = c.sem("a_feat_free")
    mix_ready = c.sem("a_mix_ready")
    mix_free = c.sem("a_mix_free")
    on_turned = c.sem("a_on_turned")
    onT_ready = c.sem("a_onT_ready")
    out_ready = c.sem("a_out_ready")
    out_used = c.sem("a_out_used")
    den_step = c.sem("a_den_step")
    mv_ready = c.sem("a_mv_ready")
    var_ready = c.sem("a_var_ready")
    rstd_ready = c.sem("a_rstd_ready")
    rows_done = c.sem("a_rows_done")
    piece_ready = [c.sem(f"a_piece_ready{j}") for j in range(2)]
    piece_upper = c.sem("a_piece_upper")
    qkv_ready = c.sem("a_B_qkv_ready")
    qkv_upper = c.sem("a_B_qkv_upper")

    x_dram = a["L0_attn_x"].rearrange("b n d -> (b n) d")

    with nc.Block() as block:

        @block.sync
        def _(sp):
            def load(b, p):
                sp.dma_start(x_in[:, p, :, :], x_dram[ds(b * N, N), :].rearrange("(t p) d -> p t d", p=P))\
                  .then_inc(x_in_ready[p], 16)

            load(0, 0)
            for j, n in enumerate("kqv"):
                sp.dma_start(w_full[:, j, :], a["L0_attn_W" + n]).then_inc(w_ready[j], 16)
            load(1, 1)
            sp.dma_start(wa["o"][:, :, :], a["L0_attn_Wo"].rearrange("(m p) n -> p m n", p=P)).then_inc(wa["ready"], 16)
            sp.dma_start(wa["bo"][:, :], a["L0_attn_bo"].rearrange("(a n) -> a n", a=1)).then_inc(wa["ready"], 16)
            sp.dma_start(x_all[:, :, :], x_dram.rearrange("(t p) d -> p t d", p=P)).then_inc(x_all_ready, 16)
            for j, n in enumerate("qkv"):
                sp.dma_start(qkv[:, j * D:(j + 1) * D], a["L0_ffn_W" + n].rearrange("p h f -> p (h f)"))\
                    .then_inc(qkv_ready, 16)
            load_small_weights(sp, a, w)
            with sp.Fori(0, B // 2 - 1) as i:
                for p in range(2):
                    sp.wait_ge(x_turned, 2 * i + p + 1)
                    load(2 * i + p + 2, p)

        @block.gpsimd
        def _(pool):
            nc.gpsimd.memset(kv[:, :, :], 0.0).then_inc(slots_set, 1)
            nc.gpsimd.memset(v[:, :, :, :, 0:1], 1.0).then_inc(slots_set, 1)
            nc.gpsimd.memset(v[:, :, :, :, VB - 1:VB], 1.0).then_inc(slots_set, 1)
            def load(n):
                pool.dma_start(*weight_piece(a, n, piece[:, n % 2, :])).then_inc(piece_ready[n % 2], 16)

            def power(b):
                pool.wait_ge(var_ready, b + 1)
                nc.gpsimd.tensor_tensor(rstd[:, :], mv[:, :, 1], mhalf[:, 0:TT], ALU.pow).then_inc(rstd_ready, 1)

            load(0)
            load(1)
            for b in range(B):
                power(b)
                if 1 <= b and b + 1 < PIECES:
                    pool.wait_ge(w["split"], b)
                    load(b + 1)

        @block.tensor
        def _(pe):
            pe.wait_ge(consts_ready, CONSTS)
            pe.wait_ge(slots_set, 3)

            def turn_x(b, p):
                pe.wait_ge(x_in_ready[p], (b - p) * 8 + 16)
                for t in range(TT):
                    last = nc.tensor.transpose(ps_turn[0][:, t * P:(t + 1) * P], x_in[:, p, t, :], ident[:, :])
                last.then_inc(x_turned, 1)

            def halves(out, lhs_h, lhs_l, rhs_h, rhs_l):
                nc.tensor.matmul(out, lhs_h, rhs_h, start=True, stop=False)
                nc.tensor.matmul(out, lhs_h, rhs_l, start=False, stop=False)
                return nc.tensor.matmul(out, lhs_l, rhs_h, start=False, stop=True)

            def project(b, p, u):
                if u == 0:
                    pe.wait_ge(xTl_ready, b + 1)
                pe.wait_ge(proj_free, b * PROJ + u + 1)
                bank = ps_proj[u % RING]
                kind, r = divmod(u, UNIT)
                if zero(b) and r == 0:
                    pe.wait_ge(wl_ready, kind + 1)
                if kind == 1:
                    for s in range(2):
                        m = slice((2 * r + s) * P, (2 * r + s + 1) * P)
                        last = halves(bank[:, s * N:(s + 1) * N], wh[:, 1, m], wl[:, 1, m], xTh[:, p, :], xTl[:, p, :])
                else:
                    t, h = divmod(r, HD // BANK)
                    m, s = slice(h * BANK, (h + 1) * BANK), slice(t * P, (t + 1) * P)
                    last = halves(bank[:, :], xTh[:, p, s], xTl[:, p, s], wh[:, kind, m], wl[:, kind, m])
                last.then_inc(proj_ready, 1)

            def key_values(b, p, n):
                if n == 0:
                    pe.wait_ge(feat_free, 2 + b * FEAT + UNIT)
                    pe.wait_ge(proj_free, RING + b * PROJ + PROJ)
                pe.wait_ge(mix_free, b * MIX + n + 1)
                m0, m1 = KVG[n]
                for m in range(m0, m1):
                    for t in range(TT):
                        last = nc.tensor.matmul(ps_mix[n % 2][:, (m - m0) * VB:(m - m0 + 1) * VB],
                                                k[:, p, t, m * P:(m + 1) * P], v[:, p, t, m, :],
                                                start=(t == 0), stop=(t == TT - 1))
                last.then_inc(mix_ready, 1)

            def query(b, p, n):
                if n == len(KVG):
                    pe.wait_ge(feat_free, 2 + b * FEAT + FEAT)
                t, g = divmod(n - len(KVG), len(APG))
                m0, m1 = APG[g]
                pe.wait_ge(mix_free, b * MIX + n + 1)
                pe.wait_ge(mix_free, 2 + b * MIX + min((m1 + 1) // 2, len(KVG)))
                for m in range(m0, m1):
                    last = nc.tensor.matmul(ps_mix[n % 2][:, (m - m0) * VB:(m - m0 + 1) * VB],
                                            qT[:, p, m, t * P:(t + 1) * P], kv[:, m, :], start=True, stop=True)
                last.then_inc(mix_ready, 1)

            def turn_on(b, j):
                t, half = divmod(j, 2)
                if j == 0:
                    pe.wait_ge(mix_free, 2 + b * MIX + MIX)
                    pe.wait_ge(xTl_ready, min(b + 3, B) if isinstance(b, int) else b + 3)
                elif j == 1:
                    if not zero(b):
                        pe.wait_ge(onT_ready, b * 4)
                else:
                    pe.wait_ge(onT_ready, b * 4 + j - 1)
                for i in range(4):
                    m = 4 * half + i
                    last = nc.tensor.transpose(ps_turn[j % 2][:, i * P:(i + 1) * P], on[:, t, m * P:(m + 1) * P],
                                               ident[:, :])
                last.then_inc(on_turned, 1)

            def out_part(b, j):
                t, half = divmod(j, 2)
                pe.wait_ge(onT_ready, b * 4 + j + 1)
                if j == 0:
                    pe.wait_ge(wa["ready"], W_A)
                    if not zero(b):
                        pe.wait_ge(out_used, b)
                for i in range(4):
                    m = 4 * half + i
                    nc.tensor.matmul(ps_out[:, t, :], onT[:, t, m, :], wa["o"][:, m, :], start=(m == 0), stop=False)
                if half == 1:
                    last = nc.tensor.matmul(ps_out[:, t, :], ones_row[:, :], wa["bo"][:, :], start=False, stop=True)
                    if t == TT - 1:
                        last.then_inc(out_ready, 1)

            def batch(b, p, first, next1, next2):
                for m in range(PROJ):
                    if next1:
                        project(b + 1, 1 - p, m)
                    if not first and m < 4:
                        turn_on(b - 1, m)
                    if m < len(KVG):
                        key_values(b, p, m)
                    elif m < MIX:
                        query(b, p, m)
                    if not first and 1 <= m < 5:
                        out_part(b - 1, m - 1)
                    if m == 5 and next2:
                        if not first:
                            pe.wait_ge(onT_ready, 4 * b)
                        turn_x(b + 2, p)

            turn_x(0, 0)
            for u in range(PROJ):
                project(0, 0, u)
            turn_x(1, 1)
            each_batch(pe, batch)
            for j in range(4):
                turn_on(B - 1, j)
                out_part(B - 1, j)

        @block.scalar
        def _(act):
            act.sem_inc(proj_free, RING)
            act.wait_ge(consts_ready, CONSTS)
            nc.scalar.activation(re[:, 0, 0:1], ident[:, 0:1], ACT.Exp)

            def split_upper(j):
                act.wait_ge(w_ready[j], 16)
                nc.scalar.mul(wh[:, j, :], w_full[:, j, :], W_SCALE).then_inc(wh_ready, 1)

            def piece_hi(b, p):
                act.wait_ge(piece_ready[p], (b - PEELED - p) * 8 + 16)
                nc.scalar.mul(w["h"][:, ds((b - PEELED) * PIECE, PIECE)], piece[:, p, :], W_SCALE)\
                    .then_inc(piece_upper, 1)

            def x_hi(b, p):
                act.wait_ge(x_turned, b + 1)
                if not (isinstance(b, int) and b < 2):
                    act.wait_ge(proj_ready, (b - 1) * PROJ)
                nc.scalar.copy(xTh[:, p, :], ps_turn[0][:, 0:N]).then_inc(xTh_ready, 1)

            def take(b, p, u):
                bank = ps_proj[u % RING]
                act.wait_ge(proj_ready, b * PROJ + u + 1)
                if u >= FEAT:
                    t, h = divmod(u - FEAT, HD // BANK)
                    nc.scalar.mul(v[:, p, t, 4 * h:4 * h + 4, 1:1 + P], bank[:, :].rearrange("p (m e) -> p m e", e=P),
                                  SCALE).then_inc(proj_free, 1)
                else:
                    act.wait_ge(feat_free, b * FEAT + u + 1)
                    nc.scalar.activation(ex[:, u % 2, :], bank[:, :], ACT.Exp, scale=SCALE)
                    nc.scalar.activation(re[:, u % 2, :], bank[:, :], ACT.Relu, scale=SCALE).then_inc(proj_free, 1)

            def take_on(b, j):
                t, half = divmod(j, 2)
                if j == 0 and not zero(b):
                    act.wait_ge(out_ready, b)
                act.wait_ge(on_turned, b * 4 + j + 1)
                nc.scalar.copy(onT[:, t, 4 * half:4 * half + 4, :],
                               ps_turn[j % 2][:, :].rearrange("p (m q) -> p m q", q=P)).then_inc(onT_ready, 1)

            def batch(b, p, first, next1, next2):
                for m in range(PROJ):
                    if next1:
                        take(b + 1, 1 - p, m)
                    if not first and m < 4:
                        take_on(b - 1, m)
                    if m == 6 and next2:
                        x_hi(b + 2, p)
                    if m == FEAT and not isinstance(b, int):
                        piece_hi(b, p)
                if first:
                    act.wait_ge(qkv_ready, 3 * 16)
                    nc.scalar.mul(w["B_wh"][:, :], qkv[:, :], W_SCALE).then_inc(qkv_upper, 1)

            split_upper(0)
            x_hi(0, 0)
            split_upper(1)
            split_upper(2)
            for u in range(PROJ):
                take(0, 0, u)
            x_hi(1, 1)
            each_batch(act, batch)
            for j in range(4):
                take_on(B - 1, j)

        @block.vector
        def _(dve):
            dve.sem_inc(feat_free, 2)
            dve.sem_inc(mix_free, 2)
            dve.wait_ge(slots_set, 3)

            def split_lower(j):
                dve.wait_ge(wh_ready, j + 1)
                nc.vector.scalar_tensor_tensor(wl[:, j, :], w_full[:, j, :], W_SCALE, wh[:, j, :],
                                               ALU.mult, ALU.subtract).then_inc(wl_ready, 1)

            def piece_lo(b, p):
                dve.wait_ge(piece_upper, b - PEELED + 1)
                at = ds((b - PEELED) * PIECE, PIECE)
                nc.vector.scalar_tensor_tensor(w["l"][:, at], piece[:, p, :], W_SCALE, w["h"][:, at],
                                               ALU.mult, ALU.subtract).then_inc(w["split"], 1)

            def x_lo(b, p):
                dve.wait_ge(xTh_ready, b + 1)
                nc.vector.tensor_tensor(xTl[:, p, :], ps_turn[0][:, 0:N], xTh[:, p, :], ALU.subtract)\
                    .then_inc(xTl_ready, 1)

            def feature(b, p, u):
                kind, r = divmod(u, UNIT)
                t, h = divmod(r, HD // BANK)
                out = (k[:, p, t, h * BANK:(h + 1) * BANK],
                       qT[:, p, 2 * r:2 * r + 2, :].rearrange("p m q -> p (m q)"))[kind]
                dve.wait_ge(proj_free, RING + b * PROJ + u + 1)
                nc.vector.scalar_tensor_tensor(out, ex[:, u % 2, :], 1.0, re[:, u % 2, :], ALU.min, ALU.add)\
                    .then_inc(feat_free, 1)

            def take_kv(b, n):
                m0, m1 = KVG[n]
                dve.wait_ge(mix_ready, b * MIX + n + 1)
                src = ps_mix[n % 2][:, 0:(m1 - m0) * VB].rearrange("p (m e) -> p m e", e=VB)
                nc.vector.tensor_copy(kv[0:DH, m0:m1, 0:DH + 1], src[0:DH, :, 0:DH + 1])
                nc.vector.tensor_copy(kv[DH:P, m0:m1, DH + 1:VB], src[DH:P, :, DH + 1:VB]).then_inc(mix_free, 1)

            def divide(b, n):
                t, g = divmod(n - len(KVG), len(APG))
                m0, m1 = APG[g]
                ms, step = m1 - m0, b * 2 * (MIX - len(KVG)) + 2 * (n - len(KVG))
                if n == len(KVG) and not zero(b):
                    dve.wait_ge(on_turned, 4 * b)
                dve.wait_ge(mix_ready, b * MIX + n + 1)
                src = ps_mix[n % 2][:, 0:ms * VB].rearrange("p (m e) -> p m e", e=VB)
                d = den[:, n, 0:2 * ms].rearrange("p (m s) -> p m s", s=2)
                r = rden[:, n, 0:2 * ms].rearrange("p (m s) -> p m s", s=2)
                nc.vector.tensor_scalar(d, src[:, :, 0:VB:VB - 1], 1e-6, None, ALU.add).then_inc(den_step, 1)
                dve.wait_ge(den_step, step + 1)
                nc.vector.reciprocal(r, d).then_inc(den_step, 1)
                dve.wait_ge(den_step, step + 2)
                nc.vector.tensor_tensor(
                    on[:, t, m0 * P:m1 * P].rearrange("p (m s e) -> p m s e", s=2, e=DH),
                    src[:, :, 1:1 + P].rearrange("p m (s e) -> p m s e", s=2),
                    r.unsqueeze(3).broadcast_to([P, ms, 2, DH]), ALU.mult).then_inc(mix_free, 1)

            def add_residual(b):
                if not zero(b):
                    dve.wait_ge(rows_done, b)
                dve.wait_ge(out_ready, b + 1)
                nc.vector.tensor_tensor(rows[:, :, :], ps_out[:, :, :], x_all[:, ds(b * TT, TT), :], ALU.add)\
                    .then_inc(out_used, 1)

            def variance(b):
                dve.wait_ge(out_used, b + 1)
                row_variance(dve, nc, rows, stats, mv, TT, mv_ready, b + 1, var_ready)

            def normalise(b):
                dve.wait_ge(rstd_ready, b + 1)
                row_normalise(nc, rows, mv, rstd, TT,
                              lambda t: x_all[:, ds(b * TT + t, 1), :].squeeze(1)).then_inc(rows_done, 1)

            def batch(b, p, first, next1, next2):
                for m in range(PROJ):
                    if m < len(KVG):
                        take_kv(b, m)
                    elif m < MIX:
                        divide(b, m)
                    if next1 and m < FEAT:
                        feature(b + 1, 1 - p, m)
                    if m == 5 and not first:
                        add_residual(b - 1)
                    if m == MIX and not first:
                        variance(b - 1)
                    if m == 6 and next2:
                        x_lo(b + 2, p)
                    if m == PROJ - 1 and not first:
                        normalise(b - 1)
                    if m == FEAT + 1 and not isinstance(b, int):
                        piece_lo(b, p)
                if first:
                    dve.wait_ge(qkv_upper, 1)
                    nc.vector.scalar_tensor_tensor(w["B_wl"][:, :], qkv[:, :], W_SCALE, w["B_wh"][:, :],
                                                   ALU.mult, ALU.subtract).then_inc(w["B_split"], 1)

            split_lower(0)
            x_lo(0, 0)
            split_lower(1)
            split_lower(2)
            for u in range(FEAT):
                feature(0, 0, u)
            x_lo(1, 1)
            dve.wait_ge(x_all_ready, 16)
            each_batch(dve, batch)
            add_residual(B - 1)
            variance(B - 1)
            normalise(B - 1)
            dve.wait_ge(rows_done, B)


def stage_b_attention(nc, c, x_all, y_all, w, ident, consts_ready, mhalf, lnrow):
    G, HH, F = 4, 4, 8
    CH = 32
    MROW = 3 * F
    SC = 3 * P
    EXP_SCALE = 8 * float(D) ** -0.5
    SIDE = 7
    QKV0, QKV1, TQ, TK, BACK0, BACK1, TX = -1, 1, 2, 3, 4, 5, 6

    x_in = c.sb("b_x_in", [P, 2, TT, D])
    xTh = c.sb("b_xTh", [P, N], F16)
    xTl = c.sb("b_xTl", [P, N], F16)
    qs = c.sb("b_qs", [P, TT, G * HH, CH], F16)
    ks = c.sb("b_ks", [P, TT, G * HH, CH], F16)
    qsT = c.sb("b_qsT", [P, 2, G, N], F16)
    ksT = c.sb("b_ksT", [P, 2, G, N], F16)
    qmT = c.sb("b_qmT", [P, 2, N], F16)
    v = c.sb("b_v", [P, 2, TT, G * HH, 32])
    v_next = c.sb("b_v_next", [P, TT, D])
    negmax = c.sb("b_negmax", [P, 2, TT, HH, CH], F16)
    probs = c.sb("b_probs", [P, 2, HH, SC])
    oT = c.sb("b_oT", [P, G, N])
    rsum = c.sb("b_rsum", [P, TT, G * HH])
    attn = c.sb("b_attn", [P, TT, D])
    z = c.sb("b_z", [P, TT, D])
    zg = c.sb("b_zg", [P, TT, D])
    xb = c.sb("b_xb", [P, 2, TT, D])
    stats = c.sb("b_stats", [P, TT, 6])
    mv = c.sb("b_mv", [P, TT, 2])
    rstd = c.sb("b_rstd", [P, TT])
    mask = c.sb("b_mask", [P, 2, P], BF16)
    identb = c.sb("b_identb", [P, P], BF16)
    identh = c.sb("b_identh", [P, P], F16)
    turn_mark = c.sb("b_turn_mark", [P, 6])
    ps_sc = c.ps("b_ps_sc", [P, HH, BANK])
    ps_st = [c.ps(f"b_ps_st{j}", [P, BANK]) for j in range(2)]
    ps_pv = c.ps("b_ps_pv", [P, 2, N])
    ps_side = c.ps("b_ps_side", [P, BANK])
    side_h = ps_side[:, :].bitcast(F16)
    ps_mx = ps_st[0][:, SC:BANK].bitcast(F16)

    x_in_ready = [c.sem(f"b_x_in_ready{j}") for j in range(2)]
    x_turned = c.sem("b_x_turned")
    xb_ready = c.sem("b_xb_ready")
    v_ready = c.sem("b_v_ready")
    set_step = c.sem("b_set_step")
    slots_set = c.sem("b_slots_set")
    xTh_ready = c.sem("b_xTh_ready")
    xTl_ready = c.sem("b_xTl_ready")
    qkv_made = c.sem("b_qkv_made")
    hi_ready = c.sem("b_hi_ready")
    lo_ready = c.sem("b_lo_ready")
    stacks_turned = c.sem("b_stacks_turned")
    qsT_ready = c.sem("b_qsT_ready")
    ksT_ready = c.sem("b_ksT_ready")
    scores_ready = c.sem("b_scores_ready")
    max_ready = c.sem("b_max_ready")
    max_turned = c.sem("b_max_turned")
    qmT_ready = c.sem("b_qmT_ready")
    st_ready = c.sem("b_st_ready")
    st_free = c.sem("b_st_free")
    masked = c.sem("b_masked")
    pv_ready = c.sem("b_pv_ready")
    oT_ready = c.sem("b_oT_ready")
    back_ready = c.sem("b_back_ready")
    back_read = c.sem("b_back_read")
    dve_step = c.sem("b_dve_step")
    var_ready = c.sem("b_var_ready")
    rstd_ready = c.sem("b_rstd_ready")
    z_ready = c.sem("b_z_ready")
    zg_ready = c.sem("b_zg_ready")
    y_ready = c.sem("b_y_ready")

    with nc.Block() as block:

        @block.sync
        def _(sp):
            def load(b, p):
                sp.dma_start(x_in[:, p, :, :], x_all[:, ds(b * TT, TT), :]).then_inc(x_in_ready[p], 16)

            load(0, 0)
            load(1, 1)
            with sp.Fori(0, B // 2 - 1) as i:
                for p in range(2):
                    b = 2 * i + p
                    sp.wait_ge(x_turned, b + 1)
                    sp.wait_ge(xb_ready, b + 1)
                    load(b + 2, p)

        @block.gpsimd
        def _(pool):
            nc.gpsimd.memset(negmax[:, :, :, :, :], 0.0).then_inc(slots_set, 1)
            nc.gpsimd.memset(turn_mark[:, :], 1.0).then_inc(slots_set, 1)
            nc.gpsimd.memset(qs[:, :, :, MROW:CH], 0.0).then_inc(slots_set, 1)
            nc.gpsimd.memset(ks[:, :, :, MROW + 1:CH], 0.0).then_inc(slots_set, 1)
            nc.gpsimd.memset(ks[:, :, :, MROW:MROW + 1], 1.0).then_inc(slots_set, 1)
            nc.gpsimd.memset(v[:, :, :, :, F + 1:32], 0.0).then_inc(slots_set, 1)
            nc.gpsimd.memset(v[:, :, :, :, F:F + 1], 1.0).then_inc(slots_set, 1)
            nc.gpsimd.memset(mask[:, :, :], 0.0).then_inc(set_step, 1)
            nc.gpsimd.memset(identb[:, :], 0.0).then_inc(set_step, 1)
            nc.gpsimd.memset(identh[:, :], 0.0).then_inc(set_step, 1)
            pool.wait_ge(set_step, 3)
            nc.gpsimd.affine_select(out=mask[:, :, :], in_=mask[:, :, :], compare_op=ALU.is_ge, fill=-1e30,
                                    base=0, pattern=[[0, 2], [-1, P]], channel_multiplier=1).then_inc(slots_set, 1)
            for m in (identb, identh):
                nc.gpsimd.affine_select(out=m[:, :], in_=m[:, :], compare_op=ALU.not_equal, fill=1.0,
                                        base=0, pattern=[[-1, P]], channel_multiplier=1).then_inc(slots_set, 1)

            def carry_wait(j):
                nc.gpsimd.tensor_tensor(turn_mark[:, j:j + 1], turn_mark[:, 5:6], turn_mark[:, 5:6], ALU.mult)

            def mask_probs(n, g):
                pool.wait_ge(st_free, 2 + n * HH + HH)
                carry_wait(g)
                diag = probs[:, g % 2, :, 0:2 * P]
                nc.gpsimd.affine_select(out=diag, in_=diag, compare_op=ALU.is_ge, fill=0.0, base=0,
                                        pattern=[[0, HH], [0, 2], [1, P]], channel_multiplier=-1)\
                    .then_inc(masked, 1)

            def take_v(b, p):
                pool.wait_ge(hi_ready, 2 * b + 2)
                if not (isinstance(b, int) and b < 2):
                    pool.wait_ge(pv_ready, (b - 1) * G)
                carry_wait(G)
                nc.gpsimd.tensor_copy(v[:, p, :, :, 0:F], v_next[:, :, :].rearrange("p t (h f) -> p t h f", f=F))\
                    .then_inc(v_ready, 1)

            def power(b):
                pool.wait_ge(var_ready, b + 1)
                nc.gpsimd.tensor_tensor(rstd[:, :], mv[:, :, 1], mhalf[:, 0:TT], ALU.pow).then_inc(rstd_ready, 1)

            def finish(b, p):
                pool.wait_ge(z_ready, b + 1)
                nc.gpsimd.tensor_tensor(zg[:, :, :], z[:, :, :],
                                        lnrow[:, 0, :].unsqueeze(1).broadcast_to([P, TT, D]), ALU.mult)\
                    .then_inc(zg_ready, 1)
                pool.wait_ge(zg_ready, b + 1)
                pool.wait_ge(xb_ready, b + 1)
                nc.gpsimd.tensor_tensor(y_all[:, ds(b * TT, TT), :], zg[:, :, :], xb[:, p, :, :], ALU.add)\
                    .then_inc(y_ready, 1)

            def batch(b, p, first, next1, next2):
                for g in range(G):
                    mask_probs(b * G + g, g)
                    if g == 1 and next1:
                        take_v(b + 1, 1 - p)
                    if g == 2 and not first:
                        power(b - 1)
                    if g == 3 and not first:
                        finish(b - 1, 1 - p)
                    if g == 0:
                        if not (isinstance(b, int) and b < 2):
                            pool.wait_ge(y_ready, b - 1)
                        pool.wait_ge(x_in_ready[p], (b - p) * 8 + 16)
                        nc.gpsimd.tensor_tensor(xb[:, p, :, :], x_in[:, p, :, :],
                                                lnrow[:, 1, :].unsqueeze(1).broadcast_to([P, TT, D]), ALU.add)\
                            .then_inc(xb_ready, 1)

            take_v(0, 0)
            each_batch(pool, batch)
            power(B - 1)
            finish(B - 1, 1)

        @block.tensor
        def _(pe):
            pe.wait_ge(consts_ready, CONSTS)
            pe.wait_ge(w["B_split"], 1)
            pe.wait_ge(slots_set, 10)

            def turn_x(b, p):
                pe.wait_ge(x_in_ready[p], (b - p) * 8 + 16)
                for t in range(TT):
                    last = nc.tensor.transpose(ps_side[:, t * P:(t + 1) * P], x_in[:, p, t, :], ident[:, :])
                last.then_inc(x_turned, 1)

            def qkv(b, t):
                if t == 0:
                    pe.wait_ge(xTl_ready, b + 1)
                else:
                    pe.wait_ge(lo_ready, 2 * b + t)
                a, s = ps_side[:, 0:SC], slice(t * P, (t + 1) * P)
                nc.tensor.matmul(a, xTh[:, s], w["B_wh"][:, :], start=True, stop=False)
                nc.tensor.matmul(a, xTh[:, s], w["B_wl"][:, :], start=False, stop=False)
                nc.tensor.matmul(a, xTl[:, s], w["B_wh"][:, :], start=False, stop=True).then_inc(qkv_made, 1)

            def turn_stack(b, slot, stack):
                if stack is qs:
                    pe.wait_ge(lo_ready, 2 * b + 2)
                else:
                    pe.wait_ge(qsT_ready, b + 1)
                for g in range(G):
                    for t in range(TT):
                        last = nc.tensor.transpose(side_h[:, g * N + t * P:g * N + (t + 1) * P],
                                                   stack[:, t, g * HH:(g + 1) * HH, :].rearrange("p h c -> p (h c)"),
                                                   identh[:, :])
                last.then_inc(stacks_turned, 1)

            def turn_back(b, t):
                if t == 0:
                    pe.wait_ge(oT_ready, 2 * b + 2)
                    if not (isinstance(b, int) and b == 0):
                        pe.wait_ge(back_read, 2 * b)
                else:
                    pe.wait_ge(back_read, 2 * b + t)
                for g in range(G):
                    last = nc.tensor.transpose(ps_side[:, g * P:(g + 1) * P], oT[:, g, t * P:(t + 1) * P], ident[:, :])
                last.then_inc(back_ready, 1)

            def scores(b, p, g):
                n = b * G + g
                if g == 0:
                    pe.wait_ge(qsT_ready, b + 1)
                    pe.wait_ge(ksT_ready, b + 1)
                if not (isinstance(n, int) and n == 0):
                    pe.wait_ge(max_ready, n)
                for hh in range(HH):
                    nc.tensor.matmul(ps_sc[:, hh, 0:SC].rearrange("p (j s) -> p j s", s=P)[:, 0:3:2, :], identb[:, :],
                                     mask[:, :, :], start=True, stop=True, skip_group_check=True)
                for t, (c0, c1) in enumerate(((0, P), (P, SC))):
                    for hh in range(HH):
                        r0 = CH * hh
                        last = nc.tensor.matmul(ps_sc[:, hh, c0:c1], qsT[r0:r0 + CH, p, g, t * P:(t + 1) * P],
                                                ksT[r0:r0 + CH, p, g, 0:c1 - c0], start=False, stop=True,
                                                skip_group_check=True)
                last.then_inc(scores_ready, 1)

            def maxima(n, g):
                pe.wait_ge(max_ready, n + 1)
                pe.wait_ge(st_free, n * HH + 1)
                for t in range(TT):
                    last = nc.tensor.transpose(ps_mx[:, t * P:(t + 1) * P],
                                               negmax[:, g % 2, t, :, :].rearrange("p h f -> p (h f)"), identh[:, :])
                last.then_inc(max_turned, 1)

            def scores_t(n, p, g, heads):
                pe.wait_ge(qmT_ready, n + 1)
                for hh in heads:
                    r0, bank = CH * hh, ps_st[hh % 2]
                    pe.wait_ge(st_free, n * HH + hh + 1)
                    nc.tensor.matmul(bank[:, 0:SC].rearrange("p (j t) -> p j t", t=P)[:, 0:3:2, :],
                                     ksT[r0:r0 + CH, p, g, 0:P], qmT[r0:r0 + CH, g % 2, :], start=True, stop=True)
                    nc.tensor.matmul(bank[:, P:N], ksT[r0:r0 + CH, p, g, P:N], qmT[r0:r0 + CH, g % 2, P:N],
                                     start=True, stop=True).then_inc(st_ready, 1)

            def attend_s0(b, p, g):
                n = b * G + g
                pe.wait_ge(masked, n + 1)
                if g == 0:
                    pe.wait_ge(v_ready, b + 1)
                if g % 2 == 0 and not zero(n):
                    pe.wait_ge(oT_ready, b * (G // 2) + g // 2)
                for hh in range(HH):
                    pr, h = probs[:, g % 2, hh, :], g * HH + hh
                    nc.tensor.matmul(ps_pv[32 * hh:32 * hh + 32, g % 2, :].rearrange("p (j t) -> p j t", t=P),
                                     v[:, p, 0, h, :], pr.rearrange("p (j t) -> p j t", t=P)[:, 0:3:2, :],
                                     start=True, stop=True, skip_group_check=True)

            def attend_s1(b, p, g):
                for hh in range(HH):
                    pr, h = probs[:, g % 2, hh, :], g * HH + hh
                    last = nc.tensor.matmul(ps_pv[32 * hh:32 * hh + 32, g % 2, P:N], v[:, p, 1, h, :], pr[:, P:N],
                                            start=False, stop=True, skip_group_check=True)
                last.then_inc(pv_ready, 1)

            def batch(b, p, first, next1, next2):
                for g in range(G):
                    n = b * G + g
                    maxima(n, g)
                    if g + 1 < G:
                        scores(b, p, g + 1)
                    elif next1:
                        scores(b + 1, 1 - p, 0)
                    if g == 0 and next1:
                        qkv(b + 1, 1)
                    if g == 1 and next1:
                        turn_stack(b + 1, 1 - p, qs)
                    if g == 2 and not first:
                        if next1:
                            pe.wait_ge(ksT_ready, b + 2)
                        turn_back(b - 1, 0)
                    if g == 3 and next2:
                        if not first:
                            pe.wait_ge(back_read, 2 * b)
                        else:
                            pe.wait_ge(ksT_ready, b + 2)
                        turn_x(b + 2, p)
                    scores_t(n, p, g, (0, 1))
                    before = (b, p, g - 1) if g > 0 else (b - 1, 1 - p, G - 1)
                    if g > 0 or not first:
                        attend_s0(*before)
                    scores_t(n, p, g, (2, 3))
                    if g > 0 or not first:
                        attend_s1(*before)
                    if g == 1 and next1:
                        turn_stack(b + 1, 1 - p, ks)
                    if g == 2 and not first:
                        turn_back(b - 1, 1)
                    if g == 3 and next2:
                        qkv(b + 2, 0)

            turn_x(0, 0)
            qkv(0, 0)
            qkv(0, 1)
            turn_stack(0, 0, qs)
            turn_stack(0, 0, ks)
            scores(0, 0, 0)
            turn_x(1, 1)
            qkv(1, 0)
            each_batch(pe, batch)
            attend_s0(B - 1, 1, G - 1)
            attend_s1(B - 1, 1, G - 1)
            turn_back(B - 1, 0)
            turn_back(B - 1, 1)

        @block.scalar
        def _(act):
            act.wait_ge(slots_set, 10)
            act.sem_inc(st_free, 2)

            def x_hi(b):
                act.wait_ge(x_turned, b + 1)
                nc.scalar.copy(xTh[:, :], ps_side[:, 0:N]).then_inc(xTh_ready, 1)

            def qkv_hi(b, p, t):
                act.wait_ge(qkv_made, 2 * b + t + 1)
                src = ps_side[:, 0:SC].rearrange("p (j h f) -> p j h f", j=3, f=F)
                pair = [P, G * HH, 2, F]
                nc.scalar.mul(qs[:, t, :, 0:2 * F].rearrange("p h (j f) -> p h j f", f=F),
                              src[:, 0, :, :].unsqueeze(2).broadcast_to(pair), 1.0 / 512)
                nc.scalar.mul(ks[:, t, :, 0:CH].rearrange("p h (j f) -> p h j f", f=F)[:, :, 0:3:2, :],
                              src[:, 1, :, :].unsqueeze(2).broadcast_to(pair), 1.0 / 64)
                if t == 0 and not (isinstance(b, int) and b == 0):
                    act.wait_ge(v_ready, b)
                nc.scalar.mul(v_next[:, t, :].rearrange("p (h f) -> p h f", f=F), src[:, 2, :, :], 1.0 / 64)\
                    .then_inc(hi_ready, 1)

            def q_rows(b, p):
                act.wait_ge(stacks_turned, 2 * b + 1)
                nc.scalar.copy(qsT[:, p, :, :].rearrange("p g n -> p (g n)"), side_h).then_inc(qsT_ready, 1)

            def exps(n, g):
                if not (isinstance(n, int) and n < 2):
                    act.wait_ge(pv_ready, n - 1)
                for hh in range(HH):
                    act.wait_ge(st_ready, n * HH + hh + 1)
                    nc.scalar.activation(probs[:, g % 2, hh, :], ps_st[hh % 2][:, 0:SC], ACT.Exp, scale=EXP_SCALE)\
                        .then_inc(st_free, 1)

            def take_pv(b, j):
                act.wait_ge(pv_ready, b * G + 2 * j + 2)
                nc.scalar.copy(oT[:, 2 * j:2 * j + 2, :].rearrange("p g n -> p (g n)"),
                               ps_pv[:, :, :].rearrange("p g n -> p (g n)")).then_inc(oT_ready, 1)

            def batch(b, p, first, next1, next2):
                for g in range(G):
                    if g == 0 and next1:
                        qkv_hi(b + 1, 1 - p, 1)
                    if g == 1 and next1:
                        q_rows(b + 1, 1 - p)
                    if g == 3 and next2:
                        x_hi(b + 2)
                    exps(b * G + g, g)
                    if g == 0 and not first:
                        take_pv(b - 1, 1)
                    if g == 2:
                        if not first:
                            act.wait_ge(back_ready, 2 * b)
                        take_pv(b, 0)
                    if g == 3 and next2:
                        qkv_hi(b + 2, p, 0)

            x_hi(0)
            qkv_hi(0, 0, 0)
            qkv_hi(0, 0, 1)
            q_rows(0, 0)
            x_hi(1)
            qkv_hi(1, 1, 0)
            each_batch(act, batch)
            take_pv(B - 1, 1)

        @block.vector
        def _(dve):
            dve.wait_ge(slots_set, 10)

            def x_lo(b):
                dve.wait_ge(xTh_ready, b + 1)
                nc.vector.tensor_tensor(xTl[:, :], ps_side[:, 0:N], xTh[:, :], ALU.subtract).then_inc(xTl_ready, 1)

            def qkv_lo(b, t):
                dve.wait_ge(hi_ready, 2 * b + t + 1)
                src = ps_side[:, 0:SC].rearrange("p (j h f) -> p j h f", j=3, f=F)
                nc.vector.scalar_tensor_tensor(qs[:, t, :, 2 * F:3 * F], src[:, 0, :, :], 1.0 / 512, qs[:, t, :, 0:F],
                                               ALU.mult, ALU.subtract)
                nc.vector.scalar_tensor_tensor(ks[:, t, :, F:2 * F], src[:, 1, :, :], 1.0 / 64, ks[:, t, :, 0:F],
                                               ALU.mult, ALU.subtract).then_inc(lo_ready, 1)

            def k_rows(b, p):
                dve.wait_ge(stacks_turned, 2 * b + 2)
                nc.vector.tensor_copy(ksT[:, p, :, :].rearrange("p g n -> p (g n)"), side_h).then_inc(ksT_ready, 1)

            def row_max(n, g):
                dve.wait_ge(scores_ready, n + 1)
                for t, (c0, c1) in enumerate(((0, P), (P, SC))):
                    last = nc.vector.tensor_reduce(negmax[:, g % 2, t, :, MROW:MROW + 1], ps_sc[:, :, c0:c1],
                                                   AX_X, ALU.max, negate=True)
                last.then_inc(max_ready, 1)

            def add_max(n, p, g):
                if not (isinstance(n, int) and n < 2):
                    dve.wait_ge(st_ready, (n - 1) * HH)
                dve.wait_ge(max_turned, n + 1)
                nc.vector.tensor_tensor(qmT[:, g % 2, :], ps_mx, qsT[:, p, g, :], ALU.add).then_inc(qmT_ready, 1)

            def divide(b, t):
                dve.wait_ge(back_ready, 2 * b + t + 1)
                src = ps_side[:, :].rearrange("p (h f) -> p h f", f=32)
                nc.vector.reciprocal(rsum[:, t, :], src[:, :, F]).then_inc(dve_step, 1)
                dve.wait_ge(dve_step, b * 3 + t + 1)
                nc.vector.tensor_tensor(attn[:, t, :].rearrange("p (h f) -> p h f", f=F), src[:, :, 0:F],
                                        rsum[:, t, :].unsqueeze(2).broadcast_to([P, G * HH, F]), ALU.mult)\
                    .then_inc(back_read, 1)

            def variance(b):
                dve.wait_ge(back_read, 2 * b + 2)
                for t in range(TT):
                    nc.vector.bn_stats(stats[:, t, :], attn[:, t, :])
                dve.drain()
                for t in range(TT):
                    last = nc.vector.bn_aggr(mv[:, t, :], stats[:, t, :])
                last.then_inc(dve_step, 1)
                dve.wait_ge(dve_step, b * 3 + 3)
                nc.vector.tensor_scalar(mv[:, :, 1], mv[:, :, 1], LN_EPS, None, ALU.add).then_inc(var_ready, 1)

            def normalise(b):
                if not (isinstance(b, int) and b == 0):
                    dve.wait_ge(y_ready, b)
                dve.wait_ge(rstd_ready, b + 1)
                for t in range(TT):
                    last = nc.vector.tensor_scalar(z[:, t, :], attn[:, t, :], mv[:, t, 0:1], rstd[:, t:t + 1],
                                                   ALU.subtract, ALU.mult)
                last.then_inc(z_ready, 1)

            def batch(b, p, first, next1, next2):
                for g in range(G):
                    n = b * G + g
                    add_max(n, p, g)
                    if g + 1 < G or next1:
                        row_max(n + 1, (g + 1) % G)
                    if g == 0 and next1:
                        qkv_lo(b + 1, 1)
                    if g == 3 and next2:
                        x_lo(b + 2)
                    if g == 1 and next1:
                        k_rows(b + 1, 1 - p)
                    if g == 2 and not first:
                        divide(b - 1, 0)
                        divide(b - 1, 1)
                        variance(b - 1)
                    if g == 3:
                        if next2:
                            qkv_lo(b + 2, 0)
                        if not first:
                            normalise(b - 1)

            x_lo(0)
            qkv_lo(0, 0)
            qkv_lo(0, 1)
            k_rows(0, 0)
            row_max(0, 0)
            x_lo(1)
            qkv_lo(1, 0)
            each_batch(dve, batch)
            divide(B - 1, 0)
            divide(B - 1, 1)
            variance(B - 1)
            normalise(B - 1)


def stage_b_experts(nc, c, x_all, y_all, w, ident, consts_ready, mhalf, lnrow):
    E, FF = 8, 4 * D
    TM = BANK // P
    TURNS = TILES // TM
    C = FF // P
    UNITS = E * C
    HF = 4
    SCALE = 1 / W_SCALE

    y_in = c.sb("m_y_in", [P, 2, TM, D])
    xy = c.sb("m_xy", [P, TM, D])
    yT = c.sb("m_yT", [P, BANK])
    yTh = c.sb("m_yTh", [P, 2, BANK], F16)
    yTl = c.sb("m_yTl", [P, 2, BANK], F16)
    lg = c.sb("m_lg", [P, TM, E])
    mx = c.sb("m_mx", [P, TM, 8])
    ix = c.sb("m_ix", [P, TM, 8], U32)
    ixf = c.sb("m_ixf", [P, TM, 2])
    gap = c.sb("m_gap", [P, TM])
    eg = c.sb("m_eg", [P, TM])
    wsum = c.sb("m_wsum", [P, TM])
    wt = c.sb("m_wt", [P, 2, TM])
    pick = c.sb("m_pick", [P, 2, TM, E])
    comb = c.sb("m_comb", [P, 2, TM, E])
    combT = c.sb("m_combT", [E, BANK])
    experts = c.sb("m_experts", [P, E])
    hf = c.sb("m_hf", [P, HF, BANK])
    hh = c.sb("m_hh", [P, 2, C, BANK], F16)
    hl = c.sb("m_hl", [P, 2, C, BANK], F16)
    acc = c.sb("m_acc", [P, 2, TM, D])
    z = c.sb("m_z", [P, TM, D])
    zg = c.sb("m_zg", [P, TM, D])
    rows = c.sb("m_rows", [P, TM, D])
    stats = c.sb("m_stats", [P, TM, 6])
    mv = c.sb("m_mv", [P, TM, 2])
    rstd = c.sb("m_rstd", [P, TM])
    ps_h = [c.ps(f"m_ps_h{j}", [P, BANK]) for j in range(4)]
    ps_eo = [c.ps(f"m_ps_eo{j}", [P, BANK]) for j in range(2)]
    ps_turn = c.ps("m_ps_turn", [P, BANK])
    ps_row = c.ps("m_ps_row", [P, BANK])

    y_in_ready = [c.sem(f"m_y_in_ready{j}") for j in range(2)]
    iota_ready = c.sem("m_iota_ready")
    y_turned = c.sem("m_y_turned")
    yT_ready = c.sem("m_yT_ready")
    yTl_ready = c.sem("m_yTl_ready")
    logits_made = c.sem("m_logits_made")
    logits_read = c.sem("m_logits_read")
    gap_ready = c.sem("m_gap_ready")
    eg_ready = c.sem("m_eg_ready")
    comb_ready = c.sem("m_comb_ready")
    comb_turned = c.sem("m_comb_turned")
    combT_ready = c.sem("m_combT_ready")
    b2_made = c.sem("m_b2_made")
    acc_ready = c.sem("m_acc_ready")
    h_made = c.sem("m_h_made")
    h_free = c.sem("m_h_free")
    hh_ready = c.sem("m_hh_ready")
    hl_ready = c.sem("m_hl_ready")
    eo_ready = c.sem("m_eo_ready")
    eo_free = c.sem("m_eo_free")
    route_step = c.sem("m_route_step")
    mv_ready = c.sem("m_mv_ready")
    var_ready = c.sem("m_var_ready")
    rstd_ready = c.sem("m_rstd_ready")
    z_ready = c.sem("m_z_ready")
    zg_ready = c.sem("m_zg_ready")
    sum_step = c.sem("m_sum_step")
    xy_ready = c.sem("m_xy_ready")
    rows_ready = c.sem("m_rows_ready")
    rows_done = c.sem("m_rows_done")

    def each_turn(eng, body):
        body(0, 0, True, True)
        with eng.Fori(0, (TURNS - 2) // 2) as k:
            body(2 * k + 1, 1, False, True)
            body(2 * k + 2, 0, False, True)
        body(TURNS - 1, 1, False, False)

    def ahead(i, p, e):
        return (i, p, e + 2) if e + 2 < E else (i + 1, 1 - p, e + 2 - E)

    with nc.Block() as block:

        @block.sync
        def _(sp):
            def load(i, p):
                sp.dma_start(y_in[:, p, :, :], y_all[:, ds(i * TM, TM), :]).then_inc(y_in_ready[p], 16)

            load(0, 0)
            load(1, 1)
            with sp.Fori(0, TURNS // 2 - 1) as k:
                for p in range(2):
                    i = 2 * k + p
                    sp.wait_ge(y_turned, i + 1)
                    sp.wait_ge(xy_ready, i + 1)
                    load(i + 2, p)

        @block.gpsimd
        def _(pool):
            nc.gpsimd.iota(experts[:, :], pattern=[[1, E]], base=0, channel_multiplier=0,
                           allow_small_or_imprecise_dtypes=True).then_inc(iota_ready, 1)

            def lower(i, p, e):
                for j in range(C):
                    n = e * C + j
                    pool.wait_ge(hh_ready, i * UNITS + n + 1)
                    nc.gpsimd.tensor_tensor(hl[:, e % 2, j, :], hf[:, n % HF, :], hh[:, e % 2, j, :], ALU.subtract)\
                        .then_inc(hl_ready, 1)

            def power(i, ln):
                pool.wait_ge(var_ready, 2 * i + ln + 1)
                nc.gpsimd.tensor_tensor(rstd[:, :], mv[:, :, 1], mhalf[:, 0:TM], ALU.pow).then_inc(rstd_ready, 1)

            def add_up(i):
                pool.wait_ge(z_ready, i + 1)
                nc.gpsimd.tensor_tensor(zg[:, :, :], z[:, :, :],
                                        lnrow[:, 2, :].unsqueeze(1).broadcast_to([P, TM, D]), ALU.mult)\
                    .then_inc(zg_ready, 1)
                pool.wait_ge(zg_ready, i + 1)
                nc.gpsimd.tensor_tensor(rows[:, :, :], zg[:, :, :], xy[:, :, :], ALU.add).then_inc(rows_ready, 1)

            def residual(i, p):
                if not zero(i):
                    pool.wait_ge(rows_ready, i)
                pool.wait_ge(y_in_ready[p], (i - p) * 8 + 16)
                nc.gpsimd.tensor_tensor(xy[:, :, :], x_all[:, ds(i * TM, TM), :], y_in[:, p, :, :], ALU.add)\
                    .then_inc(sum_step, 1)
                pool.wait_ge(sum_step, i + 1)
                nc.gpsimd.tensor_tensor(xy[:, :, :], xy[:, :, :],
                                        lnrow[:, 3, :].unsqueeze(1).broadcast_to([P, TM, D]), ALU.add)\
                    .then_inc(xy_ready, 1)
                pool.wait_ge(xy_ready, i + 1)

            def turn(i, p, first, more):
                for e in range(E):
                    if e + 2 < E or more:
                        lower(*ahead(i, p, e))
                    if e == 0 and not first:
                        power(i - 1, 0)
                    if e == 1 and not first:
                        add_up(i - 1)
                    if e == 2 and not first:
                        power(i - 1, 1)
                    if e == 3:
                        residual(i, p)

            lower(0, 0, 0)
            lower(0, 0, 1)
            each_turn(pool, turn)
            power(TURNS - 1, 0)
            add_up(TURNS - 1)
            power(TURNS - 1, 1)

        @block.tensor
        def _(pe):
            pe.wait_ge(w["B_ready"], W_B)
            pe.wait_ge(w["split"], PIECES)
            pe.wait_ge(consts_ready, CONSTS)

            def turn_y(i, p):
                pe.wait_ge(y_in_ready[p], (i - p) * 8 + 16)
                if not zero(i):
                    pe.wait_ge(combT_ready, i)
                for t in range(TM):
                    last = nc.tensor.transpose(ps_turn[:, t * P:(t + 1) * P], y_in[:, p, t, :], ident[:, :])
                last.then_inc(y_turned, 1)

            def logits(i):
                pe.wait_ge(yT_ready, 2 * i + 1)
                if not zero(i):
                    pe.wait_ge(acc_ready, i)
                for t in range(TM):
                    last = nc.tensor.matmul(ps_row[:, t * E:(t + 1) * E], yT[:, t * P:(t + 1) * P],
                                            w["B_gate"][:, :], start=True, stop=True)
                last.then_inc(logits_made, 1)

            def turn_comb(i, p):
                pe.wait_ge(comb_ready, i + 1)
                pe.wait_ge(yTl_ready, i + 1)
                for t in range(TM):
                    last = nc.tensor.transpose(ps_turn[0:E, t * P:(t + 1) * P], comb[:, p, t, :], ident[:, :])
                last.then_inc(comb_turned, 1)

            def b2_part(i):
                pe.wait_ge(combT_ready, i + 1)
                pe.wait_ge(logits_read, i + 1)
                for t in range(TM):
                    last = nc.tensor.matmul(ps_row[:, t * P:(t + 1) * P], combT[:, t * P:(t + 1) * P],
                                            w["B_b2"][:, :], start=True, stop=True)
                last.then_inc(b2_made, 1)

            def hidden(i, p, e):
                if e == 0:
                    pe.wait_ge(yTl_ready, i + 1)
                for j in range(C):
                    n = e * C + j
                    wh = w["B_W1h"][:, n * P:(n + 1) * P]
                    pe.wait_ge(h_free, i * UNITS + n + 1)
                    nc.tensor.matmul(ps_h[n % 4][:, :], wh, yTh[:, p, :], start=True, stop=False)
                    nc.tensor.matmul(ps_h[n % 4][:, :], wh, yTl[:, p, :], start=False, stop=False)
                    nc.tensor.matmul(ps_h[n % 4][:, :], w["B_W1l"][:, n * P:(n + 1) * P], yTh[:, p, :],
                                     start=False, stop=True).then_inc(h_made, 1)

            def outputs(i, e):
                pe.wait_ge(eo_free, i * E + e + 1)
                pe.wait_ge(hl_ready, i * UNITS + (e + 1) * C)
                for t in range(TM):
                    out = ps_eo[e % 2][:, t * P:(t + 1) * P]
                    for j in range(C):
                        up, low = hh[:, e % 2, j, t * P:(t + 1) * P], hl[:, e % 2, j, t * P:(t + 1) * P]
                        cols = slice((e * C + j) * D, (e * C + j + 1) * D)
                        nc.tensor.matmul(out, up, w["B_W2h"][:, cols], start=(j == 0), stop=False)
                        nc.tensor.matmul(out, up, w["B_W2l"][:, cols], start=False, stop=False)
                        last = nc.tensor.matmul(out, low, w["B_W2h"][:, cols], start=False, stop=(j == C - 1))
                last.then_inc(eo_ready, 1)

            def turn(i, p, first, more):
                for e in range(E):
                    outputs(i, e)
                    if e == 7 and more:
                        turn_comb(i + 1, 1 - p)
                    if e + 2 < E or more:
                        hidden(*ahead(i, p, e))
                    if e == 2 and more:
                        turn_y(i + 1, 1 - p)
                    if e == 3 and more:
                        logits(i + 1)
                    if e == 7 and more:
                        b2_part(i + 1)

            turn_y(0, 0)
            logits(0)
            hidden(0, 0, 0)
            hidden(0, 0, 1)
            turn_comb(0, 0)
            b2_part(0)
            each_turn(pe, turn)

        @block.scalar
        def _(act):
            act.sem_inc(h_free, 4)
            act.wait_ge(w["B_ready"], W_B)
            act.wait_ge(consts_ready, CONSTS)
            nc.scalar.activation(hf[:, 0, 0:1], ident[:, 0:1], ACT.Exp)

            def take_y(i, p):
                act.wait_ge(y_turned, i + 1)
                if not zero(i):
                    act.wait_ge(logits_made, i)
                nc.scalar.copy(yT[:, :], ps_turn[:, :]).then_inc(yT_ready, 1)
                nc.scalar.copy(yTh[:, p, :], ps_turn[:, :]).then_inc(yT_ready, 1)

            def gap_exp(i):
                act.wait_ge(gap_ready, i + 1)
                nc.scalar.activation(eg[:, :], gap[:, :], ACT.Exp).then_inc(eg_ready, 1)

            def take_comb(i):
                act.wait_ge(comb_turned, i + 1)
                if not zero(i):
                    act.wait_ge(b2_made, i)
                nc.scalar.copy(combT[:, :], ps_turn[0:E, :]).then_inc(combT_ready, 1)

            def take_b2(i, p):
                act.wait_ge(b2_made, i + 1)
                if not (isinstance(i, int) and i < 2):
                    act.wait_ge(z_ready, i - 1)
                nc.scalar.mul(acc[:, p, :, :].rearrange("p t d -> p (t d)"), ps_row[:, :], 1 / SCALE)\
                    .then_inc(acc_ready, 1)

            def relu(i, p, e):
                for j in range(C):
                    n = e * C + j
                    act.wait_ge(h_made, i * UNITS + n + 1)
                    if not (zero(i) and n < HF):
                        act.wait_ge(hl_ready, i * UNITS + n + 1 - HF)
                    nc.scalar.activation(hf[:, n % HF, :], ps_h[n % 4][:, :], ACT.Relu,
                                         bias=w["B_b1"][:, n:n + 1], scale=SCALE).then_inc(h_free, 1)

            def turn(i, p, first, more):
                for e in range(E):
                    if e == 5 and more:
                        gap_exp(i + 1)
                    if e == 7 and more:
                        take_comb(i + 1)
                    if e + 2 < E or more:
                        relu(*ahead(i, p, e))
                    if e == 2 and more:
                        take_y(i + 1, 1 - p)
                    if e == 7 and more:
                        take_b2(i + 1, 1 - p)

            take_y(0, 0)
            gap_exp(0)
            relu(0, 0, 0)
            relu(0, 0, 1)
            take_comb(0)
            take_b2(0, 0)
            each_turn(act, turn)

        @block.vector
        def _(dve):
            dve.sem_inc(eo_free, 2)
            dve.wait_ge(iota_ready, 1)

            def y_lower(i, p):
                dve.wait_ge(yT_ready, 2 * i + 2)
                nc.vector.tensor_tensor(yTl[:, p, :], ps_turn[:, :], yTh[:, p, :], ALU.subtract)\
                    .then_inc(yTl_ready, 1)

            def top_two(i):
                dve.wait_ge(logits_made, i + 1)
                nc.vector.tensor_copy(lg[:, :, :].rearrange("p t e -> p (t e)"), ps_row[:, 0:TM * E])\
                    .then_inc(logits_read, 1)
                dve.drain()
                for t in range(TM):
                    nc.vector.max(mx[:, t, :], lg[:, t, :])
                dve.drain()
                for t in range(TM):
                    nc.vector.max_index(ix[:, t, :], mx[:, t, :], lg[:, t, :])
                nc.vector.tensor_tensor(gap[:, :], mx[:, :, 1], mx[:, :, 0], ALU.subtract).then_inc(gap_ready, 1)
                dve.drain()
                nc.vector.tensor_copy(ixf[:, :, :], ix[:, :, 0:2])

            def combine(i, p):
                dve.wait_ge(eg_ready, i + 1)
                nc.vector.tensor_scalar(wsum[:, :], eg[:, :], 1.0, 1 / SCALE, ALU.add, ALU.mult).then_inc(route_step, 1)
                dve.wait_ge(route_step, i * 4 + 1)
                nc.vector.reciprocal(wt[:, 0, :], wsum[:, :]).then_inc(route_step, 1)
                dve.wait_ge(route_step, i * 4 + 2)
                nc.vector.tensor_tensor(wt[:, 1, :], eg[:, :], wt[:, 0, :], ALU.mult).then_inc(route_step, 1)
                dve.wait_ge(route_step, i * 4 + 3)
                for s in range(2):
                    for t in range(TM):
                        last = nc.vector.tensor_scalar(pick[:, s, t, :], experts[:, :], ixf[:, t, s:s + 1],
                                                       wt[:, s, t:t + 1], ALU.is_equal, ALU.mult)
                last.then_inc(route_step, 1)
                dve.wait_ge(route_step, i * 4 + 4)
                nc.vector.tensor_tensor(comb[:, p, :, :], pick[:, 0, :, :], pick[:, 1, :, :], ALU.add)\
                    .then_inc(comb_ready, 1)

            def upper(i, p, e):
                for j in range(C):
                    n = e * C + j
                    dve.wait_ge(h_free, 4 + i * UNITS + n + 1)
                    nc.vector.tensor_copy(hh[:, e % 2, j, :], hf[:, n % HF, :]).then_inc(hh_ready, 1)

            def accumulate(i, p, e):
                if e == 0:
                    dve.wait_ge(acc_ready, i + 1)
                dve.wait_ge(eo_ready, i * E + e + 1)
                for t in range(TM):
                    last = nc.vector.scalar_tensor_tensor(acc[:, p, t, :], ps_eo[e % 2][:, t * P:(t + 1) * P],
                                                          comb[:, p, t, e:e + 1], acc[:, p, t, :],
                                                          ALU.mult, ALU.add)
                last.then_inc(eo_free, 1)
                dve.wait_ge(eo_free, 2 + i * E + e + 1)

            def variance(i, ln, src):
                row_variance(dve, nc, src, stats, mv, TM, mv_ready, 2 * i + ln + 1, var_ready)

            def normalise_mixture(i, p):
                dve.wait_ge(rstd_ready, 2 * i + 1)
                row_normalise(nc, acc[:, p, :, :], mv, rstd, TM, lambda t: z[:, t, :]).then_inc(z_ready, 1)

            def rows_variance(i):
                dve.wait_ge(rows_ready, i + 1)
                variance(i, 1, rows)

            def normalise_rows(i):
                dve.wait_ge(rstd_ready, 2 * i + 2)
                row_normalise(nc, rows, mv, rstd, TM,
                              lambda t: x_all[:, ds(i * TM + t, 1), :].squeeze(1)).then_inc(rows_done, 1)

            def turn(i, p, first, more):
                for e in range(E):
                    accumulate(i, p, e)
                    if e + 2 < E or more:
                        upper(*ahead(i, p, e))
                    if not first:
                        if e == 0:
                            variance(i - 1, 0, acc[:, 1 - p, :, :])
                        if e == 1:
                            normalise_mixture(i - 1, 1 - p)
                        if e == 2:
                            rows_variance(i - 1)
                        if e == 3:
                            normalise_rows(i - 1)
                    if more:
                        if e == 2:
                            y_lower(i + 1, 1 - p)
                        if e == 4:
                            top_two(i + 1)
                        if e == 5:
                            combine(i + 1, 1 - p)

            y_lower(0, 0)
            top_two(0)
            upper(0, 0, 0)
            combine(0, 0)
            upper(0, 0, 1)
            each_turn(dve, turn)
            variance(TURNS - 1, 0, acc[:, 1, :, :])
            normalise_mixture(TURNS - 1, 1)
            rows_variance(TURNS - 1)
            normalise_rows(TURNS - 1)
            dve.wait_ge(rows_done, TURNS)


def stage_c(nc, c, x_all, w, ident, consts_ready, mhalf):
    VB = DH + 1
    SC = 3 * P
    SCALE = 1 / W_SCALE
    HALF = HD // BANK
    QK = PAIRS
    V = TT * HALF
    PROJ = QK + 2 * V
    ACT_FREES = QK + V
    assert PROJ == 2 * PAIRS

    x_in = c.sb("c_x_in", [P, 2, TT, D])
    xTh = c.sb("c_xTh", [P, 2, N], F16)
    xTl = c.sb("c_xTl", [P, 2, N], F16)
    qT = c.sb("c_qT", [P, 2, PAIRS, N])
    kT = c.sb("c_kT", [P, 2, PAIRS, N])
    vh = c.sb("c_vh", [P, 2, TT, H, VB], F16)
    vl = c.sb("c_vl", [P, 2, TT, H, VB], F16)
    gate = c.sb("c_gate", [P, 2, TT, HD])
    ex = c.sb("c_exp", [P, 2, BANK])
    re = c.sb("c_relu", [P, 2, BANK])
    sc = c.sb("c_sc", [P, 2, 2, 2, SC], F16)
    turn_mark = c.sb("c_turn_mark", [P, PAIRS + 1])
    den = c.sb("c_den", [P, PAIRS, TT * 2])
    rden = c.sb("c_rden", [P, PAIRS, TT * 2])
    o = c.sb("c_o", [P, 2, TT, P])
    og = c.sb("c_og", [P, 2, TT, HD])
    oT = c.sb("c_oT", [P, TT, PAIRS, P])
    rows = c.sb("c_rows", [P, TT, D])
    stats = c.sb("c_stats", [P, TT, 6])
    mv = c.sb("c_mv", [P, TT, 2])
    rstd = c.sb("c_rstd", [P, TT])
    ps_proj = [c.ps(f"c_ps_proj{j}", [P, BANK]) for j in range(2)]
    ps_sc = [c.ps(f"c_ps_sc{j}", [P, BANK]) for j in range(2)]
    ps_att = [c.ps(f"c_ps_att{j}", [P, BANK]) for j in range(2)]
    ps_turn = c.ps("c_ps_turn", [P, BANK])
    ps_out = c.ps("c_ps_out", [P, TT, D])

    x_in_ready = [c.sem(f"c_x_in_ready{j}") for j in range(2)]
    x_turned = c.sem("c_x_turned")
    slots_set = c.sem("c_slots_set")
    xTh_ready = c.sem("c_xTh_ready")
    xTl_ready = c.sem("c_xTl_ready")
    proj_ready = c.sem("c_proj_ready")
    proj_free = c.sem("c_proj_free")
    feat_free = c.sem("c_feat_free")
    vh_ready = c.sem("c_vh_ready")
    vl_ready = c.sem("c_vl_ready")
    sc_ready = c.sem("c_sc_ready")
    sc_hi = c.sem("c_sc_hi")
    sc_lo = c.sem("c_sc_lo")
    sc_masked = c.sem("c_sc_masked")
    att_ready = c.sem("c_att_ready")
    att_free = c.sem("c_att_free")
    gated = c.sem("c_gated")
    o_turned = c.sem("c_o_turned")
    oT_ready = c.sem("c_oT_ready")
    out_ready = c.sem("c_out_ready")
    out_used = c.sem("c_out_used")
    den_step = c.sem("c_den_step")
    mv_ready = c.sem("c_mv_ready")
    rows_done = c.sem("c_rows_done")
    var_ready = c.sem("c_var_ready")
    rstd_ready = c.sem("c_rstd_ready")

    with nc.Block() as block:

        @block.sync
        def _(sp):
            def load(b, p):
                sp.dma_start(x_in[:, p, :, :], x_all[:, ds(b * TT, TT), :]).then_inc(x_in_ready[p], 16)

            load(0, 0)
            load(1, 1)
            with sp.Fori(0, B // 2 - 1) as i:
                for p in range(2):
                    b = 2 * i + p
                    sp.wait_ge(x_turned, b + 1)
                    load(b + 2, p)

        @block.gpsimd
        def _(pool):
            nc.gpsimd.memset(vh[:, :, :, :, DH:VB], 1.0).then_inc(slots_set, 1)
            nc.gpsimd.memset(vl[:, :, :, :, DH:VB], 0.0).then_inc(slots_set, 1)
            nc.gpsimd.memset(turn_mark[:, :], 1.0).then_inc(slots_set, 1)
            pool.wait_ge(slots_set, 3)

            def batch(b, p, first, next1, next2):
                for m in range(PAIRS):
                    pool.wait_ge(sc_lo, 2 + b * H + 2 * m + 2)
                    nc.gpsimd.tensor_tensor(turn_mark[:, m:m + 1], turn_mark[:, PAIRS:PAIRS + 1],
                                            turn_mark[:, PAIRS:PAIRS + 1], ALU.mult)
                    diag = sc[:, m % 2, :, :, :].rearrange("p l h t -> p (l h) t")[:, :, 0:2 * P]
                    nc.gpsimd.affine_select(out=diag, in_=diag, compare_op=ALU.is_ge, fill=0.0, base=0,
                                            pattern=[[0, 4], [0, 2], [1, P]], channel_multiplier=-1)\
                        .then_inc(sc_masked, 1)
                    if m == 7 and not first:
                        power(b - 1)

            def power(b):
                pool.wait_ge(var_ready, b + 1)
                nc.gpsimd.tensor_tensor(rstd[:, :], mv[:, :, 1], mhalf[:, 0:TT], ALU.pow).then_inc(rstd_ready, 1)

            each_batch(pool, batch)
            power(B - 1)

        @block.tensor
        def _(pe):
            pe.wait_ge(consts_ready, CONSTS)
            pe.wait_ge(w["split"], PIECES)
            pe.wait_ge(w["C_ready"], W_C)
            pe.wait_ge(slots_set, 3)

            def turn_x(b, p):
                pe.wait_ge(x_in_ready[p], (b - p) * 8 + 16)
                for t in range(TT):
                    last = nc.tensor.transpose(ps_turn[:, t * P:(t + 1) * P], x_in[:, p, t, :], ident[:, :])
                last.then_inc(x_turned, 1)

            def halves(out, lhs_h, lhs_l, rhs_h, rhs_l):
                nc.tensor.matmul(out, lhs_h, rhs_h, start=True, stop=False)
                nc.tensor.matmul(out, lhs_h, rhs_l, start=False, stop=False)
                return nc.tensor.matmul(out, lhs_l, rhs_h, start=False, stop=True)

            def bank_used(b, u):
                if u < 2:
                    if not zero(b):
                        pe.wait_ge(proj_free, (b - 1) * ACT_FREES + ACT_FREES - 1 + u)
                elif u - 2 < QK:
                    pe.wait_ge(proj_free, b * ACT_FREES + u - 1)
                elif u - 2 < QK + V:
                    pe.wait_ge(vl_ready, b * V + u - 2 - QK + 1)
                else:
                    pe.wait_ge(proj_free, b * ACT_FREES + u - 2 - V + 1)

            def project(b, p, u):
                if u == 0:
                    pe.wait_ge(xTl_ready, b + 1)
                bank_used(b, u)
                bank = ps_proj[u % 2]
                if u < QK:
                    for s in range(2):
                        c0 = (u % 2) * HD + (2 * (u // 2) + s) * P
                        last = halves(bank[:, s * N:(s + 1) * N], w["C_wh"][:, c0:c0 + P], w["C_wl"][:, c0:c0 + P],
                                      xTh[:, p, :], xTl[:, p, :])
                else:
                    t, h = divmod((u - QK) % V, HALF)
                    c0 = (2 + (u - QK) // V) * HD + h * BANK
                    s = slice(t * P, (t + 1) * P)
                    last = halves(bank[:, :], xTh[:, p, s], xTl[:, p, s], w["C_wh"][:, c0:c0 + BANK],
                                  w["C_wl"][:, c0:c0 + BANK])
                last.then_inc(proj_ready, 1)

            def scores(b, p, m):
                if m == 0:
                    pe.wait_ge(feat_free, 2 + b * QK + QK)
                for s in range(2):
                    pe.wait_ge(sc_lo, b * H + 2 * m + s + 1)
                for s in range(2):
                    r0 = DH * s
                    nc.tensor.matmul(ps_sc[s][:, 0:SC].rearrange("p (j t) -> p j t", t=P)[:, 0:3:2, :],
                                     kT[r0:r0 + DH, p, m, 0:P], qT[r0:r0 + DH, p, m, :], start=True, stop=True)
                    nc.tensor.matmul(ps_sc[s][:, P:N], kT[r0:r0 + DH, p, m, P:N], qT[r0:r0 + DH, p, m, P:N],
                                     start=True, stop=True).then_inc(sc_ready, 1)

            def attend(b, p, m):
                if m == 0:
                    pe.wait_ge(vl_ready, b * V + V)
                pe.wait_ge(sc_masked, b * PAIRS + m + 1)
                pe.wait_ge(att_free, b * PAIRS + m + 1)
                for s in range(2):
                    hd, a = 2 * m + s, sc[:, m % 2, :, s, :]
                    for t, blocks in enumerate((((0, 0),), ((0, 2), (1, 1)))):
                        out = ps_att[m % 2][:, (2 * t + s) * VB:(2 * t + s + 1) * VB]
                        terms = [(sb, j, ah, vv) for sb, j in blocks for ah, vv in ((0, vh), (0, vl), (1, vh))]
                        for n, (sb, j, ah, vv) in enumerate(terms):
                            last = nc.tensor.matmul(out, a[:, ah, j * P:(j + 1) * P], vv[:, p, sb, hd, :],
                                                    start=(n == 0), stop=(n == len(terms) - 1))
                last.then_inc(att_ready, 1)

            def turn_o(b, p, k):
                t, half = divmod(k, 2)
                if k == 0:
                    pe.wait_ge(gated, b * PAIRS + PAIRS)
                    pe.wait_ge(xTl_ready, min(b + 3, B) if isinstance(b, int) else b + 3)
                else:
                    pe.wait_ge(oT_ready, b * 4 + k)
                for j in range(4):
                    m = 4 * half + j
                    last = nc.tensor.transpose(ps_turn[:, j * P:(j + 1) * P], og[:, p, t, m * P:(m + 1) * P], ident[:, :])
                last.then_inc(o_turned, 1)

            def out_part(b, k):
                t, half = divmod(k, 2)
                pe.wait_ge(oT_ready, b * 4 + k + 1)
                if k == 0 and not zero(b):
                    pe.wait_ge(out_used, b)
                for j in range(4):
                    m = 4 * half + j
                    last = nc.tensor.matmul(ps_out[:, t, :], oT[:, t, m, :], w["C_out"][:, m, :],
                                            start=(m == 0), stop=(m == PAIRS - 1))
                if k == 3:
                    last.then_inc(out_ready, 1)

            def batch(b, p, first, next1, next2):
                for m in range(PAIRS):
                    if m + 1 < PAIRS:
                        scores(b, p, m + 1)
                    elif next1:
                        scores(b + 1, 1 - p, 0)
                    if next1:
                        project(b + 1, 1 - p, 2 * m)
                    if not first and 1 <= m < 5:
                        out_part(b - 1, m - 1)
                    attend(b, p, m)
                    if not first and m < 4:
                        turn_o(b - 1, 1 - p, m)
                    if next1:
                        project(b + 1, 1 - p, 2 * m + 1)
                    if m == 5 and next2:
                        if not first:
                            pe.wait_ge(oT_ready, 4 * b)
                        turn_x(b + 2, p)

            turn_x(0, 0)
            for u in range(PROJ):
                project(0, 0, u)
            turn_x(1, 1)
            scores(0, 0, 0)
            each_batch(pe, batch)
            for k in range(4):
                turn_o(B - 1, 1, k)
                out_part(B - 1, k)

        @block.scalar
        def _(act):
            act.wait_ge(slots_set, 3)

            def x_hi(b, p):
                act.wait_ge(x_turned, b + 1)
                if not (isinstance(b, int) and b < 2):
                    act.wait_ge(proj_ready, (b - 1) * PROJ)
                nc.scalar.copy(xTh[:, p, :], ps_turn[:, 0:N]).then_inc(xTh_ready, 1)

            def take(b, p, u):
                bank = ps_proj[u % 2]
                act.wait_ge(proj_ready, b * PROJ + u + 1)
                if u < QK:
                    act.wait_ge(feat_free, b * QK + u + 1)
                    nc.scalar.activation(ex[:, u % 2, :], bank[:, :], ACT.Exp, scale=SCALE)
                    nc.scalar.activation(re[:, u % 2, :], bank[:, :], ACT.Relu, scale=SCALE).then_inc(proj_free, 1)
                    return
                kind, r = divmod(u - QK, V)
                t, h = divmod(r, HALF)
                if kind == 0:
                    nc.scalar.mul(vh[:, p, t, 8 * h:8 * h + 8, 0:DH], bank[:, :].rearrange("p (m e) -> p m e", e=DH),
                                  SCALE).then_inc(vh_ready, 1)
                else:
                    if r == 0 and not (isinstance(b, int) and b < 2):
                        act.wait_ge(gated, (b - 1) * PAIRS)
                    nc.scalar.activation(gate[:, p, t, h * BANK:(h + 1) * BANK], bank[:, :], ACT.Tanh,
                                         scale=0.5 * SCALE).then_inc(proj_free, 1)

            def score_hi(b, h):
                if h % 2 == 0 and not (zero(b) and h < 4):
                    act.wait_ge(att_ready, b * PAIRS + h // 2 - 1)
                act.wait_ge(sc_ready, b * H + h + 1)
                nc.scalar.mul(sc[:, (h // 2) % 2, 0, h % 2, :], ps_sc[h % 2][:, 0:SC], SCALE).then_inc(sc_hi, 1)

            def take_o(b, k):
                t, half = divmod(k, 2)
                if k == 0 and not zero(b):
                    act.wait_ge(out_ready, b)
                act.wait_ge(o_turned, b * 4 + k + 1)
                nc.scalar.copy(oT[:, t, 4 * half:4 * half + 4, :],
                               ps_turn[:, :].rearrange("p (m q) -> p m q", q=P)).then_inc(oT_ready, 1)

            def batch(b, p, first, next1, next2):
                for m in range(PAIRS):
                    if m + 1 < PAIRS:
                        score_hi(b, 2 * m + 2)
                        score_hi(b, 2 * m + 3)
                    elif next1:
                        score_hi(b + 1, 0)
                        score_hi(b + 1, 1)
                    if next1:
                        take(b + 1, 1 - p, 2 * m)
                    if not first and m < 4:
                        take_o(b - 1, m)
                    if next1:
                        take(b + 1, 1 - p, 2 * m + 1)
                    if m == 5 and next2:
                        x_hi(b + 2, p)

            x_hi(0, 0)
            for u in range(PROJ):
                take(0, 0, u)
            x_hi(1, 1)
            score_hi(0, 0)
            score_hi(0, 1)
            each_batch(act, batch)
            for k in range(4):
                take_o(B - 1, k)

        @block.vector
        def _(dve):
            dve.sem_inc(feat_free, 2)
            dve.sem_inc(sc_lo, 2)
            dve.sem_inc(att_free, 2)
            dve.wait_ge(slots_set, 3)

            def x_lo(b, p):
                dve.wait_ge(xTh_ready, b + 1)
                nc.vector.tensor_tensor(xTl[:, p, :], ps_turn[:, 0:N], xTh[:, p, :], ALU.subtract).then_inc(xTl_ready, 1)

            def take(b, p, u):
                if u < QK:
                    out = (qT, kT)[u % 2][:, p, 2 * (u // 2):2 * (u // 2) + 2, :].rearrange("p m q -> p (m q)")
                    dve.wait_ge(proj_free, b * ACT_FREES + u + 1)
                    nc.vector.scalar_tensor_tensor(out, ex[:, u % 2, :], 1.0, re[:, u % 2, :], ALU.min, ALU.add)\
                        .then_inc(feat_free, 1)
                elif u < QK + V:
                    t, h = divmod(u - QK, HALF)
                    dve.wait_ge(vh_ready, b * V + u - QK + 1)
                    heads = slice(8 * h, 8 * h + 8)
                    nc.vector.scalar_tensor_tensor(vl[:, p, t, heads, 0:DH],
                                                   ps_proj[u % 2][:, :].rearrange("p (m e) -> p m e", e=DH), SCALE,
                                                   vh[:, p, t, heads, 0:DH], ALU.mult, ALU.subtract)\
                        .then_inc(vl_ready, 1)

            def score_lo(b, h):
                dve.wait_ge(sc_hi, b * H + h + 1)
                nc.vector.scalar_tensor_tensor(sc[:, (h // 2) % 2, 1, h % 2, :], ps_sc[h % 2][:, 0:SC], SCALE,
                                               sc[:, (h // 2) % 2, 0, h % 2, :], ALU.mult, ALU.subtract)\
                    .then_inc(sc_lo, 1)

            def divide(b, m):
                dve.wait_ge(att_ready, b * PAIRS + m + 1)
                src = ps_att[m % 2][:, 0:4 * VB].rearrange("p (g e) -> p g e", e=VB)
                nc.vector.tensor_scalar(den[:, m, :], src[:, :, DH], 1e-6 * SCALE, 2.0, ALU.add, ALU.mult)\
                    .then_inc(den_step, 1)
                dve.wait_ge(den_step, b * 2 * PAIRS + 2 * m + 1)
                nc.vector.reciprocal(rden[:, m, :], den[:, m, :]).then_inc(den_step, 1)
                dve.wait_ge(den_step, b * 2 * PAIRS + 2 * m + 2)
                nc.vector.tensor_tensor(
                    o[:, m % 2, :, :].rearrange("p t (s e) -> p t s e", s=2),
                    src[:, :, 0:DH].rearrange("p (t s) e -> p t s e", t=TT),
                    rden[:, m, :].rearrange("p (t s) -> p t s", t=TT).unsqueeze(3).broadcast_to([P, TT, 2, DH]),
                    ALU.mult).then_inc(att_free, 1)

            def apply_gate(b, p, m):
                if m == 0:
                    dve.wait_ge(proj_free, b * ACT_FREES + ACT_FREES)
                    if not (isinstance(b, int) and b < 2):
                        dve.wait_ge(o_turned, 4 * (b - 1))
                dve.wait_ge(att_free, 2 + b * PAIRS + m + 1)
                at = slice(m * P, (m + 1) * P)
                nc.vector.scalar_tensor_tensor(og[:, p, :, at], gate[:, p, :, at], 1.0, o[:, m % 2, :, :],
                                               ALU.add, ALU.mult).then_inc(gated, 1)

            def add_residual(b):
                if not zero(b):
                    dve.wait_ge(rows_done, b)
                dve.wait_ge(out_ready, b + 1)
                nc.vector.tensor_tensor(rows[:, :, :], ps_out[:, :, :], x_all[:, ds(b * TT, TT), :], ALU.add)\
                    .then_inc(out_used, 1)

            def variance(b):
                dve.wait_ge(out_used, b + 1)
                row_variance(dve, nc, rows, stats, mv, TT, mv_ready, b + 1, var_ready)

            def normalise(b):
                dve.wait_ge(rstd_ready, b + 1)
                row_normalise(nc, rows, mv, rstd, TT,
                              lambda t: x_all[:, ds(b * TT + t, 1), :].squeeze(1)).then_inc(rows_done, 1)

            def batch(b, p, first, next1, next2):
                for m in range(PAIRS):
                    if m + 1 < PAIRS:
                        score_lo(b, 2 * m + 2)
                        score_lo(b, 2 * m + 3)
                    elif next1:
                        score_lo(b + 1, 0)
                        score_lo(b + 1, 1)
                    if next1:
                        take(b + 1, 1 - p, 2 * m)
                    divide(b, m)
                    if next1:
                        take(b + 1, 1 - p, 2 * m + 1)
                    apply_gate(b, p, m)
                    if m == 5 and not first:
                        add_residual(b - 1)
                    if m == 5 and next2:
                        x_lo(b + 2, p)
                    if m == 6 and not first:
                        variance(b - 1)
                    if m == 7 and not first:
                        normalise(b - 1)

            x_lo(0, 0)
            for u in range(PROJ):
                take(0, 0, u)
            x_lo(1, 1)
            score_lo(0, 0)
            score_lo(0, 1)
            each_batch(dve, batch)
            add_residual(B - 1)
            variance(B - 1)
            normalise(B - 1)
            dve.wait_ge(rows_done, B)


def stage_d(nc, c, x_all, out, w, ident, ones_row, consts_ready, mhalf, stored):
    TM = BANK // P
    TURNS = TILES // TM
    C = 4
    MAGIC = 1.5 * 2.0 ** 23

    x_in = c.sb("d_x_in", [P, 2, TM, D])
    xTh = c.sb("d_xTh", [P, 2, BANK], F16)
    xTl = c.sb("d_xTl", [P, 2, BANK], F16)
    h = c.sb("d_h", [P, 2, C, BANK])
    rows = c.sb("d_rows", [P, TM, D])
    final = c.sb("d_final", [P, 2, TM, D])
    stats = c.sb("d_stats", [P, TM, 6])
    mv = c.sb("d_mv", [P, TM, 2])
    rstd = c.sb("d_rstd", [P, TM])
    total = c.sb("d_total", [P, 2])
    scale = c.sb("d_scale", [P, 2])
    rscale = c.sb("d_rscale", [P, 2])
    ones = c.sb("d_ones", [P, P])
    tern = c.sb("d_tern", [P, 2, BANK])
    wt1 = c.sb("d_wt1", [P, BANK], F16)
    wt2 = c.sb("d_wt2", [P, BANK])
    ps_x = c.ps("d_ps_x", [P, BANK])
    ps_h = [c.ps(f"d_ps_h{j}", [P, BANK]) for j in range(4)]
    ps_out = [c.ps(f"d_ps_out{j}", [P, TM, D]) for j in range(2)]
    ps_sum = c.ps("d_ps_sum", [P, 2])

    x_in_ready = [c.sem(f"d_x_in_ready{j}") for j in range(2)]
    x_turned = c.sem("d_x_turned")
    xTh_ready = c.sem("d_xTh_ready")
    xTl_ready = c.sem("d_xTl_ready")
    ones_set = c.sem("d_ones_set")
    total_ready = c.sem("d_total_ready")
    sum_ready = c.sem("d_sum_ready")
    tern_step = c.sem("d_tern_step")
    wt_ready = c.sem("d_wt_ready")
    h_made = c.sem("d_h_made")
    h_ready = c.sem("d_h_ready")
    out_ready = c.sem("d_out_ready")
    out_used = c.sem("d_out_used")
    mv_ready = c.sem("d_mv_ready")
    var_ready = c.sem("d_var_ready")
    rstd_ready = c.sem("d_rstd_ready")
    final_ready = c.sem("d_final_ready")

    def each_turn(eng, body):
        for i in range(2):
            body(i, i, True, True)
        with eng.Fori(1, TURNS // 2 - 1) as k:
            for p in range(2):
                body(2 * k + p, p, True, True)
        for p in range(2):
            body(TURNS - 2 + p, p, p == 0, False)

    with nc.Block() as block:

        @block.sync
        def _(sp):
            out_rows = out.rearrange("b n d -> (b n) d")

            def load(i, p):
                sp.dma_start(x_in[:, p, :, :], x_all[:, ds(i * TM, TM), :]).then_inc(x_in_ready[p], 16)

            def turn(i, p, next1, next2):
                if next2:
                    sp.wait_ge(x_turned, i + 1)
                    load(i + 2, p)
                sp.wait_ge(final_ready, i + 1)
                sp.dma_start(out_rows[ds(i * BANK, BANK), :].rearrange("(t p) d -> p t d", p=P), final[:, p, :, :])\
                  .then_inc(stored[p], 16)

            load(0, 0)
            load(1, 1)
            each_turn(sp, turn)

        @block.gpsimd
        def _(pool):
            nc.gpsimd.memset(ones[:, :], 1.0).then_inc(ones_set, 1)
            with pool.Fori(0, TURNS) as i:
                pool.wait_ge(var_ready, i + 1)
                nc.gpsimd.tensor_tensor(rstd[:, :], mv[:, :, 1], mhalf[:, 0:TM], ALU.pow).then_inc(rstd_ready, 1)

        @block.tensor
        def _(pe):
            pe.wait_ge(consts_ready, CONSTS)
            pe.wait_ge(w["D_ready"], W_D)

            def turn_x(i, p):
                pe.wait_ge(x_in_ready[p], (i - p) * 8 + 16)
                if not zero(i):
                    pe.wait_ge(xTl_ready, i)
                for t in range(TM):
                    last = nc.tensor.transpose(ps_x[:, t * P:(t + 1) * P], x_in[:, p, t, :], ident[:, :])
                last.then_inc(x_turned, 1)

            def hidden(i, p):
                pe.wait_ge(xTl_ready, i + 1)
                for j in range(C):
                    if not zero(i):
                        pe.wait_ge(h_ready, (i - 1) * C + j + 1)
                    nc.tensor.matmul(ps_h[j][:, :], wt1[:, j * P:(j + 1) * P], xTh[:, p, :], start=True, stop=False)
                    nc.tensor.matmul(ps_h[j][:, :], wt1[:, j * P:(j + 1) * P], xTl[:, p, :], start=False, stop=True)\
                        .then_inc(h_made, 1)

            def outputs(i, p):
                if not (isinstance(i, int) and i < 2):
                    pe.wait_ge(out_used, i - 1)
                pe.wait_ge(h_ready, i * C + C)
                for t in range(TM):
                    for j in range(C):
                        nc.tensor.matmul(ps_out[p][:, t, :], h[:, p, j, t * P:(t + 1) * P], wt2[:, j * P:(j + 1) * P],
                                         start=(j == 0), stop=False)
                    last = nc.tensor.matmul(ps_out[p][:, t, :], ones_row[:, :], w["D_b2"][:, :],
                                            start=False, stop=True)
                last.then_inc(out_ready, 1)

            def turn(i, p, next1, next2):
                if next1:
                    hidden(i + 1, 1 - p)
                outputs(i, p)
                if next2:
                    turn_x(i + 2, p)

            turn_x(0, 0)
            pe.wait_ge(ones_set, 1)
            pe.wait_ge(total_ready, 1)
            nc.tensor.matmul(ps_sum[:, :], ones[:, :], total[:, :], start=True, stop=True).then_inc(sum_ready, 1)
            turn_x(1, 1)
            pe.wait_ge(wt_ready, 1)
            hidden(0, 0)
            pe.wait_ge(wt_ready, 2)
            each_turn(pe, turn)

        @block.scalar
        def _(act):
            act.wait_ge(w["D_ready"], W_D)

            def x_hi(i, p):
                act.wait_ge(x_turned, i + 1)
                if not (isinstance(i, int) and i < 2):
                    act.wait_ge(h_made, (i - 1) * C)
                nc.scalar.copy(xTh[:, p, :], ps_x[:, :]).then_inc(xTh_ready, 1)

            def gelu(i, p):
                if not (isinstance(i, int) and i < 2):
                    act.wait_ge(out_ready, i - 1)
                for j in range(C):
                    act.wait_ge(h_made, i * C + j + 1)
                    nc.scalar.activation(h[:, p, j, :], ps_h[j][:, :], ACT.Gelu, bias=w["D_b1"][:, j:j + 1])\
                        .then_inc(h_ready, 1)

            def turn(i, p, next1, next2):
                if next1:
                    gelu(i + 1, 1 - p)
                if next2:
                    x_hi(i + 2, p)

            x_hi(0, 0)
            x_hi(1, 1)
            gelu(0, 0)
            each_turn(act, turn)

        @block.vector
        def _(dve):
            dve.wait_ge(w["D_ready"], W_D)
            for j in range(2):
                last = nc.vector.tensor_reduce(total[:, j:j + 1], w[f"D_W{j + 1}"][:, :], AX_X, ALU.add,
                                               apply_absolute_value=True)
            last.then_inc(total_ready, 1)
            dve.wait_ge(sum_ready, 1)
            n = 0

            def step(ins):
                nonlocal n
                n += 1
                ins.then_inc(tern_step, 1)
                dve.wait_ge(tern_step, n)

            def x_lo(i, p):
                dve.wait_ge(xTh_ready, i + 1)
                nc.vector.tensor_tensor(xTl[:, p, :], ps_x[:, :], xTh[:, p, :], ALU.subtract).then_inc(xTl_ready, 1)

            def finish(i, p):
                dve.wait_ge(out_ready, i + 1)
                if not zero(i):
                    dve.wait_ge(final_ready, i)
                nc.vector.tensor_tensor(rows[:, :, :], ps_out[p][:, :, :], x_all[:, ds(i * TM, TM), :], ALU.add)\
                    .then_inc(out_used, 1)
                dve.wait_ge(out_used, i + 1)
                row_variance(dve, nc, rows, stats, mv, TM, mv_ready, i + 1, var_ready)
                if not (isinstance(i, int) and i < 2):
                    dve.wait_ge(stored[p], (i - p) * 8)
                dve.wait_ge(rstd_ready, i + 1)
                row_normalise(nc, rows, mv, rstd, TM, lambda t: final[:, p, t, :]).then_inc(final_ready, 1)

            def turn(i, p, next1, next2):
                if next2:
                    x_lo(i + 2, p)
                finish(i, p)

            step(nc.vector.tensor_scalar(scale[:, :], ps_sum[:, :], 1.0 / (4 * D * D), 1e-8, ALU.mult, ALU.max))
            step(nc.vector.reciprocal(rscale[:, :], scale[:, :]))
            x_lo(0, 0)
            for j, wt in enumerate((wt1, wt2)):
                src, t = w[f"D_W{j + 1}"][:, :], tern[:, j, :]
                step(nc.vector.tensor_scalar(t, src, rscale[:, j:j + 1], None, ALU.mult))
                step(nc.vector.tensor_scalar(t, t, MAGIC, None, ALU.add))
                step(nc.vector.tensor_scalar(t, t, -MAGIC, None, ALU.add))
                step(nc.vector.tensor_scalar(t, t, -1.0, 1.0, ALU.max, ALU.min))
                step(nc.vector.tensor_tensor(t, t, src, ALU.subtract))
                nc.vector.tensor_tensor(wt[:, :], src, t, ALU.add).then_inc(wt_ready, 1)
                if j == 0:
                    x_lo(1, 1)
            each_turn(dve, turn)


CONSTS = 4
W_SCALE = 64.0
PIECE = 1024
PIECES = 3 * 4
W_A = 16 * 2
W_B = 16 * 7
W_C = 16
W_D = 16 * 4


def load_small_weights(eng, a, w):
    eng.dma_start(w["B_gate"][:, :], a["L0_ffn_gate_W"]).then_inc(w["B_ready"], 16)
    for j, n in enumerate(("ln1_g", "ln1_b", "ln2_g", "ln2_b")):
        eng.dma_start(w["B_lnrow"][:, j, :], a["L0_ffn_" + n].partition_broadcast(P)).then_inc(w["B_ready"], 16)
    eng.dma_start(w["B_b1"][:, :], a["L0_ffn_b1"]).then_inc(w["B_ready"], 16)
    eng.dma_start(w["B_b2"][:, :], a["L0_ffn_b2"]).then_inc(w["B_ready"], 16)
    eng.dma_start(w["C_out"][:, :, :], a["L1_attn_w_out"].rearrange("(m p) n -> p m n", p=P))\
        .then_inc(w["C_ready"], 16)
    eng.dma_start(w["D_W1"][:, :], a["L1_ffn_W1"]).then_inc(w["D_ready"], 16)
    eng.dma_start(w["D_W2"][:, :].rearrange("p (j d) -> p j d", d=D),
                  a["L1_ffn_W2"].rearrange("(j p) d -> p j d", p=P)).then_inc(w["D_ready"], 16)
    eng.dma_start(w["D_b1"][:, :], a["L1_ffn_b1"]).then_inc(w["D_ready"], 16)
    eng.dma_start(w["D_b2"][:, :], a["L1_ffn_b2"].rearrange("(a n) -> a n", a=1)).then_inc(w["D_ready"], 16)


def weight_piece(a, n, slot):
    kind, j = divmod(n, 4)
    if kind == 0:
        return slot.rearrange("p (e f) -> p e f", e=2), a["L0_ffn_W1"][2 * j:2 * j + 2].rearrange("e p f -> p e f")
    if kind == 1:
        return (slot.rearrange("p (n d) -> p n d", d=D),
                a["L0_ffn_W2"][2 * j:2 * j + 2].rearrange("e (j p) d -> p (e j) d", p=P))
    return slot, (a["L1_attn_w_qkv"][:, j * PIECE:(j + 1) * PIECE] if j < 3 else a["L1_attn_w_gate"])


def two_blocks(nc, a, out, stages="ABCD"):
    with ExitStack() as stack:
        c = Chip(nc, stack)
        x_all = c.sb("x_all", [P, TILES, D])
        ident = c.sb("ident", [P, P])
        ones_row = c.sb("ones_row", [1, P])
        mhalf = c.sb("mhalf", [P, 8])
        consts_ready = c.sem("consts_ready")
        consts_step = c.sem("consts_step")

        w = {"split": c.sem("w_split"), "B_split": c.sem("B_split"), "B_ready": c.sem("B_ready"), "C_ready": c.sem("C_ready"),
             "D_ready": c.sem("D_ready")}
        for half in "hl":
            w[half] = c.sb("w_" + half, [P, PIECES * PIECE], F16)
            for j, name in enumerate(("B_W1", "B_W2", "C_w")):
                w[name + half] = w[half][:, 4 * j * PIECE:4 * (j + 1) * PIECE]
        w["C_out"] = c.sb("C_out", [P, PAIRS, D])
        w["D_W1"] = c.sb("D_W1", [P, 4 * D])
        w["D_W2"] = c.sb("D_W2", [P, 4 * D])
        w["D_b1"] = c.sb("D_b1", [P, 4])
        w["D_b2"] = c.sb("D_b2", [1, D])

        b_stack = stack.enter_context(ExitStack())
        b_mem = Chip(nc, b_stack)
        for half in "hl":
            w["B_w" + half] = b_mem.sb("B_w" + half, [P, 3 * D], F16)
        w["B_gate"] = b_mem.sb("B_gate", [P, 8])
        w["B_b1"] = b_mem.sb("B_b1", [P, 32])
        w["B_b2"] = b_mem.sb("B_b2", [8, D])
        lnrow = w["B_lnrow"] = b_mem.sb("B_lnrow", [P, 4, D])

        a_stack = stack.enter_context(ExitStack())
        a_mem = Chip(nc, a_stack)
        wa = {"ready": a_mem.sem("A_ready"), "o": a_mem.sb("A_wo", [P, PAIRS, D]), "bo": a_mem.sb("A_bo", [1, D])}

        with nc.Block() as block:

            @block.gpsimd
            def _(pool):
                nc.gpsimd.memset(ident[:, :], 0.0).then_inc(consts_step, 1)
                nc.gpsimd.memset(ones_row[:, :], 1.0).then_inc(consts_ready, 1)
                nc.gpsimd.memset(mhalf[:, :], -0.5).then_inc(consts_ready, 1)
                pool.wait_ge(consts_step, 1)
                nc.gpsimd.affine_select(out=ident[:, :], in_=ident[:, :], compare_op=ALU.not_equal, fill=1.0,
                                        base=0, pattern=[[-1, P]], channel_multiplier=1).then_inc(consts_ready, 2)

        def stage(f, *args):
            with ExitStack() as inner:
                f(nc, Chip(nc, inner), *args)

        if "A" in stages:
            stage(stage_a, a, x_all, w, wa, ident, ones_row, mhalf, consts_ready)
        a_stack.close()
        y_all = b_mem.sb("y_all", [P, TILES, D])
        if "b" in stages:
            stage(stage_b_attention, x_all, y_all, w, ident, consts_ready, mhalf, lnrow)
        if "B" in stages:
            stage(stage_b_experts, x_all, y_all, w, ident, consts_ready, mhalf, lnrow)
        b_stack.close()
        if "C" in stages:
            stage(stage_c, x_all, w, ident, consts_ready, mhalf)
        stored = [c.sem(f"stored{j}") for j in range(2)]
        if "D" in stages:
            stage(stage_d, x_all, out, w, ident, ones_row, consts_ready, mhalf, stored)
        with nc.Block() as block:
            @block.sync
            def _(sp):
                if "D" in stages:
                    for s in stored:
                        sp.wait_ge(s, 16 * TILES // 8)
                else:
                    sp.dma_start(out.rearrange("b (t p) d -> p (b t) d", p=P), x_all[:, :, :]).then_inc(stored[0], 16)
                    sp.wait_ge(stored[0], 16)


_INS = ['L0_attn_x', 'L0_attn_Wq', 'L0_attn_Wk', 'L0_attn_Wv', 'L0_attn_Wo', 'L0_attn_bo',
        'L0_ffn_Wq', 'L0_ffn_Wk', 'L0_ffn_Wv', 'L0_ffn_gate_W', 'L0_ffn_W1', 'L0_ffn_b1', 'L0_ffn_W2', 'L0_ffn_b2',
        'L0_ffn_ln1_g', 'L0_ffn_ln1_b', 'L0_ffn_ln2_g', 'L0_ffn_ln2_b',
        'L1_attn_w_qkv', 'L1_attn_w_gate', 'L1_attn_w_out', 'L1_ffn_W1', 'L1_ffn_b1', 'L1_ffn_W2', 'L1_ffn_b2']
_OUTS = [((B, N, D), 'float32')]


def kernel(**inputs):
    import numpy as _np
    import concourse.bacc as _bacc
    from concourse import mybir as _mybir
    from concourse.bass_utils import run_bass_kernel_spmd as _run

    nc = _bacc.Bacc("TRN2", target_bir_lowering=False, num_devices=1)
    arrays, args = {}, {}
    for name in _INS:
        a = _np.asarray(inputs[name])
        if name in ('L0_ffn_Wq', 'L0_ffn_Wk', 'L0_ffn_Wv'):
            a = a.transpose(1, 0, 2)
        if name in ('L1_ffn_W1', 'L1_ffn_W2'):
            a = a.T
        if name in ('L0_ffn_b1', 'L1_ffn_b1'):
            a = a.reshape(-1, 128).T
        a = _np.ascontiguousarray(a)
        arrays[f"in_{name}_dram"] = a
        args[name] = nc.dram_tensor(f"in_{name}_dram", a.shape, _mybir.dt.from_np(a.dtype), kind="ExternalInput").ap()
    shape, dtype = _OUTS[0]
    out = nc.dram_tensor("out_0_dram", shape, _mybir.dt.from_np(_np.dtype(dtype)), kind="ExternalOutput").ap()
    two_blocks(nc, args, out, "AbBCD")
    r = _run(nc, [arrays], core_ids=[0])
    return r.results[0]["out_0_dram"]
```

```python
from contextlib import ExitStack

import concourse.bass as bass
from concourse import mybir

F32 = mybir.dt.float32
BF16 = mybir.dt.bfloat16
F16 = mybir.dt.float16
U32 = mybir.dt.uint32
ALU = mybir.AluOpType
ACT = mybir.ActivationFunctionType
AX_X = mybir.AxisListType.X
ds = bass.ds

P = 128
BANK = 512
B, N, D = 16, 256, 128
TT = N // P
TILES = B * TT
H, DH = 16, 64
PAIRS = H // 2
HD = H * DH
LN_EPS = 1e-5


class Chip:

    given = set()

    def __init__(self, nc, stack):
        self.nc, self.stack = nc, stack

    def sb(self, name, shape, dt=F32):
        return self.stack.enter_context(self.nc.sbuf_tensor(name, shape, dt))

    def ps(self, name, shape, dt=F32):
        return self.stack.enter_context(self.nc.psum_tensor(name, shape, dt))

    def sem(self, name):
        sem = self.stack.enter_context(self.nc.semaphore(name))
        assert sem.num not in Chip.given, name
        Chip.given.add(sem.num)
        return sem


def each_batch(eng, body):
    for b in range(2):
        body(b, b, b == 0, True, True)
    with eng.Fori(1, B // 2 - 1) as i:
        for p in range(2):
            body(2 * i + p, p, False, True, True)
    for p in range(2):
        b = B - 2 + p
        body(b, p, False, b + 1 < B, b + 2 < B)


def zero(b):
    return isinstance(b, int) and b == 0


def row_variance(dve, nc, rows, stats, mv, tiles, step, value, var_ready):
    for t in range(tiles):
        nc.vector.bn_stats(stats[:, t, :], rows[:, t, :])
    dve.drain()
    for t in range(tiles):
        ins = nc.vector.bn_aggr(mv[:, t, :], stats[:, t, :])
    ins.then_inc(step, 1)
    dve.wait_ge(step, value)
    nc.vector.tensor_scalar(mv[:, :, 1], mv[:, :, 1], LN_EPS, None, ALU.add).then_inc(var_ready, 1)


def row_normalise(nc, rows, mv, rstd, tiles, out):
    for t in range(tiles):
        last = nc.vector.tensor_scalar(out(t), rows[:, t, :], mv[:, t, 0:1], rstd[:, t:t + 1],
                                       ALU.subtract, ALU.mult)
    return last


def stage_a(nc, c, a, x_all, w, wa, ident, mhalf, consts_ready):
    VB = 2 * DH + 2
    RING = 3
    UNIT = TT * (HD // BANK)
    PROJ = 3 * UNIT
    FEAT = 2 * UNIT
    KVG = [(0, 2), (2, 4), (4, 6), (6, 8)]
    APG = [(0, 3), (3, 6), (6, 8)]
    MIX = len(KVG) + TT * len(APG)
    SCALE = 1.0 / 64
    assert PROJ % RING == 0 and MIX % 2 == 0 and MIX + 2 == PROJ

    x_in = c.sb("a_x_in", [P, 2, TT, D])
    wh = c.sb("a_wh", [P, 3, HD], F16)
    wl = c.sb("a_wl", [P, 3, HD], F16)
    xTh = c.sb("a_xTh", [P, 2, N], F16)
    xTl = c.sb("a_xTl", [P, 2, N], F16)
    k = c.sb("a_k", [P, 2, TT, HD])
    v = c.sb("a_v", [P, 2, TT, PAIRS, VB])
    qT = c.sb("a_qT", [P, 2, PAIRS, N])
    w_full = [k[:, 1, 0, :], k[:, 1, 1, :], qT[:, 1, 0:HD // N, :].rearrange("p m n -> p (m n)")]
    kv = c.sb("a_kv", [P, PAIRS, VB])
    ex = c.sb("a_exp", [P, 2, BANK])
    re = c.sb("a_relu", [P, 2, BANK])
    den = c.sb("a_den", [P, MIX, 6])
    rden = c.sb("a_rden", [P, MIX, 6])
    on = c.sb("a_on", [P, 2, 3 * P])
    onh = c.sb("a_onh", [P, 2, TT, HD], F16)
    onl = c.sb("a_onl", [P, 2, TT, HD], F16)
    onT = c.sb("a_onT", [P, TT, 2, 2, BANK], F16)
    woh = c.sb("a_woh", [P, PAIRS, D], F16)
    wol = c.sb("a_wol", [P, PAIRS, D], F16)
    row64 = c.sb("a_row64", [1, P])
    identh = c.sb("a_identh", [P, P], F16)
    rows = c.sb("a_rows", [P, TT, D])
    stats = c.sb("a_stats", [P, TT, 6])
    mv = c.sb("a_mv", [P, TT, 2])
    rstd = c.sb("a_rstd", [P, TT])
    piece = c.sb("a_piece", [P, 2, PIECE])
    qkv = c.sb("a_B_qkv", [P, 3 * D])
    PEELED = 2
    assert PIECES == B - 2 * PEELED
    ps_proj = [c.ps(f"a_ps_proj{j}", [P, BANK]) for j in range(RING)]
    ps_mix = [c.ps(f"a_ps_mix{j}", [P, BANK]) for j in range(2)]
    ps_turn = [c.ps(f"a_ps_turn{j}", [P, BANK]) for j in range(2)]
    ps_out = c.ps("a_ps_out", [P, TT, D])

    x_in_ready = [c.sem(f"a_x_in_ready{j}") for j in range(2)]
    x_all_ready = c.sem("a_x_all_ready")
    w_ready = [c.sem(f"a_w_ready{j}") for j in range(3)]
    wh_ready = c.sem("a_wh_ready")
    wl_ready = c.sem("a_wl_ready")
    x_turned = c.sem("a_x_turned")
    xTh_ready = c.sem("a_xTh_ready")
    xTl_ready = c.sem("a_xTl_ready")
    slots_set = c.sem("a_slots_set")
    proj_ready = c.sem("a_proj_ready")
    proj_free = c.sem("a_proj_free")
    feat_free = c.sem("a_feat_free")
    mix_ready = c.sem("a_mix_ready")
    mix_free = c.sem("a_mix_free")
    on_turned = c.sem("a_on_turned")
    onT_ready = c.sem("a_onT_ready")
    onh_ready = c.sem("a_onh_ready")
    onl_ready = c.sem("a_onl_ready")
    out_ready = c.sem("a_out_ready")
    out_used = c.sem("a_out_used")
    den_step = c.sem("a_den_step")
    mv_ready = c.sem("a_mv_ready")
    var_ready = c.sem("a_var_ready")
    rstd_ready = c.sem("a_rstd_ready")
    rows_done = c.sem("a_rows_done")
    piece_ready = [c.sem(f"a_piece_ready{j}") for j in range(2)]
    piece_upper = c.sem("a_piece_upper")
    qkv_ready = c.sem("a_B_qkv_ready")
    small_upper = c.sem("a_small_upper")

    x_dram = a["L0_attn_x"].rearrange("b n d -> (b n) d")

    def rows_of(b, n):
        t, g = divmod(n - len(KVG), len(APG))
        return (t, *APG[g], b * TT * len(APG) + n - len(KVG))

    with nc.Block() as block:

        @block.sync
        def _(sp):
            def load(b, p):
                sp.dma_start(x_in[:, p, :, :], x_dram[ds(b * N, N), :].rearrange("(t p) d -> p t d", p=P))\
                  .then_inc(x_in_ready[p], 16)

            load(0, 0)
            for j, n in enumerate("kqv"):
                sp.dma_start(w_full[j], a["L0_attn_W" + n]).then_inc(w_ready[j], 16)
            load(1, 1)
            sp.dma_start(wa["o"][:, :, :], a["L0_attn_Wo"].rearrange("(m p) n -> p m n", p=P)).then_inc(wa["ready"], 16)
            sp.dma_start(wa["bo"][:, :], a["L0_attn_bo"].rearrange("(a n) -> a n", a=1)).then_inc(wa["ready"], 16)
            sp.dma_start(x_all[:, :, :], x_dram.rearrange("(t p) d -> p t d", p=P)).then_inc(x_all_ready, 16)
            for j, n in enumerate("qkv"):
                sp.dma_start(qkv[:, j * D:(j + 1) * D], a["L0_ffn_W" + n].rearrange("p h f -> p (h f)"))\
                    .then_inc(qkv_ready, 16)
            load_small_weights(sp, a, w, wa)
            with sp.Fori(0, B // 2 - 1) as i:
                for p in range(2):
                    sp.wait_ge(x_turned, 2 * i + p + 1)
                    load(2 * i + p + 2, p)

        @block.gpsimd
        def _(pool):
            nc.gpsimd.memset(kv[:, :, :], 0.0).then_inc(slots_set, 1)
            nc.gpsimd.memset(v[:, :, :, :, 0:1], 1.0).then_inc(slots_set, 1)
            nc.gpsimd.memset(v[:, :, :, :, VB - 1:VB], 1.0).then_inc(slots_set, 1)
            nc.gpsimd.memset(row64[:, :], W_SCALE).then_inc(slots_set, 1)
            pool.wait_ge(consts_ready, CONSTS)
            nc.gpsimd.tensor_copy(identh[:, :], ident[:, :]).then_inc(slots_set, 1)
            def load(n):
                pool.dma_start(*weight_piece(a, n, piece[:, n % 2, :])).then_inc(piece_ready[n % 2], 16)

            def power(b):
                pool.wait_ge(var_ready, b + 1)
                nc.gpsimd.tensor_tensor(rstd[:, :], mv[:, :, 1], mhalf[:, 0:TT], ALU.pow).then_inc(rstd_ready, 1)

            def on_lo(b, p, n):
                t, m0, m1, u = rows_of(b, n)
                pool.wait_ge(onh_ready, u + 1)
                nc.gpsimd.tensor_tensor(onl[:, p, t, m0 * P:m1 * P], on[:, n % 2, 0:(m1 - m0) * P],
                                        onh[:, p, t, m0 * P:m1 * P], ALU.subtract).then_inc(onl_ready, 1)

            load(0)
            load(1)
            def batch(b, p, first, next1, next2):
                for n in range(len(KVG), MIX):
                    on_lo(b, p, n)
                if not first:
                    power(b - 1)

            def fetch(n):
                pool.wait_ge(w["split"], n - 1)
                load(n)

            for b in range(B):
                batch(b, b % 2, b == 0, True, True)
                if PEELED <= b and b < PIECES:
                    fetch(b)
            power(B - 1)

        @block.tensor
        def _(pe):
            pe.wait_ge(consts_ready, CONSTS)
            pe.wait_ge(slots_set, 5)

            def turn_x(b, p):
                pe.wait_ge(x_in_ready[p], (b - p) * 8 + 16)
                for t in range(TT):
                    last = nc.tensor.transpose(ps_turn[0][:, t * P:(t + 1) * P], x_in[:, p, t, :], ident[:, :])
                last.then_inc(x_turned, 1)

            def halves(out, lhs_h, lhs_l, rhs_h, rhs_l):
                nc.tensor.matmul(out, lhs_h, rhs_h, start=True, stop=False)
                nc.tensor.matmul(out, lhs_h, rhs_l, start=False, stop=False)
                return nc.tensor.matmul(out, lhs_l, rhs_h, start=False, stop=True)

            def project(b, p, u):
                if u == 0:
                    pe.wait_ge(xTl_ready, b + 1)
                pe.wait_ge(proj_free, b * PROJ + u + 1)
                bank = ps_proj[u % RING]
                kind, r = divmod(u, UNIT)
                if zero(b) and r == 0:
                    pe.wait_ge(wl_ready, kind + 1)
                if kind == 1:
                    for s in range(2):
                        m = slice((2 * r + s) * P, (2 * r + s + 1) * P)
                        last = halves(bank[:, s * N:(s + 1) * N], wh[:, 1, m], wl[:, 1, m], xTh[:, p, :], xTl[:, p, :])
                else:
                    t, h = divmod(r, HD // BANK)
                    m, s = slice(h * BANK, (h + 1) * BANK), slice(t * P, (t + 1) * P)
                    last = halves(bank[:, :], xTh[:, p, s], xTl[:, p, s], wh[:, kind, m], wl[:, kind, m])
                last.then_inc(proj_ready, 1)

            def key_values(b, p, n):
                if n == 0:
                    pe.wait_ge(feat_free, 2 + b * FEAT + UNIT)
                    pe.wait_ge(proj_free, RING + b * PROJ + PROJ)
                pe.wait_ge(mix_free, b * MIX + n + 1)
                m0, m1 = KVG[n]
                for m in range(m0, m1):
                    for t in range(TT):
                        last = nc.tensor.matmul(ps_mix[n % 2][:, (m - m0) * VB:(m - m0 + 1) * VB],
                                                k[:, p, t, m * P:(m + 1) * P], v[:, p, t, m, :],
                                                start=(t == 0), stop=(t == TT - 1))
                last.then_inc(mix_ready, 1)

            def query(b, p, n):
                if n == len(KVG):
                    pe.wait_ge(feat_free, 2 + b * FEAT + FEAT)
                t, g = divmod(n - len(KVG), len(APG))
                m0, m1 = APG[g]
                pe.wait_ge(mix_free, b * MIX + n + 1)
                pe.wait_ge(mix_free, 2 + b * MIX + min((m1 + 1) // 2, len(KVG)))
                for m in range(m0, m1):
                    last = nc.tensor.matmul(ps_mix[n % 2][:, (m - m0) * VB:(m - m0 + 1) * VB],
                                            qT[:, p, m, t * P:(t + 1) * P], kv[:, m, :], start=True, stop=True)
                last.then_inc(mix_ready, 1)

            def turn_on(b, p, j):
                t, half = divmod(j, 2)
                if j == 0:
                    pe.wait_ge(onl_ready, (b + 1) * TT * len(APG))
                    pe.wait_ge(xTl_ready, min(b + 4, B) if isinstance(b, int) else b + 4)
                elif j == 1:
                    if not zero(b):
                        pe.wait_ge(onT_ready, b * 4)
                else:
                    pe.wait_ge(onT_ready, b * 4 + j - 1)
                bank = ps_turn[j % 2][:, :].bitcast(F16)
                for l, src in enumerate((onh, onl)):
                    for i in range(4):
                        m = 4 * half + i
                        last = nc.tensor.transpose(bank[:, l * BANK + i * P:l * BANK + (i + 1) * P],
                                                   src[:, p, t, m * P:(m + 1) * P], identh[:, :])
                last.then_inc(on_turned, 1)

            def out_part(b, j):
                t, half = divmod(j, 2)
                pe.wait_ge(onT_ready, b * 4 + j + 1)
                if j == 0:
                    pe.wait_ge(w["split_small"], 1)
                    pe.wait_ge(wa["ready"], W_A)
                    if not zero(b):
                        pe.wait_ge(out_used, b)
                out = ps_out[:, t, :]
                for i in range(4):
                    m, at = 4 * half + i, slice(i * P, (i + 1) * P)
                    nc.tensor.matmul(out, onT[:, t, half, 0, at], woh[:, m, :], start=(m == 0), stop=False)
                    nc.tensor.matmul(out, onT[:, t, half, 0, at], wol[:, m, :], start=False, stop=False)
                    nc.tensor.matmul(out, onT[:, t, half, 1, at], woh[:, m, :], start=False, stop=False)
                if half == 1:
                    last = nc.tensor.matmul(out, row64[:, :], wa["bo"][:, :], start=False, stop=True)
                    if t == TT - 1:
                        last.then_inc(out_ready, 1)

            def batch(b, p, first, next1, next2):
                for m in range(PROJ):
                    if next1:
                        project(b + 1, 1 - p, m)
                    if not first and 5 <= m < 9:
                        turn_on(b - 1, 1 - p, m - 5)
                    if 1 <= m <= len(KVG):
                        key_values(b, p, m - 1)
                    elif 1 <= m <= MIX:
                        query(b, p, m - 1)
                    if not first and 6 <= m < 10:
                        out_part(b - 1, m - 6)
                    if m == 3 and next2:
                        if not (isinstance(b, int) and b < 2):
                            pe.wait_ge(onT_ready, 4 * (b - 1))
                        turn_x(b + 2, p)

            turn_x(0, 0)
            for u in range(PROJ):
                project(0, 0, u)
            turn_x(1, 1)
            each_batch(pe, batch)
            turn_on(B - 1, 1, 0)
            for j in range(4):
                if j < 3:
                    turn_on(B - 1, 1, j + 1)
                out_part(B - 1, j)

        @block.scalar
        def _(act):
            act.sem_inc(proj_free, RING)
            act.wait_ge(consts_ready, CONSTS)
            nc.scalar.activation(re[:, 0, 0:1], ident[:, 0:1], ACT.Exp)

            def split_upper(j):
                act.wait_ge(w_ready[j], 16)
                nc.scalar.mul(wh[:, j, :], w_full[j], W_SCALE).then_inc(wh_ready, 1)

            def piece_hi(b, p):
                act.wait_ge(piece_ready[p], (b - PEELED - p) * 8 + 16)
                nc.scalar.mul(w["h"][:, ds((b - PEELED) * PIECE, PIECE)], piece[:, p, :], W_SCALE)\
                    .then_inc(piece_upper, 1)

            def x_hi(b, p):
                act.wait_ge(x_turned, b + 1)
                if not (isinstance(b, int) and b < 2):
                    act.wait_ge(proj_ready, (b - 1) * PROJ)
                nc.scalar.copy(xTh[:, p, :], ps_turn[0][:, 0:N]).then_inc(xTh_ready, 1)

            def take(b, p, u):
                bank = ps_proj[u % RING]
                act.wait_ge(proj_ready, b * PROJ + u + 1)
                if u >= FEAT:
                    t, h = divmod(u - FEAT, HD // BANK)
                    nc.scalar.mul(v[:, p, t, 4 * h:4 * h + 4, 1:1 + P], bank[:, :].rearrange("p (m e) -> p m e", e=P),
                                  SCALE).then_inc(proj_free, 1)
                else:
                    act.wait_ge(feat_free, b * FEAT + u + 1)
                    nc.scalar.activation(ex[:, u % 2, :], bank[:, :], ACT.Exp, scale=SCALE)
                    nc.scalar.activation(re[:, u % 2, :], bank[:, :], ACT.Relu, scale=SCALE).then_inc(proj_free, 1)

            def take_on(b, j):
                t, half = divmod(j, 2)
                if j == 0 and not zero(b):
                    act.wait_ge(out_ready, b)
                act.wait_ge(on_turned, b * 4 + j + 1)
                nc.scalar.copy(onT[:, t, half, :, :].rearrange("p l q -> p (l q)"), ps_turn[j % 2][:, :].bitcast(F16))\
                    .then_inc(onT_ready, 1)

            def on_hi(b, p, n):
                t, m0, m1, u = rows_of(b, n)
                if n == len(KVG) and not (isinstance(b, int) and b < 2):
                    act.wait_ge(on_turned, 4 * (b - 1))
                act.wait_ge(mix_free, 2 + b * MIX + n + 1)
                nc.scalar.copy(onh[:, p, t, m0 * P:m1 * P], on[:, n % 2, 0:(m1 - m0) * P]).then_inc(onh_ready, 1)

            def batch(b, p, first, next1, next2):
                for m in range(PROJ):
                    if next1:
                        take(b + 1, 1 - p, m)
                    if not first and 5 <= m < 9:
                        take_on(b - 1, m - 5)
                    if len(KVG) + 2 <= m:
                        on_hi(b, p, m - 2)
                    if m == 3 and next2:
                        x_hi(b + 2, p)
                    if m == FEAT and not isinstance(b, int):
                        piece_hi(b, p)
                if first:
                    act.wait_ge(wa["ready"], W_A)
                    nc.scalar.mul(woh[:, :, :], wa["o"][:, :, :], W_SCALE).then_inc(small_upper, 1)
                    act.wait_ge(w["C_ready"], W_C)
                    nc.scalar.mul(w["C_oh"][:, :, :], wa["C_out"][:, :, :], W_SCALE).then_inc(small_upper, 1)
                    act.wait_ge(qkv_ready, 3 * 16)
                    nc.scalar.mul(w["B_wh"][:, :], qkv[:, :], W_SCALE).then_inc(small_upper, 1)

            split_upper(0)
            x_hi(0, 0)
            split_upper(1)
            split_upper(2)
            for u in range(PROJ):
                take(0, 0, u)
            x_hi(1, 1)
            each_batch(act, batch)
            for j in range(4):
                take_on(B - 1, j)

        @block.vector
        def _(dve):
            dve.sem_inc(feat_free, 2)
            dve.sem_inc(mix_free, 2)
            dve.wait_ge(slots_set, 5)

            def split_lower(j):
                dve.wait_ge(wh_ready, j + 1)
                nc.vector.scalar_tensor_tensor(wl[:, j, :], w_full[j], W_SCALE, wh[:, j, :],
                                               ALU.mult, ALU.subtract).then_inc(wl_ready, 1)

            def piece_lo(b, p):
                dve.wait_ge(piece_upper, b - PEELED + 1)
                at = ds((b - PEELED) * PIECE, PIECE)
                nc.vector.scalar_tensor_tensor(w["l"][:, at], piece[:, p, :], W_SCALE, w["h"][:, at],
                                               ALU.mult, ALU.subtract).then_inc(w["split"], 1)

            def x_lo(b, p):
                dve.wait_ge(xTh_ready, b + 1)
                nc.vector.tensor_tensor(xTl[:, p, :], ps_turn[0][:, 0:N], xTh[:, p, :], ALU.subtract)\
                    .then_inc(xTl_ready, 1)

            def feature(b, p, u):
                kind, r = divmod(u, UNIT)
                t, h = divmod(r, HD // BANK)
                out = (k[:, p, t, h * BANK:(h + 1) * BANK],
                       qT[:, p, 2 * r:2 * r + 2, :].rearrange("p m q -> p (m q)"))[kind]
                dve.wait_ge(proj_free, RING + b * PROJ + u + 1)
                nc.vector.scalar_tensor_tensor(out, ex[:, u % 2, :], 1.0, re[:, u % 2, :], ALU.min, ALU.add)\
                    .then_inc(feat_free, 1)

            def take_kv(b, n):
                m0, m1 = KVG[n]
                dve.wait_ge(mix_ready, b * MIX + n + 1)
                src = ps_mix[n % 2][:, 0:(m1 - m0) * VB].rearrange("p (m e) -> p m e", e=VB)
                nc.vector.tensor_copy(kv[0:DH, m0:m1, 0:DH + 1], src[0:DH, :, 0:DH + 1])
                nc.vector.tensor_copy(kv[DH:P, m0:m1, DH + 1:VB], src[DH:P, :, DH + 1:VB]).then_inc(mix_free, 1)

            def divide(b, n):
                t, g = divmod(n - len(KVG), len(APG))
                m0, m1 = APG[g]
                ms, u = m1 - m0, b * (MIX - len(KVG)) + n - len(KVG)
                if not (zero(b) and n < len(KVG) + 2):
                    dve.wait_ge(onl_ready, u - 1)
                dve.wait_ge(mix_ready, b * MIX + n + 1)
                src = ps_mix[n % 2][:, 0:ms * VB].rearrange("p (m e) -> p m e", e=VB)
                d = den[:, n, 0:2 * ms].rearrange("p (m s) -> p m s", s=2)
                r = rden[:, n, 0:2 * ms].rearrange("p (m s) -> p m s", s=2)
                nc.vector.tensor_scalar(d, src[:, :, 0:VB:VB - 1], 1e-6, None, ALU.add).then_inc(den_step, 1)
                dve.wait_ge(den_step, 2 * u + 1)
                nc.vector.reciprocal(r, d).then_inc(den_step, 1)
                dve.wait_ge(den_step, 2 * u + 2)
                nc.vector.tensor_tensor(
                    on[:, n % 2, 0:ms * P].rearrange("p (m s e) -> p m s e", s=2, e=DH),
                    src[:, :, 1:1 + P].rearrange("p m (s e) -> p m s e", s=2),
                    r.unsqueeze(3).broadcast_to([P, ms, 2, DH]), ALU.mult).then_inc(mix_free, 1)

            def add_residual(b):
                if not zero(b):
                    dve.wait_ge(rows_done, b)
                dve.wait_ge(out_ready, b + 1)
                nc.vector.scalar_tensor_tensor(rows[:, :, :], ps_out[:, :, :], SCALE, x_all[:, ds(b * TT, TT), :],
                                               ALU.mult, ALU.add)\
                    .then_inc(out_used, 1)

            def variance(b):
                dve.wait_ge(out_used, b + 1)
                row_variance(dve, nc, rows, stats, mv, TT, mv_ready, b + 1, var_ready)

            def normalise(b):
                dve.wait_ge(rstd_ready, b + 1)
                row_normalise(nc, rows, mv, rstd, TT,
                              lambda t: x_all[:, ds(b * TT + t, 1), :].squeeze(1)).then_inc(rows_done, 1)

            def batch(b, p, first, next1, next2):
                for m in range(PROJ):
                    if 1 <= m <= len(KVG):
                        take_kv(b, m - 1)
                    elif 1 <= m <= MIX:
                        divide(b, m - 1)
                    if next1 and 1 <= m <= FEAT:
                        feature(b + 1, 1 - p, m - 1)
                    if m == MIX and not first:
                        add_residual(b - 1)
                    if m == MIX and not first:
                        variance(b - 1)
                    if m == 3 and next2:
                        x_lo(b + 2, p)
                    if m == PROJ - 1 and not first:
                        normalise(b - 1)
                    if m == FEAT + 1 and not isinstance(b, int):
                        piece_lo(b, p)
                if first:
                    dve.wait_ge(small_upper, 1)
                    nc.vector.scalar_tensor_tensor(wol[:, :, :], wa["o"][:, :, :], W_SCALE, woh[:, :, :],
                                                   ALU.mult, ALU.subtract).then_inc(w["split_small"], 1)
                    dve.wait_ge(small_upper, 2)
                    nc.vector.scalar_tensor_tensor(w["C_ol"][:, :, :], wa["C_out"][:, :, :], W_SCALE,
                                                   w["C_oh"][:, :, :], ALU.mult, ALU.subtract)\
                        .then_inc(w["split_small"], 1)
                    dve.wait_ge(small_upper, 3)
                    nc.vector.scalar_tensor_tensor(w["B_wl"][:, :], qkv[:, :], W_SCALE, w["B_wh"][:, :],
                                                   ALU.mult, ALU.subtract).then_inc(w["split_small"], 1)

            split_lower(0)
            x_lo(0, 0)
            split_lower(1)
            split_lower(2)
            for u in range(FEAT):
                feature(0, 0, u)
            x_lo(1, 1)
            dve.wait_ge(x_all_ready, 16)
            each_batch(dve, batch)
            add_residual(B - 1)
            variance(B - 1)
            normalise(B - 1)
            dve.wait_ge(rows_done, B)


def stage_b_attention(nc, c, x_all, y_all, w, ident, consts_ready, mhalf, lnrow):
    G, HH, F = 4, 4, 8
    CH = 32
    MROW = 3 * F
    SC = 3 * P
    EXP_SCALE = 8 * float(D) ** -0.5
    SIDE = 7
    QKV0, QKV1, TQ, TK, BACK0, BACK1, TX = -1, 1, 2, 3, 4, 5, 6

    x_in = c.sb("b_x_in", [P, 2, TT, D])
    xTh = c.sb("b_xTh", [P, N], F16)
    xTl = c.sb("b_xTl", [P, N], F16)
    qs = c.sb("b_qs", [P, TT, G * HH, CH], F16)
    ks = c.sb("b_ks", [P, TT, G * HH, CH], F16)
    qsT = c.sb("b_qsT", [P, 2, G, N], F16)
    ksT = c.sb("b_ksT", [P, 2, G, N], F16)
    qmT = c.sb("b_qmT", [P, 2, N], F16)
    v = c.sb("b_v", [P, 2, TT, G * HH, 32])
    v_next = c.sb("b_v_next", [P, TT, D])
    negmax = c.sb("b_negmax", [P, 2, TT, HH, CH], F16)
    probs = c.sb("b_probs", [P, 2, HH, SC])
    oT = c.sb("b_oT", [P, G, N])
    rsum = c.sb("b_rsum", [P, TT, G * HH])
    attn = c.sb("b_attn", [P, TT, D])
    z = c.sb("b_z", [P, TT, D])
    zg = c.sb("b_zg", [P, TT, D])
    xb = c.sb("b_xb", [P, 2, TT, D])
    stats = c.sb("b_stats", [P, TT, 6])
    mv = c.sb("b_mv", [P, TT, 2])
    rstd = c.sb("b_rstd", [P, TT])
    mask = c.sb("b_mask", [P, 2, P], BF16)
    identb = c.sb("b_identb", [P, P], BF16)
    identh = c.sb("b_identh", [P, P], F16)
    turn_mark = c.sb("b_turn_mark", [P, 6])
    ps_sc = c.ps("b_ps_sc", [P, HH, BANK])
    ps_st = [c.ps(f"b_ps_st{j}", [P, BANK]) for j in range(2)]
    ps_pv = c.ps("b_ps_pv", [P, 2, N])
    ps_side = c.ps("b_ps_side", [P, BANK])
    side_h = ps_side[:, :].bitcast(F16)
    ps_mx = ps_st[0][:, SC:BANK].bitcast(F16)

    x_in_ready = [c.sem(f"b_x_in_ready{j}") for j in range(2)]
    x_turned = c.sem("b_x_turned")
    xb_ready = c.sem("b_xb_ready")
    v_ready = c.sem("b_v_ready")
    set_step = c.sem("b_set_step")
    slots_set = c.sem("b_slots_set")
    xTh_ready = c.sem("b_xTh_ready")
    xTl_ready = c.sem("b_xTl_ready")
    qkv_made = c.sem("b_qkv_made")
    hi_ready = c.sem("b_hi_ready")
    lo_ready = c.sem("b_lo_ready")
    stacks_turned = c.sem("b_stacks_turned")
    qsT_ready = c.sem("b_qsT_ready")
    ksT_ready = c.sem("b_ksT_ready")
    scores_ready = c.sem("b_scores_ready")
    max_ready = c.sem("b_max_ready")
    max_turned = c.sem("b_max_turned")
    qmT_ready = c.sem("b_qmT_ready")
    st_ready = c.sem("b_st_ready")
    st_free = c.sem("b_st_free")
    masked = c.sem("b_masked")
    pv_ready = c.sem("b_pv_ready")
    oT_ready = c.sem("b_oT_ready")
    back_ready = c.sem("b_back_ready")
    back_read = c.sem("b_back_read")
    dve_step = c.sem("b_dve_step")
    var_ready = c.sem("b_var_ready")
    rstd_ready = c.sem("b_rstd_ready")
    z_ready = c.sem("b_z_ready")
    zg_ready = c.sem("b_zg_ready")
    y_ready = c.sem("b_y_ready")

    with nc.Block() as block:

        @block.sync
        def _(sp):
            def load(b, p):
                sp.dma_start(x_in[:, p, :, :], x_all[:, ds(b * TT, TT), :]).then_inc(x_in_ready[p], 16)

            load(2, 0)
            load(3, 1)
            with sp.Fori(1, B // 2 - 1) as i:
                for p in range(2):
                    b = 2 * i + p
                    sp.wait_ge(x_turned, b + 1)
                    load(b + 2, p)

        @block.gpsimd
        def _(pool):
            nc.gpsimd.memset(negmax[:, :, :, :, :], 0.0).then_inc(slots_set, 1)
            nc.gpsimd.memset(turn_mark[:, :], 1.0).then_inc(slots_set, 1)
            nc.gpsimd.memset(qs[:, :, :, MROW:CH], 0.0).then_inc(slots_set, 1)
            nc.gpsimd.memset(ks[:, :, :, MROW + 1:CH], 0.0).then_inc(slots_set, 1)
            nc.gpsimd.memset(ks[:, :, :, MROW:MROW + 1], 1.0).then_inc(slots_set, 1)
            nc.gpsimd.memset(v[:, :, :, :, F + 1:32], 0.0).then_inc(slots_set, 1)
            nc.gpsimd.memset(v[:, :, :, :, F:F + 1], 1.0).then_inc(slots_set, 1)
            nc.gpsimd.memset(mask[:, :, :], 0.0).then_inc(set_step, 1)
            nc.gpsimd.memset(identb[:, :], 0.0).then_inc(set_step, 1)
            nc.gpsimd.memset(identh[:, :], 0.0).then_inc(set_step, 1)
            pool.wait_ge(set_step, 3)
            nc.gpsimd.affine_select(out=mask[:, :, :], in_=mask[:, :, :], compare_op=ALU.is_ge, fill=-1e30,
                                    base=0, pattern=[[0, 2], [-1, P]], channel_multiplier=1).then_inc(slots_set, 1)
            for m in (identb, identh):
                nc.gpsimd.affine_select(out=m[:, :], in_=m[:, :], compare_op=ALU.not_equal, fill=1.0,
                                        base=0, pattern=[[-1, P]], channel_multiplier=1).then_inc(slots_set, 1)

            def carry_wait(j):
                nc.gpsimd.tensor_tensor(turn_mark[:, j:j + 1], turn_mark[:, 5:6], turn_mark[:, 5:6], ALU.mult)

            def mask_probs(n, g):
                pool.wait_ge(st_free, 2 + n * HH + HH)
                carry_wait(g)
                diag = probs[:, g % 2, :, 0:2 * P]
                nc.gpsimd.affine_select(out=diag, in_=diag, compare_op=ALU.is_ge, fill=0.0, base=0,
                                        pattern=[[0, HH], [0, 2], [1, P]], channel_multiplier=-1)\
                    .then_inc(masked, 1)

            def take_v(b, p):
                pool.wait_ge(hi_ready, 2 * b + 2)
                if not (isinstance(b, int) and b < 2):
                    pool.wait_ge(pv_ready, (b - 1) * G)
                carry_wait(G)
                nc.gpsimd.tensor_copy(v[:, p, :, :, 0:F], v_next[:, :, :].rearrange("p t (h f) -> p t h f", f=F))\
                    .then_inc(v_ready, 1)

            def power(b):
                pool.wait_ge(var_ready, b + 1)
                nc.gpsimd.tensor_tensor(rstd[:, :], mv[:, :, 1], mhalf[:, 0:TT], ALU.pow).then_inc(rstd_ready, 1)

            def finish(b, p):
                pool.wait_ge(z_ready, b + 1)
                nc.gpsimd.tensor_tensor(zg[:, :, :], z[:, :, :],
                                        lnrow[:, 0, :].unsqueeze(1).broadcast_to([P, TT, D]), ALU.mult)\
                    .then_inc(zg_ready, 1)
                pool.wait_ge(zg_ready, b + 1)
                pool.wait_ge(xb_ready, b + 1)
                nc.gpsimd.tensor_tensor(y_all[:, ds(b * TT, TT), :], zg[:, :, :], xb[:, p, :, :], ALU.add)\
                    .then_inc(y_ready, 1)

            def batch(b, p, first, next1, next2):
                for g in range(G):
                    mask_probs(b * G + g, g)
                    if g == 1 and next1:
                        take_v(b + 1, 1 - p)
                    if g == 2 and not first:
                        power(b - 1)
                    if g == 3 and not first:
                        finish(b - 1, 1 - p)
                    if g == 0:
                        if not (isinstance(b, int) and b < 2):
                            pool.wait_ge(y_ready, b - 1)
                        nc.gpsimd.tensor_tensor(xb[:, p, :, :], x_all[:, ds(b * TT, TT), :],
                                                lnrow[:, 1, :].unsqueeze(1).broadcast_to([P, TT, D]), ALU.add)\
                            .then_inc(xb_ready, 1)

            pool.wait_ge(w["B_ready"], W_B)
            take_v(0, 0)
            each_batch(pool, batch)
            power(B - 1)
            finish(B - 1, 1)

        @block.tensor
        def _(pe):
            pe.wait_ge(consts_ready, CONSTS)
            pe.wait_ge(w["split_small"], 3)

            def turn_x(b, p):
                here = isinstance(b, int) and b < 2
                if not here:
                    pe.wait_ge(x_in_ready[p], (b - p) * 8)
                for t in range(TT):
                    rows = x_all[:, b * TT + t, :] if here else x_in[:, p, t, :]
                    last = nc.tensor.transpose(ps_side[:, t * P:(t + 1) * P], rows, ident[:, :])
                last.then_inc(x_turned, 1)

            def qkv(b, t):
                if t == 0:
                    pe.wait_ge(xTl_ready, b + 1)
                else:
                    pe.wait_ge(lo_ready, 2 * b + t)
                a, s = ps_side[:, 0:SC], slice(t * P, (t + 1) * P)
                nc.tensor.matmul(a, xTh[:, s], w["B_wh"][:, :], start=True, stop=False)
                nc.tensor.matmul(a, xTh[:, s], w["B_wl"][:, :], start=False, stop=False)
                nc.tensor.matmul(a, xTl[:, s], w["B_wh"][:, :], start=False, stop=True).then_inc(qkv_made, 1)

            def turn_stack(b, slot, stack):
                if stack is qs:
                    pe.wait_ge(lo_ready, 2 * b + 2)
                else:
                    pe.wait_ge(qsT_ready, b + 1)
                for g in range(G):
                    for t in range(TT):
                        last = nc.tensor.transpose(side_h[:, g * N + t * P:g * N + (t + 1) * P],
                                                   stack[:, t, g * HH:(g + 1) * HH, :].rearrange("p h c -> p (h c)"),
                                                   identh[:, :])
                last.then_inc(stacks_turned, 1)

            def turn_back(b, t):
                if t == 0:
                    pe.wait_ge(oT_ready, 2 * b + 2)
                    if not (isinstance(b, int) and b == 0):
                        pe.wait_ge(back_read, 2 * b)
                else:
                    pe.wait_ge(back_read, 2 * b + t)
                for g in range(G):
                    last = nc.tensor.transpose(ps_side[:, g * P:(g + 1) * P], oT[:, g, t * P:(t + 1) * P], ident[:, :])
                last.then_inc(back_ready, 1)

            def scores(b, p, g):
                n = b * G + g
                if g == 0:
                    pe.wait_ge(qsT_ready, b + 1)
                    pe.wait_ge(ksT_ready, b + 1)
                if not (isinstance(n, int) and n == 0):
                    pe.wait_ge(max_ready, n)
                for hh in range(HH):
                    nc.tensor.matmul(ps_sc[:, hh, 0:SC].rearrange("p (j s) -> p j s", s=P)[:, 0:3:2, :], identb[:, :],
                                     mask[:, :, :], start=True, stop=True, skip_group_check=True)
                for t, (c0, c1) in enumerate(((0, P), (P, SC))):
                    for hh in range(HH):
                        r0 = CH * hh
                        last = nc.tensor.matmul(ps_sc[:, hh, c0:c1], qsT[r0:r0 + CH, p, g, t * P:(t + 1) * P],
                                                ksT[r0:r0 + CH, p, g, 0:c1 - c0], start=False, stop=True,
                                                skip_group_check=True)
                last.then_inc(scores_ready, 1)

            def maxima(n, g):
                pe.wait_ge(max_ready, n + 1)
                pe.wait_ge(st_free, n * HH + 1)
                for t in range(TT):
                    last = nc.tensor.transpose(ps_mx[:, t * P:(t + 1) * P],
                                               negmax[:, g % 2, t, :, :].rearrange("p h f -> p (h f)"), identh[:, :])
                last.then_inc(max_turned, 1)

            def scores_t(n, p, g, heads):
                pe.wait_ge(qmT_ready, n + 1)
                for hh in heads:
                    r0, bank = CH * hh, ps_st[hh % 2]
                    pe.wait_ge(st_free, n * HH + hh + 1)
                    nc.tensor.matmul(bank[:, 0:SC].rearrange("p (j t) -> p j t", t=P)[:, 0:3:2, :],
                                     ksT[r0:r0 + CH, p, g, 0:P], qmT[r0:r0 + CH, g % 2, :], start=True, stop=True)
                    nc.tensor.matmul(bank[:, P:N], ksT[r0:r0 + CH, p, g, P:N], qmT[r0:r0 + CH, g % 2, P:N],
                                     start=True, stop=True).then_inc(st_ready, 1)

            def attend_s0(b, p, g):
                n = b * G + g
                pe.wait_ge(masked, n + 1)
                if g == 0:
                    pe.wait_ge(v_ready, b + 1)
                if g % 2 == 0 and not zero(n):
                    pe.wait_ge(oT_ready, b * (G // 2) + g // 2)
                for hh in range(HH):
                    pr, h = probs[:, g % 2, hh, :], g * HH + hh
                    nc.tensor.matmul(ps_pv[32 * hh:32 * hh + 32, g % 2, :].rearrange("p (j t) -> p j t", t=P),
                                     v[:, p, 0, h, :], pr.rearrange("p (j t) -> p j t", t=P)[:, 0:3:2, :],
                                     start=True, stop=True, skip_group_check=True)

            def attend_s1(b, p, g):
                for hh in range(HH):
                    pr, h = probs[:, g % 2, hh, :], g * HH + hh
                    last = nc.tensor.matmul(ps_pv[32 * hh:32 * hh + 32, g % 2, P:N], v[:, p, 1, h, :], pr[:, P:N],
                                            start=False, stop=True, skip_group_check=True)
                last.then_inc(pv_ready, 1)

            def batch(b, p, first, next1, next2):
                for g in range(G):
                    n = b * G + g
                    maxima(n, g)
                    if g + 1 < G:
                        scores(b, p, g + 1)
                    elif next1:
                        scores(b + 1, 1 - p, 0)
                    if g == 0 and next1:
                        qkv(b + 1, 1)
                    if g == 1 and next1:
                        turn_stack(b + 1, 1 - p, qs)
                    if g == 2 and not first:
                        if next1:
                            pe.wait_ge(ksT_ready, b + 2)
                        turn_back(b - 1, 0)
                    if g == 3 and next2:
                        if not first:
                            pe.wait_ge(back_read, 2 * b)
                        else:
                            pe.wait_ge(ksT_ready, b + 2)
                        turn_x(b + 2, p)
                    scores_t(n, p, g, (0, 1))
                    before = (b, p, g - 1) if g > 0 else (b - 1, 1 - p, G - 1)
                    if g > 0 or not first:
                        attend_s0(*before)
                    scores_t(n, p, g, (2, 3))
                    if g > 0 or not first:
                        attend_s1(*before)
                    if g == 1 and next1:
                        turn_stack(b + 1, 1 - p, ks)
                    if g == 2 and not first:
                        turn_back(b - 1, 1)
                    if g == 3 and next2:
                        qkv(b + 2, 0)

            turn_x(0, 0)
            qkv(0, 0)
            qkv(0, 1)
            pe.wait_ge(slots_set, 10)
            turn_stack(0, 0, qs)
            turn_stack(0, 0, ks)
            scores(0, 0, 0)
            turn_x(1, 1)
            qkv(1, 0)
            each_batch(pe, batch)
            attend_s0(B - 1, 1, G - 1)
            attend_s1(B - 1, 1, G - 1)
            turn_back(B - 1, 0)
            turn_back(B - 1, 1)

        @block.scalar
        def _(act):
            act.sem_inc(st_free, 2)

            def x_hi(b):
                act.wait_ge(x_turned, b + 1)
                nc.scalar.copy(xTh[:, :], ps_side[:, 0:N]).then_inc(xTh_ready, 1)

            def qkv_hi(b, p, t):
                act.wait_ge(qkv_made, 2 * b + t + 1)
                src = ps_side[:, 0:SC].rearrange("p (j h f) -> p j h f", j=3, f=F)
                pair = [P, G * HH, 2, F]
                nc.scalar.mul(qs[:, t, :, 0:2 * F].rearrange("p h (j f) -> p h j f", f=F),
                              src[:, 0, :, :].unsqueeze(2).broadcast_to(pair), 1.0 / 512)
                nc.scalar.mul(ks[:, t, :, 0:CH].rearrange("p h (j f) -> p h j f", f=F)[:, :, 0:3:2, :],
                              src[:, 1, :, :].unsqueeze(2).broadcast_to(pair), 1.0 / 64)
                if t == 0 and not (isinstance(b, int) and b == 0):
                    act.wait_ge(v_ready, b)
                nc.scalar.mul(v_next[:, t, :].rearrange("p (h f) -> p h f", f=F), src[:, 2, :, :], 1.0 / 64)\
                    .then_inc(hi_ready, 1)

            def q_rows(b, p):
                act.wait_ge(stacks_turned, 2 * b + 1)
                nc.scalar.copy(qsT[:, p, :, :].rearrange("p g n -> p (g n)"), side_h).then_inc(qsT_ready, 1)

            def exps(n, g):
                if not (isinstance(n, int) and n < 2):
                    act.wait_ge(pv_ready, n - 1)
                for hh in range(HH):
                    act.wait_ge(st_ready, n * HH + hh + 1)
                    nc.scalar.activation(probs[:, g % 2, hh, :], ps_st[hh % 2][:, 0:SC], ACT.Exp, scale=EXP_SCALE)\
                        .then_inc(st_free, 1)

            def take_pv(b, j):
                act.wait_ge(pv_ready, b * G + 2 * j + 2)
                nc.scalar.copy(oT[:, 2 * j:2 * j + 2, :].rearrange("p g n -> p (g n)"),
                               ps_pv[:, :, :].rearrange("p g n -> p (g n)")).then_inc(oT_ready, 1)

            def batch(b, p, first, next1, next2):
                for g in range(G):
                    if g == 0 and next1:
                        qkv_hi(b + 1, 1 - p, 1)
                    if g == 1 and next1:
                        q_rows(b + 1, 1 - p)
                    if g == 3 and next2:
                        x_hi(b + 2)
                    exps(b * G + g, g)
                    if g == 0 and not first:
                        take_pv(b - 1, 1)
                    if g == 2:
                        if not first:
                            act.wait_ge(back_ready, 2 * b)
                        take_pv(b, 0)
                    if g == 3 and next2:
                        qkv_hi(b + 2, p, 0)

            x_hi(0)
            qkv_hi(0, 0, 0)
            qkv_hi(0, 0, 1)
            q_rows(0, 0)
            x_hi(1)
            qkv_hi(1, 1, 0)
            each_batch(act, batch)
            take_pv(B - 1, 1)

        @block.vector
        def _(dve):
            def x_lo(b):
                dve.wait_ge(xTh_ready, b + 1)
                nc.vector.tensor_tensor(xTl[:, :], ps_side[:, 0:N], xTh[:, :], ALU.subtract).then_inc(xTl_ready, 1)

            def qkv_lo(b, t):
                dve.wait_ge(hi_ready, 2 * b + t + 1)
                src = ps_side[:, 0:SC].rearrange("p (j h f) -> p j h f", j=3, f=F)
                nc.vector.scalar_tensor_tensor(qs[:, t, :, 2 * F:3 * F], src[:, 0, :, :], 1.0 / 512, qs[:, t, :, 0:F],
                                               ALU.mult, ALU.subtract)
                nc.vector.scalar_tensor_tensor(ks[:, t, :, F:2 * F], src[:, 1, :, :], 1.0 / 64, ks[:, t, :, 0:F],
                                               ALU.mult, ALU.subtract).then_inc(lo_ready, 1)

            def k_rows(b, p):
                dve.wait_ge(stacks_turned, 2 * b + 2)
                nc.vector.tensor_copy(ksT[:, p, :, :].rearrange("p g n -> p (g n)"), side_h).then_inc(ksT_ready, 1)

            def row_max(n, g):
                dve.wait_ge(scores_ready, n + 1)
                for t, (c0, c1) in enumerate(((0, P), (P, SC))):
                    last = nc.vector.tensor_reduce(negmax[:, g % 2, t, :, MROW:MROW + 1], ps_sc[:, :, c0:c1],
                                                   AX_X, ALU.max, negate=True)
                last.then_inc(max_ready, 1)

            def add_max(n, p, g):
                if not (isinstance(n, int) and n < 2):
                    dve.wait_ge(st_ready, (n - 1) * HH)
                dve.wait_ge(max_turned, n + 1)
                nc.vector.tensor_tensor(qmT[:, g % 2, :], ps_mx, qsT[:, p, g, :], ALU.add).then_inc(qmT_ready, 1)

            def divide(b, t):
                dve.wait_ge(back_ready, 2 * b + t + 1)
                src = ps_side[:, :].rearrange("p (h f) -> p h f", f=32)
                nc.vector.reciprocal(rsum[:, t, :], src[:, :, F]).then_inc(dve_step, 1)
                dve.wait_ge(dve_step, b * 3 + t + 1)
                nc.vector.tensor_tensor(attn[:, t, :].rearrange("p (h f) -> p h f", f=F), src[:, :, 0:F],
                                        rsum[:, t, :].unsqueeze(2).broadcast_to([P, G * HH, F]), ALU.mult)\
                    .then_inc(back_read, 1)

            def variance(b):
                dve.wait_ge(back_read, 2 * b + 2)
                for t in range(TT):
                    nc.vector.bn_stats(stats[:, t, :], attn[:, t, :])
                dve.drain()
                for t in range(TT):
                    last = nc.vector.bn_aggr(mv[:, t, :], stats[:, t, :])
                last.then_inc(dve_step, 1)
                dve.wait_ge(dve_step, b * 3 + 3)
                nc.vector.tensor_scalar(mv[:, :, 1], mv[:, :, 1], LN_EPS, None, ALU.add).then_inc(var_ready, 1)

            def normalise(b):
                if not (isinstance(b, int) and b == 0):
                    dve.wait_ge(y_ready, b)
                dve.wait_ge(rstd_ready, b + 1)
                for t in range(TT):
                    last = nc.vector.tensor_scalar(z[:, t, :], attn[:, t, :], mv[:, t, 0:1], rstd[:, t:t + 1],
                                                   ALU.subtract, ALU.mult)
                last.then_inc(z_ready, 1)

            def batch(b, p, first, next1, next2):
                for g in range(G):
                    n = b * G + g
                    add_max(n, p, g)
                    if g + 1 < G or next1:
                        row_max(n + 1, (g + 1) % G)
                    if g == 0 and next1:
                        qkv_lo(b + 1, 1)
                    if g == 3 and next2:
                        x_lo(b + 2)
                    if g == 1 and next1:
                        k_rows(b + 1, 1 - p)
                    if g == 2 and not first:
                        divide(b - 1, 0)
                        divide(b - 1, 1)
                        variance(b - 1)
                    if g == 3:
                        if next2:
                            qkv_lo(b + 2, 0)
                        if not first:
                            normalise(b - 1)

            x_lo(0)
            qkv_lo(0, 0)
            qkv_lo(0, 1)
            k_rows(0, 0)
            dve.wait_ge(slots_set, 10)
            row_max(0, 0)
            x_lo(1)
            qkv_lo(1, 0)
            each_batch(dve, batch)
            divide(B - 1, 0)
            divide(B - 1, 1)
            variance(B - 1)
            normalise(B - 1)


def stage_b_experts(nc, c, x_all, y_all, w, ident, consts_ready, mhalf, lnrow):
    E, FF = 8, 4 * D
    TM = BANK // P
    TURNS = TILES // TM
    C = FF // P
    UNITS = E * C
    HF = 4
    SCALE = 1 / W_SCALE

    y_in = c.sb("m_y_in", [P, 2, TM, D])
    xy = c.sb("m_xy", [P, TM, D])
    yT = c.sb("m_yT", [P, BANK])
    yTh = c.sb("m_yTh", [P, 2, BANK], F16)
    yTl = c.sb("m_yTl", [P, 2, BANK], F16)
    lg = c.sb("m_lg", [P, TM, E])
    mx = c.sb("m_mx", [P, TM, 8])
    ix = c.sb("m_ix", [P, TM, 8], U32)
    ixf = c.sb("m_ixf", [P, TM, 2])
    gap = c.sb("m_gap", [P, TM])
    eg = c.sb("m_eg", [P, TM])
    wsum = c.sb("m_wsum", [P, TM])
    wt = c.sb("m_wt", [P, 2, TM])
    pick = c.sb("m_pick", [P, 2, TM, E])
    comb = c.sb("m_comb", [P, 2, TM, E])
    combT = c.sb("m_combT", [E, BANK])
    experts = c.sb("m_experts", [P, E])
    hf = c.sb("m_hf", [P, HF, BANK])
    hh = c.sb("m_hh", [P, 2, C, BANK], F16)
    hl = c.sb("m_hl", [P, 2, C, BANK], F16)
    acc = c.sb("m_acc", [P, 2, TM, D])
    z = c.sb("m_z", [P, TM, D])
    zg = c.sb("m_zg", [P, TM, D])
    rows = c.sb("m_rows", [P, TM, D])
    stats = c.sb("m_stats", [P, TM, 6])
    mv = c.sb("m_mv", [P, TM, 2])
    rstd = c.sb("m_rstd", [P, TM])
    ps_h = [c.ps(f"m_ps_h{j}", [P, BANK]) for j in range(4)]
    ps_eo = [c.ps(f"m_ps_eo{j}", [P, BANK]) for j in range(2)]
    ps_turn = c.ps("m_ps_turn", [P, BANK])
    ps_row = c.ps("m_ps_row", [P, BANK])

    y_in_ready = [c.sem(f"m_y_in_ready{j}") for j in range(2)]
    iota_ready = c.sem("m_iota_ready")
    y_turned = c.sem("m_y_turned")
    yT_ready = c.sem("m_yT_ready")
    yTl_ready = c.sem("m_yTl_ready")
    logits_made = c.sem("m_logits_made")
    logits_read = c.sem("m_logits_read")
    gap_ready = c.sem("m_gap_ready")
    eg_ready = c.sem("m_eg_ready")
    comb_ready = c.sem("m_comb_ready")
    comb_turned = c.sem("m_comb_turned")
    combT_ready = c.sem("m_combT_ready")
    b2_made = c.sem("m_b2_made")
    acc_ready = c.sem("m_acc_ready")
    h_made = c.sem("m_h_made")
    h_free = c.sem("m_h_free")
    hh_ready = c.sem("m_hh_ready")
    hl_ready = c.sem("m_hl_ready")
    eo_ready = c.sem("m_eo_ready")
    eo_free = c.sem("m_eo_free")
    route_step = c.sem("m_route_step")
    mv_ready = c.sem("m_mv_ready")
    var_ready = c.sem("m_var_ready")
    rstd_ready = c.sem("m_rstd_ready")
    z_ready = c.sem("m_z_ready")
    zg_ready = c.sem("m_zg_ready")
    sum_step = c.sem("m_sum_step")
    xy_ready = c.sem("m_xy_ready")
    rows_ready = c.sem("m_rows_ready")
    rows_done = c.sem("m_rows_done")

    def each_turn(eng, body):
        body(0, 0, True, True)
        with eng.Fori(0, (TURNS - 2) // 2) as k:
            body(2 * k + 1, 1, False, True)
            body(2 * k + 2, 0, False, True)
        body(TURNS - 1, 1, False, False)

    def ahead(i, p, e):
        return (i, p, e + 2) if e + 2 < E else (i + 1, 1 - p, e + 2 - E)

    with nc.Block() as block:

        @block.sync
        def _(sp):
            def load(i, p):
                sp.dma_start(y_in[:, p, :, :], y_all[:, ds(i * TM, TM), :]).then_inc(y_in_ready[p], 16)

            load(2, 0)
            load(3, 1)
            with sp.Fori(1, TURNS // 2 - 1) as k:
                for p in range(2):
                    i = 2 * k + p
                    sp.wait_ge(y_turned, i + 1)
                    load(i + 2, p)

        @block.gpsimd
        def _(pool):
            nc.gpsimd.iota(experts[:, :], pattern=[[1, E]], base=0, channel_multiplier=0,
                           allow_small_or_imprecise_dtypes=True).then_inc(iota_ready, 1)

            def lower(i, p, e):
                for j in range(C):
                    n = e * C + j
                    pool.wait_ge(hh_ready, i * UNITS + n + 1)
                    nc.gpsimd.tensor_tensor(hl[:, e % 2, j, :], hf[:, n % HF, :], hh[:, e % 2, j, :], ALU.subtract)\
                        .then_inc(hl_ready, 1)

            def power(i, ln):
                pool.wait_ge(var_ready, 2 * i + ln + 1)
                nc.gpsimd.tensor_tensor(rstd[:, :], mv[:, :, 1], mhalf[:, 0:TM], ALU.pow).then_inc(rstd_ready, 1)

            def add_up(i):
                pool.wait_ge(z_ready, i + 1)
                nc.gpsimd.tensor_tensor(zg[:, :, :], z[:, :, :],
                                        lnrow[:, 2, :].unsqueeze(1).broadcast_to([P, TM, D]), ALU.mult)\
                    .then_inc(zg_ready, 1)
                pool.wait_ge(zg_ready, i + 1)
                nc.gpsimd.tensor_tensor(rows[:, :, :], zg[:, :, :], xy[:, :, :], ALU.add).then_inc(rows_ready, 1)

            def residual(i):
                if not zero(i):
                    pool.wait_ge(rows_ready, i)
                nc.gpsimd.tensor_tensor(xy[:, :, :], x_all[:, ds(i * TM, TM), :], y_all[:, ds(i * TM, TM), :],
                                        ALU.add)\
                    .then_inc(sum_step, 1)

            def residual_bias(i):
                pool.wait_ge(sum_step, i + 1)
                nc.gpsimd.tensor_tensor(xy[:, :, :], xy[:, :, :],
                                        lnrow[:, 3, :].unsqueeze(1).broadcast_to([P, TM, D]), ALU.add)\
                    .then_inc(xy_ready, 1)
                pool.wait_ge(xy_ready, i + 1)

            def turn(i, p, first, more):
                for e in range(E):
                    if e + 2 < E or more:
                        lower(*ahead(i, p, e))
                    if e == 0 and not first:
                        power(i - 1, 0)
                    if e == 1 and not first:
                        add_up(i - 1)
                    if e == 2 and not first:
                        power(i - 1, 1)
                    if e == 6:
                        residual(i)
                    if e == 7:
                        residual_bias(i)

            pool.wait_ge(w["B_ready"], W_B)
            lower(0, 0, 0)
            lower(0, 0, 1)
            each_turn(pool, turn)
            power(TURNS - 1, 0)
            add_up(TURNS - 1)
            power(TURNS - 1, 1)

        @block.tensor
        def _(pe):
            pe.wait_ge(w["B_ready"], W_B)
            pe.wait_ge(w["split"], PIECES)
            pe.wait_ge(consts_ready, CONSTS)

            def turn_y(i, p):
                here = isinstance(i, int) and i < 2
                if not here:
                    pe.wait_ge(y_in_ready[p], (i - p) * 8)
                if not zero(i):
                    pe.wait_ge(combT_ready, i)
                for t in range(TM):
                    rows = y_all[:, i * TM + t, :] if here else y_in[:, p, t, :]
                    last = nc.tensor.transpose(ps_turn[:, t * P:(t + 1) * P], rows, ident[:, :])
                last.then_inc(y_turned, 1)

            def logits(i):
                pe.wait_ge(yT_ready, 2 * i + 1)
                if not zero(i):
                    pe.wait_ge(acc_ready, i)
                for t in range(TM):
                    last = nc.tensor.matmul(ps_row[:, t * E:(t + 1) * E], yT[:, t * P:(t + 1) * P],
                                            w["B_gate"][:, :], start=True, stop=True)
                last.then_inc(logits_made, 1)

            def turn_comb(i, p):
                pe.wait_ge(comb_ready, i + 1)
                pe.wait_ge(yTl_ready, i + 1)
                for t in range(TM):
                    last = nc.tensor.transpose(ps_turn[0:E, t * P:(t + 1) * P], comb[:, p, t, :], ident[:, :])
                last.then_inc(comb_turned, 1)

            def b2_part(i):
                pe.wait_ge(combT_ready, i + 1)
                pe.wait_ge(logits_read, i + 1)
                for t in range(TM):
                    last = nc.tensor.matmul(ps_row[:, t * P:(t + 1) * P], combT[:, t * P:(t + 1) * P],
                                            w["B_b2"][:, :], start=True, stop=True)
                last.then_inc(b2_made, 1)

            def hidden(i, p, e):
                if e == 0:
                    pe.wait_ge(yTl_ready, i + 1)
                for j in range(C):
                    n = e * C + j
                    wh = w["B_W1h"][:, n * P:(n + 1) * P]
                    pe.wait_ge(h_free, i * UNITS + n + 1)
                    nc.tensor.matmul(ps_h[n % 4][:, :], wh, yTh[:, p, :], start=True, stop=False)
                    nc.tensor.matmul(ps_h[n % 4][:, :], wh, yTl[:, p, :], start=False, stop=False)
                    nc.tensor.matmul(ps_h[n % 4][:, :], w["B_W1l"][:, n * P:(n + 1) * P], yTh[:, p, :],
                                     start=False, stop=True).then_inc(h_made, 1)

            def outputs(i, e):
                pe.wait_ge(eo_free, i * E + e + 1)
                pe.wait_ge(hl_ready, i * UNITS + (e + 1) * C)
                for t in range(TM):
                    out = ps_eo[e % 2][:, t * P:(t + 1) * P]
                    for j in range(C):
                        up, low = hh[:, e % 2, j, t * P:(t + 1) * P], hl[:, e % 2, j, t * P:(t + 1) * P]
                        cols = slice((e * C + j) * D, (e * C + j + 1) * D)
                        nc.tensor.matmul(out, up, w["B_W2h"][:, cols], start=(j == 0), stop=False)
                        nc.tensor.matmul(out, up, w["B_W2l"][:, cols], start=False, stop=False)
                        last = nc.tensor.matmul(out, low, w["B_W2h"][:, cols], start=False, stop=(j == C - 1))
                last.then_inc(eo_ready, 1)

            def turn(i, p, first, more):
                for e in range(E):
                    outputs(i, e)
                    if e == 7 and more:
                        turn_comb(i + 1, 1 - p)
                    if e + 2 < E or more:
                        hidden(*ahead(i, p, e))
                    if e == 1 and more:
                        turn_y(i + 1, 1 - p)
                    if e == 2 and more:
                        logits(i + 1)
                    if e == 7 and more:
                        b2_part(i + 1)

            turn_y(0, 0)
            logits(0)
            hidden(0, 0, 0)
            hidden(0, 0, 1)
            turn_comb(0, 0)
            b2_part(0)
            each_turn(pe, turn)

        @block.scalar
        def _(act):
            act.sem_inc(h_free, 4)
            act.wait_ge(w["B_ready"], W_B)
            act.wait_ge(consts_ready, CONSTS)
            nc.scalar.activation(hf[:, 0, 0:1], ident[:, 0:1], ACT.Exp)

            def take_y(i, p):
                act.wait_ge(y_turned, i + 1)
                if not zero(i):
                    act.wait_ge(logits_made, i)
                nc.scalar.copy(yT[:, :], ps_turn[:, :]).then_inc(yT_ready, 1)
                nc.scalar.copy(yTh[:, p, :], ps_turn[:, :]).then_inc(yT_ready, 1)

            def gap_exp(i):
                act.wait_ge(gap_ready, i + 1)
                nc.scalar.activation(eg[:, :], gap[:, :], ACT.Exp).then_inc(eg_ready, 1)

            def take_comb(i):
                act.wait_ge(comb_turned, i + 1)
                if not zero(i):
                    act.wait_ge(b2_made, i)
                nc.scalar.copy(combT[:, :], ps_turn[0:E, :]).then_inc(combT_ready, 1)

            def take_b2(i, p):
                act.wait_ge(b2_made, i + 1)
                if not (isinstance(i, int) and i < 2):
                    act.wait_ge(z_ready, i - 1)
                nc.scalar.mul(acc[:, p, :, :].rearrange("p t d -> p (t d)"), ps_row[:, :], 1 / SCALE)\
                    .then_inc(acc_ready, 1)

            def relu(i, p, e):
                for j in range(C):
                    n = e * C + j
                    act.wait_ge(h_made, i * UNITS + n + 1)
                    if not (zero(i) and n < HF):
                        act.wait_ge(hl_ready, i * UNITS + n + 1 - HF)
                    nc.scalar.activation(hf[:, n % HF, :], ps_h[n % 4][:, :], ACT.Relu,
                                         bias=w["B_b1"][:, n:n + 1], scale=SCALE).then_inc(h_free, 1)

            def turn(i, p, first, more):
                for e in range(E):
                    if e == 4 and more:
                        gap_exp(i + 1)
                    if e == 7 and more:
                        take_comb(i + 1)
                    if e + 2 < E or more:
                        relu(*ahead(i, p, e))
                    if e == 1 and more:
                        take_y(i + 1, 1 - p)
                    if e == 7 and more:
                        take_b2(i + 1, 1 - p)

            take_y(0, 0)
            gap_exp(0)
            relu(0, 0, 0)
            relu(0, 0, 1)
            take_comb(0)
            take_b2(0, 0)
            each_turn(act, turn)

        @block.vector
        def _(dve):
            dve.sem_inc(eo_free, 2)
            dve.wait_ge(iota_ready, 1)

            def y_lower(i, p):
                dve.wait_ge(yT_ready, 2 * i + 2)
                nc.vector.tensor_tensor(yTl[:, p, :], ps_turn[:, :], yTh[:, p, :], ALU.subtract)\
                    .then_inc(yTl_ready, 1)

            def top_two(i):
                dve.wait_ge(logits_made, i + 1)
                nc.vector.tensor_copy(lg[:, :, :].rearrange("p t e -> p (t e)"), ps_row[:, 0:TM * E])\
                    .then_inc(logits_read, 1)
                dve.drain()
                for t in range(TM):
                    nc.vector.max(mx[:, t, :], lg[:, t, :])
                dve.drain()
                for t in range(TM):
                    nc.vector.max_index(ix[:, t, :], mx[:, t, :], lg[:, t, :])
                nc.vector.tensor_tensor(gap[:, :], mx[:, :, 1], mx[:, :, 0], ALU.subtract).then_inc(gap_ready, 1)
                dve.drain()
                nc.vector.tensor_copy(ixf[:, :, :], ix[:, :, 0:2])

            def combine(i, p):
                dve.wait_ge(eg_ready, i + 1)
                nc.vector.tensor_scalar(wsum[:, :], eg[:, :], 1.0, 1 / SCALE, ALU.add, ALU.mult).then_inc(route_step, 1)
                dve.wait_ge(route_step, i * 4 + 1)
                nc.vector.reciprocal(wt[:, 0, :], wsum[:, :]).then_inc(route_step, 1)
                dve.wait_ge(route_step, i * 4 + 2)
                nc.vector.tensor_tensor(wt[:, 1, :], eg[:, :], wt[:, 0, :], ALU.mult).then_inc(route_step, 1)
                dve.wait_ge(route_step, i * 4 + 3)
                for s in range(2):
                    for t in range(TM):
                        last = nc.vector.tensor_scalar(pick[:, s, t, :], experts[:, :], ixf[:, t, s:s + 1],
                                                       wt[:, s, t:t + 1], ALU.is_equal, ALU.mult)
                last.then_inc(route_step, 1)
                dve.wait_ge(route_step, i * 4 + 4)
                nc.vector.tensor_tensor(comb[:, p, :, :], pick[:, 0, :, :], pick[:, 1, :, :], ALU.add)\
                    .then_inc(comb_ready, 1)

            def upper(i, p, e):
                for j in range(C):
                    n = e * C + j
                    dve.wait_ge(h_free, 4 + i * UNITS + n + 1)
                    nc.vector.tensor_copy(hh[:, e % 2, j, :], hf[:, n % HF, :]).then_inc(hh_ready, 1)

            def accumulate(i, p, e):
                if e == 0:
                    dve.wait_ge(acc_ready, i + 1)
                dve.wait_ge(eo_ready, i * E + e + 1)
                for t in range(TM):
                    last = nc.vector.scalar_tensor_tensor(acc[:, p, t, :], ps_eo[e % 2][:, t * P:(t + 1) * P],
                                                          comb[:, p, t, e:e + 1], acc[:, p, t, :],
                                                          ALU.mult, ALU.add)
                last.then_inc(eo_free, 1)
                dve.wait_ge(eo_free, 2 + i * E + e + 1)

            def variance(i, ln, src):
                row_variance(dve, nc, src, stats, mv, TM, mv_ready, 2 * i + ln + 1, var_ready)

            def normalise_mixture(i, p):
                dve.wait_ge(rstd_ready, 2 * i + 1)
                row_normalise(nc, acc[:, p, :, :], mv, rstd, TM, lambda t: z[:, t, :]).then_inc(z_ready, 1)

            def rows_variance(i):
                dve.wait_ge(rows_ready, i + 1)
                variance(i, 1, rows)

            def normalise_rows(i):
                dve.wait_ge(rstd_ready, 2 * i + 2)
                row_normalise(nc, rows, mv, rstd, TM,
                              lambda t: x_all[:, ds(i * TM + t, 1), :].squeeze(1)).then_inc(rows_done, 1)

            def turn(i, p, first, more):
                for e in range(E):
                    accumulate(i, p, e)
                    if e + 2 < E or more:
                        upper(*ahead(i, p, e))
                    if not first:
                        if e == 0:
                            variance(i - 1, 0, acc[:, 1 - p, :, :])
                        if e == 1:
                            normalise_mixture(i - 1, 1 - p)
                        if e == 2:
                            rows_variance(i - 1)
                        if e == 3:
                            normalise_rows(i - 1)
                    if more:
                        if e == 1:
                            y_lower(i + 1, 1 - p)
                        if e == 3:
                            top_two(i + 1)
                        if e == 5:
                            combine(i + 1, 1 - p)

            y_lower(0, 0)
            top_two(0)
            upper(0, 0, 0)
            combine(0, 0)
            upper(0, 0, 1)
            each_turn(dve, turn)
            variance(TURNS - 1, 0, acc[:, 1, :, :])
            normalise_mixture(TURNS - 1, 1)
            rows_variance(TURNS - 1)
            normalise_rows(TURNS - 1)
            dve.wait_ge(rows_done, TURNS)


def stage_c(nc, c, x_all, w, ident, consts_ready, mhalf):
    VB = DH + 1
    SC = 3 * P
    SCALE = 1 / W_SCALE
    HALF = HD // BANK
    QK = PAIRS
    V = TT * HALF
    PROJ = QK + 2 * V
    ACT_FREES = QK + V
    assert PROJ == 2 * PAIRS

    x_in = c.sb("c_x_in", [P, 2, TT, D])
    xTh = c.sb("c_xTh", [P, 2, N], F16)
    xTl = c.sb("c_xTl", [P, 2, N], F16)
    qT = c.sb("c_qT", [P, 2, PAIRS, N])
    kT = c.sb("c_kT", [P, 2, PAIRS, N])
    vh = c.sb("c_vh", [P, 2, TT, H, VB], F16)
    vl = c.sb("c_vl", [P, 2, TT, H, VB], F16)
    gate = c.sb("c_gate", [P, 2, TT, HD])
    ex = c.sb("c_exp", [P, 2, BANK])
    re = c.sb("c_relu", [P, 2, BANK])
    sc = c.sb("c_sc", [P, 2, 2, 2, SC], F16)
    turn_mark = c.sb("c_turn_mark", [P, PAIRS + 1])
    den = c.sb("c_den", [P, PAIRS, TT * 2])
    rden = c.sb("c_rden", [P, PAIRS, TT * 2])
    o = c.sb("c_o", [P, 2, TT, P])
    og = c.sb("c_og", [P, 2, TT, P])
    ogh = c.sb("c_ogh", [P, 2, TT, HD], F16)
    ogl = c.sb("c_ogl", [P, 2, TT, HD], F16)
    oT = c.sb("c_oT", [P, TT, 2, 2, BANK], F16)
    identh = c.sb("c_identh", [P, P], F16)
    rows = c.sb("c_rows", [P, TT, D])
    stats = c.sb("c_stats", [P, TT, 6])
    mv = c.sb("c_mv", [P, TT, 2])
    rstd = c.sb("c_rstd", [P, TT])
    ps_proj = [c.ps(f"c_ps_proj{j}", [P, BANK]) for j in range(2)]
    ps_sc = [c.ps(f"c_ps_sc{j}", [P, BANK]) for j in range(2)]
    ps_att = [c.ps(f"c_ps_att{j}", [P, BANK]) for j in range(2)]
    ps_turn = c.ps("c_ps_turn", [P, BANK])
    ps_out = c.ps("c_ps_out", [P, TT, D])

    x_in_ready = [c.sem(f"c_x_in_ready{j}") for j in range(2)]
    x_turned = c.sem("c_x_turned")
    slots_set = c.sem("c_slots_set")
    xTh_ready = c.sem("c_xTh_ready")
    xTl_ready = c.sem("c_xTl_ready")
    proj_ready = c.sem("c_proj_ready")
    proj_free = c.sem("c_proj_free")
    feat_free = c.sem("c_feat_free")
    vh_ready = c.sem("c_vh_ready")
    vl_ready = c.sem("c_vl_ready")
    sc_ready = c.sem("c_sc_ready")
    sc_hi = c.sem("c_sc_hi")
    sc_lo = c.sem("c_sc_lo")
    sc_masked = c.sem("c_sc_masked")
    att_ready = c.sem("c_att_ready")
    att_free = c.sem("c_att_free")
    gated = c.sem("c_gated")
    ogh_ready = c.sem("c_ogh_ready")
    ogl_ready = c.sem("c_ogl_ready")
    o_turned = c.sem("c_o_turned")
    oT_ready = c.sem("c_oT_ready")
    out_ready = c.sem("c_out_ready")
    out_used = c.sem("c_out_used")
    den_step = c.sem("c_den_step")
    mv_ready = c.sem("c_mv_ready")
    rows_done = c.sem("c_rows_done")
    var_ready = c.sem("c_var_ready")
    rstd_ready = c.sem("c_rstd_ready")

    def o_bank(b, k):
        bank = ps_proj[0] if isinstance(b, int) and b == B - 1 and k % 2 else ps_turn
        return bank[:, :].bitcast(F16)

    with nc.Block() as block:

        @block.sync
        def _(sp):
            def load(b, p):
                sp.dma_start(x_in[:, p, :, :], x_all[:, ds(b * TT, TT), :]).then_inc(x_in_ready[p], 16)

            load(2, 0)
            load(3, 1)
            with sp.Fori(1, B // 2 - 1) as i:
                for p in range(2):
                    b = 2 * i + p
                    sp.wait_ge(x_turned, b + 1)
                    load(b + 2, p)

        @block.gpsimd
        def _(pool):
            nc.gpsimd.memset(vh[:, :, :, :, DH:VB], 1.0).then_inc(slots_set, 1)
            nc.gpsimd.memset(vl[:, :, :, :, DH:VB], 0.0).then_inc(slots_set, 1)
            nc.gpsimd.memset(turn_mark[:, :], 1.0).then_inc(slots_set, 1)
            pool.wait_ge(consts_ready, CONSTS)
            nc.gpsimd.tensor_copy(identh[:, :], ident[:, :]).then_inc(slots_set, 1)
            pool.wait_ge(slots_set, 4)

            def og_lo(b, p, m):
                pool.wait_ge(ogh_ready, b * PAIRS + m + 1)
                at = slice(m * P, (m + 1) * P)
                nc.gpsimd.tensor_tensor(ogl[:, p, :, at], og[:, m % 2, :, :], ogh[:, p, :, at], ALU.subtract)\
                    .then_inc(ogl_ready, 1)

            def batch(b, p, first, next1, next2):
                for m in range(PAIRS):
                    pool.wait_ge(sc_lo, 2 + b * H + 2 * m + 2)
                    nc.gpsimd.tensor_tensor(turn_mark[:, m:m + 1], turn_mark[:, PAIRS:PAIRS + 1],
                                            turn_mark[:, PAIRS:PAIRS + 1], ALU.mult)
                    diag = sc[:, m % 2, :, :, :].rearrange("p l h t -> p (l h) t")[:, :, 0:2 * P]
                    nc.gpsimd.affine_select(out=diag, in_=diag, compare_op=ALU.is_ge, fill=0.0, base=0,
                                            pattern=[[0, 4], [0, 2], [1, P]], channel_multiplier=-1)\
                        .then_inc(sc_masked, 1)
                    if m > 0:
                        og_lo(b, p, m - 1)
                    elif not first:
                        og_lo(b - 1, 1 - p, PAIRS - 1)
                    if m == 7 and not first:
                        power(b - 1)

            def power(b):
                pool.wait_ge(var_ready, b + 1)
                nc.gpsimd.tensor_tensor(rstd[:, :], mv[:, :, 1], mhalf[:, 0:TT], ALU.pow).then_inc(rstd_ready, 1)

            each_batch(pool, batch)
            og_lo(B - 1, 1, PAIRS - 1)
            power(B - 1)

        @block.tensor
        def _(pe):
            pe.wait_ge(consts_ready, CONSTS)
            pe.wait_ge(w["split"], PIECES)
            pe.wait_ge(w["split_small"], 3)

            def turn_x(b, p):
                here = isinstance(b, int) and b < 2
                if not here:
                    pe.wait_ge(x_in_ready[p], (b - p) * 8)
                for t in range(TT):
                    rows = x_all[:, b * TT + t, :] if here else x_in[:, p, t, :]
                    last = nc.tensor.transpose(ps_turn[:, t * P:(t + 1) * P], rows, ident[:, :])
                last.then_inc(x_turned, 1)

            def halves(out, lhs_h, lhs_l, rhs_h, rhs_l):
                nc.tensor.matmul(out, lhs_h, rhs_h, start=True, stop=False)
                nc.tensor.matmul(out, lhs_h, rhs_l, start=False, stop=False)
                return nc.tensor.matmul(out, lhs_l, rhs_h, start=False, stop=True)

            def bank_used(b, u):
                if u < 2:
                    if not zero(b):
                        pe.wait_ge(proj_free, (b - 1) * ACT_FREES + ACT_FREES - 1 + u)
                elif u - 2 < QK:
                    pe.wait_ge(proj_free, b * ACT_FREES + u - 1)
                elif u - 2 < QK + V:
                    pe.wait_ge(vl_ready, b * V + u - 2 - QK + 1)
                else:
                    pe.wait_ge(proj_free, b * ACT_FREES + u - 2 - V + 1)

            def project(b, p, u):
                if u == 0:
                    pe.wait_ge(xTl_ready, b + 1)
                bank_used(b, u)
                bank = ps_proj[u % 2]
                if u < QK:
                    for s in range(2):
                        c0 = (u % 2) * HD + (2 * (u // 2) + s) * P
                        last = halves(bank[:, s * N:(s + 1) * N], w["C_wh"][:, c0:c0 + P], w["C_wl"][:, c0:c0 + P],
                                      xTh[:, p, :], xTl[:, p, :])
                else:
                    t, h = divmod((u - QK) % V, HALF)
                    c0 = (2 + (u - QK) // V) * HD + h * BANK
                    s = slice(t * P, (t + 1) * P)
                    last = halves(bank[:, :], xTh[:, p, s], xTl[:, p, s], w["C_wh"][:, c0:c0 + BANK],
                                  w["C_wl"][:, c0:c0 + BANK])
                last.then_inc(proj_ready, 1)

            def scores(b, p, m):
                if m == 0:
                    pe.wait_ge(feat_free, 2 + b * QK + QK)
                for s in range(2):
                    pe.wait_ge(sc_lo, b * H + 2 * m + s + 1)
                for s in range(2):
                    r0 = DH * s
                    nc.tensor.matmul(ps_sc[s][:, 0:SC].rearrange("p (j t) -> p j t", t=P)[:, 0:3:2, :],
                                     kT[r0:r0 + DH, p, m, 0:P], qT[r0:r0 + DH, p, m, :], start=True, stop=True)
                    nc.tensor.matmul(ps_sc[s][:, P:N], kT[r0:r0 + DH, p, m, P:N], qT[r0:r0 + DH, p, m, P:N],
                                     start=True, stop=True).then_inc(sc_ready, 1)

            def attend(b, p, m):
                if m == 0:
                    pe.wait_ge(vl_ready, b * V + V)
                pe.wait_ge(sc_masked, b * PAIRS + m + 1)
                pe.wait_ge(att_free, b * PAIRS + m + 1)
                for s in range(2):
                    hd, a = 2 * m + s, sc[:, m % 2, :, s, :]
                    for t, blocks in enumerate((((0, 0),), ((0, 2), (1, 1)))):
                        out = ps_att[m % 2][:, (2 * t + s) * VB:(2 * t + s + 1) * VB]
                        terms = [(sb, j, ah, vv) for sb, j in blocks for ah, vv in ((0, vh), (0, vl), (1, vh))]
                        for n, (sb, j, ah, vv) in enumerate(terms):
                            last = nc.tensor.matmul(out, a[:, ah, j * P:(j + 1) * P], vv[:, p, sb, hd, :],
                                                    start=(n == 0), stop=(n == len(terms) - 1))
                last.then_inc(att_ready, 1)

            def turn_o(b, p, k):
                t, half = divmod(k, 2)
                last_batch = isinstance(b, int) and b == B - 1
                if k == 0 or last_batch and k == 1:
                    pe.wait_ge(ogl_ready, b * PAIRS + PAIRS)
                    pe.wait_ge(xTl_ready, min(b + 3, B) if isinstance(b, int) else b + 3)
                else:
                    pe.wait_ge(oT_ready, b * 4 + k - (1 if last_batch else 0))
                bank = o_bank(b, k)
                for l, src in enumerate((ogh, ogl)):
                    for j in range(4):
                        m = 4 * half + j
                        last = nc.tensor.transpose(bank[:, l * BANK + j * P:l * BANK + (j + 1) * P],
                                                   src[:, p, t, m * P:(m + 1) * P], identh[:, :])
                last.then_inc(o_turned, 1)

            def out_part(b, k):
                t, half = divmod(k, 2)
                pe.wait_ge(oT_ready, b * 4 + k + 1)
                if k == 0 and not zero(b):
                    pe.wait_ge(out_used, b)
                out = ps_out[:, t, :]
                for j in range(4):
                    m, at = 4 * half + j, slice(j * P, (j + 1) * P)
                    nc.tensor.matmul(out, oT[:, t, half, 0, at], w["C_oh"][:, m, :], start=(m == 0), stop=False)
                    nc.tensor.matmul(out, oT[:, t, half, 0, at], w["C_ol"][:, m, :], start=False, stop=False)
                    last = nc.tensor.matmul(out, oT[:, t, half, 1, at], w["C_oh"][:, m, :],
                                            start=False, stop=(m == PAIRS - 1))
                if k == 3:
                    last.then_inc(out_ready, 1)

            def batch(b, p, first, next1, next2):
                for m in range(PAIRS):
                    if m + 1 < PAIRS:
                        scores(b, p, m + 1)
                    elif next1:
                        scores(b + 1, 1 - p, 0)
                    if next1:
                        project(b + 1, 1 - p, 2 * m)
                    if not first and 2 <= m < 6:
                        out_part(b - 1, m - 2)
                    attend(b, p, m)
                    if not first and 1 <= m < 5:
                        turn_o(b - 1, 1 - p, m - 1)
                    if next1:
                        project(b + 1, 1 - p, 2 * m + 1)
                    if m == 5 and next2:
                        if not first:
                            pe.wait_ge(oT_ready, 4 * b)
                        turn_x(b + 2, p)

            turn_x(0, 0)
            for u in range(PROJ):
                project(0, 0, u)
            turn_x(1, 1)
            pe.wait_ge(slots_set, 4)
            scores(0, 0, 0)
            each_batch(pe, batch)
            turn_o(B - 1, 1, 0)
            for k in range(4):
                if k < 3:
                    turn_o(B - 1, 1, k + 1)
                out_part(B - 1, k)

        @block.scalar
        def _(act):

            def x_hi(b, p):
                act.wait_ge(x_turned, b + 1)
                if not (isinstance(b, int) and b < 2):
                    act.wait_ge(proj_ready, (b - 1) * PROJ)
                nc.scalar.copy(xTh[:, p, :], ps_turn[:, 0:N]).then_inc(xTh_ready, 1)

            def take(b, p, u):
                bank = ps_proj[u % 2]
                act.wait_ge(proj_ready, b * PROJ + u + 1)
                if u < QK:
                    act.wait_ge(feat_free, b * QK + u + 1)
                    nc.scalar.activation(ex[:, u % 2, :], bank[:, :], ACT.Exp, scale=SCALE)
                    nc.scalar.activation(re[:, u % 2, :], bank[:, :], ACT.Relu, scale=SCALE).then_inc(proj_free, 1)
                    return
                kind, r = divmod(u - QK, V)
                t, h = divmod(r, HALF)
                if kind == 0:
                    nc.scalar.mul(vh[:, p, t, 8 * h:8 * h + 8, 0:DH], bank[:, :].rearrange("p (m e) -> p m e", e=DH),
                                  SCALE).then_inc(vh_ready, 1)
                else:
                    if r == 0 and not (isinstance(b, int) and b < 2):
                        act.wait_ge(gated, (b - 1) * PAIRS)
                    nc.scalar.activation(gate[:, p, t, h * BANK:(h + 1) * BANK], bank[:, :], ACT.Tanh,
                                         scale=0.5 * SCALE).then_inc(proj_free, 1)

            def score_hi(b, h):
                if h % 2 == 0 and not (zero(b) and h < 4):
                    act.wait_ge(att_ready, b * PAIRS + h // 2 - 1)
                act.wait_ge(sc_ready, b * H + h + 1)
                nc.scalar.mul(sc[:, (h // 2) % 2, 0, h % 2, :], ps_sc[h % 2][:, 0:SC], SCALE).then_inc(sc_hi, 1)

            def take_o(b, k):
                t, half = divmod(k, 2)
                if k == 0 and not zero(b):
                    act.wait_ge(out_ready, b)
                act.wait_ge(o_turned, b * 4 + k + 1)
                nc.scalar.copy(oT[:, t, half, :, :].rearrange("p l q -> p (l q)"), o_bank(b, k))\
                    .then_inc(oT_ready, 1)

            def og_hi(b, p, m):
                if m == 0 and not (isinstance(b, int) and b < 2):
                    act.wait_ge(o_turned, 4 * (b - 1))
                act.wait_ge(gated, b * PAIRS + m + 1)
                nc.scalar.copy(ogh[:, p, :, m * P:(m + 1) * P], og[:, m % 2, :, :]).then_inc(ogh_ready, 1)

            def batch(b, p, first, next1, next2):
                for m in range(PAIRS):
                    if m + 1 < PAIRS:
                        score_hi(b, 2 * m + 2)
                        score_hi(b, 2 * m + 3)
                    elif next1:
                        score_hi(b + 1, 0)
                        score_hi(b + 1, 1)
                    if next1:
                        take(b + 1, 1 - p, 2 * m)
                    if m > 0:
                        og_hi(b, p, m - 1)
                    elif not first:
                        og_hi(b - 1, 1 - p, PAIRS - 1)
                    if not first and 1 <= m < 5:
                        take_o(b - 1, m - 1)
                    if next1:
                        take(b + 1, 1 - p, 2 * m + 1)
                    if m == 5 and next2:
                        x_hi(b + 2, p)

            x_hi(0, 0)
            for u in range(PROJ):
                take(0, 0, u)
            x_hi(1, 1)
            score_hi(0, 0)
            score_hi(0, 1)
            each_batch(act, batch)
            og_hi(B - 1, 1, PAIRS - 1)
            for k in range(4):
                take_o(B - 1, k)

        @block.vector
        def _(dve):
            dve.sem_inc(feat_free, 2)
            dve.sem_inc(sc_lo, 2)
            dve.sem_inc(att_free, 2)

            def x_lo(b, p):
                dve.wait_ge(xTh_ready, b + 1)
                nc.vector.tensor_tensor(xTl[:, p, :], ps_turn[:, 0:N], xTh[:, p, :], ALU.subtract)\
                    .then_inc(xTl_ready, 1)

            def take(b, p, u):
                if u < QK:
                    out = (qT, kT)[u % 2][:, p, 2 * (u // 2):2 * (u // 2) + 2, :].rearrange("p m q -> p (m q)")
                    dve.wait_ge(proj_free, b * ACT_FREES + u + 1)
                    nc.vector.scalar_tensor_tensor(out, ex[:, u % 2, :], 1.0, re[:, u % 2, :], ALU.min, ALU.add)\
                        .then_inc(feat_free, 1)
                elif u < QK + V:
                    t, h = divmod(u - QK, HALF)
                    dve.wait_ge(vh_ready, b * V + u - QK + 1)
                    heads = slice(8 * h, 8 * h + 8)
                    nc.vector.scalar_tensor_tensor(vl[:, p, t, heads, 0:DH],
                                                   ps_proj[u % 2][:, :].rearrange("p (m e) -> p m e", e=DH), SCALE,
                                                   vh[:, p, t, heads, 0:DH], ALU.mult, ALU.subtract)\
                        .then_inc(vl_ready, 1)

            def score_lo(b, h):
                dve.wait_ge(sc_hi, b * H + h + 1)
                nc.vector.scalar_tensor_tensor(sc[:, (h // 2) % 2, 1, h % 2, :], ps_sc[h % 2][:, 0:SC], SCALE,
                                               sc[:, (h // 2) % 2, 0, h % 2, :], ALU.mult, ALU.subtract)\
                    .then_inc(sc_lo, 1)

            def divide(b, m):
                dve.wait_ge(att_ready, b * PAIRS + m + 1)
                src = ps_att[m % 2][:, 0:4 * VB].rearrange("p (g e) -> p g e", e=VB)
                nc.vector.tensor_scalar(den[:, m, :], src[:, :, DH], 1e-6 * SCALE, 2.0, ALU.add, ALU.mult)\
                    .then_inc(den_step, 1)
                dve.wait_ge(den_step, b * 2 * PAIRS + 2 * m + 1)
                nc.vector.reciprocal(rden[:, m, :], den[:, m, :]).then_inc(den_step, 1)
                dve.wait_ge(den_step, b * 2 * PAIRS + 2 * m + 2)
                nc.vector.tensor_tensor(
                    o[:, m % 2, :, :].rearrange("p t (s e) -> p t s e", s=2),
                    src[:, :, 0:DH].rearrange("p (t s) e -> p t s e", t=TT),
                    rden[:, m, :].rearrange("p (t s) -> p t s", t=TT).unsqueeze(3).broadcast_to([P, TT, 2, DH]),
                    ALU.mult).then_inc(att_free, 1)

            def apply_gate(b, p, m):
                if m == 0:
                    dve.wait_ge(proj_free, b * ACT_FREES + ACT_FREES)
                dve.wait_ge(att_free, 2 + b * PAIRS + m + 1)
                if not (zero(b) and m < 2):
                    dve.wait_ge(ogl_ready, b * PAIRS + m - 1)
                nc.vector.scalar_tensor_tensor(og[:, m % 2, :, :], gate[:, p, :, m * P:(m + 1) * P], 1.0,
                                               o[:, m % 2, :, :], ALU.add, ALU.mult).then_inc(gated, 1)

            def add_residual(b):
                if not zero(b):
                    dve.wait_ge(rows_done, b)
                dve.wait_ge(out_ready, b + 1)
                nc.vector.scalar_tensor_tensor(rows[:, :, :], ps_out[:, :, :], SCALE, x_all[:, ds(b * TT, TT), :],
                                               ALU.mult, ALU.add)\
                    .then_inc(out_used, 1)

            def variance(b):
                dve.wait_ge(out_used, b + 1)
                row_variance(dve, nc, rows, stats, mv, TT, mv_ready, b + 1, var_ready)

            def normalise(b):
                dve.wait_ge(rstd_ready, b + 1)
                row_normalise(nc, rows, mv, rstd, TT,
                              lambda t: x_all[:, ds(b * TT + t, 1), :].squeeze(1)).then_inc(rows_done, 1)

            def batch(b, p, first, next1, next2):
                for m in range(PAIRS):
                    if m + 1 < PAIRS:
                        score_lo(b, 2 * m + 2)
                        score_lo(b, 2 * m + 3)
                    elif next1:
                        score_lo(b + 1, 0)
                        score_lo(b + 1, 1)
                    if next1 and 0 < m <= QK // 2:
                        take(b + 1, 1 - p, 2 * m - 1)
                    if next1 and m >= QK // 2:
                        take(b + 1, 1 - p, 2 * m)
                    divide(b, m)
                    if next1:
                        take(b + 1, 1 - p, 2 * m if m < QK // 2 else 2 * m + 1)
                    apply_gate(b, p, m)
                    if m == 5 and next2:
                        x_lo(b + 2, p)
                    if m == 6 and not first:
                        add_residual(b - 1)
                        variance(b - 1)
                    if m == 7 and not first:
                        normalise(b - 1)

            x_lo(0, 0)
            for u in range(PROJ):
                take(0, 0, u)
            x_lo(1, 1)
            score_lo(0, 0)
            score_lo(0, 1)
            each_batch(dve, batch)
            add_residual(B - 1)
            variance(B - 1)
            normalise(B - 1)
            dve.wait_ge(rows_done, B)


def stage_d(nc, c, x_all, out, w, ident, ones_row, consts_ready, mhalf, stored):
    TM = BANK // P
    TURNS = TILES // TM
    C = 4
    MAGIC = 1.5 * 2.0 ** 23

    x_in = c.sb("d_x_in", [P, 2, TM, D])
    xTh = c.sb("d_xTh", [P, 2, BANK], F16)
    xTl = c.sb("d_xTl", [P, 2, BANK], F16)
    h = c.sb("d_h", [P, 2, C, BANK])
    rows = c.sb("d_rows", [P, TM, D])
    final = c.sb("d_final", [P, 2, TM, D])
    stats = c.sb("d_stats", [P, TM, 6])
    mv = c.sb("d_mv", [P, TM, 2])
    rstd = c.sb("d_rstd", [P, TM])
    total = c.sb("d_total", [P, 2])
    scale = c.sb("d_scale", [P, 2])
    rscale = c.sb("d_rscale", [P, 2])
    ones = c.sb("d_ones", [P, P])
    tern = c.sb("d_tern", [P, 2, BANK])
    wt1 = c.sb("d_wt1", [P, BANK], F16)
    wt2 = c.sb("d_wt2", [P, BANK])
    ps_x = c.ps("d_ps_x", [P, BANK])
    ps_h = [c.ps(f"d_ps_h{j}", [P, BANK]) for j in range(4)]
    ps_out = [c.ps(f"d_ps_out{j}", [P, TM, D]) for j in range(2)]
    ps_sum = c.ps("d_ps_sum", [P, 2])

    x_in_ready = [c.sem(f"d_x_in_ready{j}") for j in range(2)]
    x_turned = c.sem("d_x_turned")
    xTh_ready = c.sem("d_xTh_ready")
    xTl_ready = c.sem("d_xTl_ready")
    ones_set = c.sem("d_ones_set")
    total_ready = c.sem("d_total_ready")
    sum_ready = c.sem("d_sum_ready")
    tern_step = c.sem("d_tern_step")
    wt_ready = c.sem("d_wt_ready")
    h_made = c.sem("d_h_made")
    h_ready = c.sem("d_h_ready")
    out_ready = c.sem("d_out_ready")
    out_used = c.sem("d_out_used")
    mv_ready = c.sem("d_mv_ready")
    var_ready = c.sem("d_var_ready")
    rstd_ready = c.sem("d_rstd_ready")
    final_ready = c.sem("d_final_ready")

    def each_turn(eng, body):
        for i in range(2):
            body(i, i, True, True)
        with eng.Fori(1, TURNS // 2 - 1) as k:
            for p in range(2):
                body(2 * k + p, p, True, True)
        for p in range(2):
            body(TURNS - 2 + p, p, p == 0, False)

    with nc.Block() as block:

        @block.sync
        def _(sp):
            def load(i, p):
                sp.dma_start(x_in[:, p, :, :], x_all[:, ds(i * TM, TM), :]).then_inc(x_in_ready[p], 16)

            load(2, 0)
            load(3, 1)
            with sp.Fori(1, TURNS // 2 - 1) as k:
                for p in range(2):
                    i = 2 * k + p
                    sp.wait_ge(x_turned, i + 1)
                    load(i + 2, p)

        @block.gpsimd
        def _(pool):
            nc.gpsimd.memset(ones[:, :], 1.0).then_inc(ones_set, 1)
            out_rows = out.rearrange("b n d -> (b n) d")
            with pool.Fori(0, TURNS // 2) as k:
                for p in range(2):
                    i = 2 * k + p
                    pool.wait_ge(var_ready, i + 1)
                    nc.gpsimd.tensor_tensor(rstd[:, :], mv[:, :, 1], mhalf[:, 0:TM], ALU.pow).then_inc(rstd_ready, 1)
                    pool.wait_ge(final_ready, i + 1)
                    pool.dma_start(out_rows[ds(i * BANK, BANK), :].rearrange("(t p) d -> p t d", p=P),
                                   final[:, p, :, :]).then_inc(stored[p], 16)

        @block.tensor
        def _(pe):
            pe.wait_ge(consts_ready, CONSTS)
            pe.wait_ge(w["D_ready"], W_D)

            def turn_x(i, p):
                here = isinstance(i, int) and i < 2
                if not here:
                    pe.wait_ge(x_in_ready[p], (i - p) * 8)
                if not zero(i):
                    pe.wait_ge(xTl_ready, i)
                for t in range(TM):
                    rows = x_all[:, i * TM + t, :] if here else x_in[:, p, t, :]
                    last = nc.tensor.transpose(ps_x[:, t * P:(t + 1) * P], rows, ident[:, :])
                last.then_inc(x_turned, 1)

            def hidden(i, p):
                pe.wait_ge(xTl_ready, i + 1)
                for j in range(C):
                    if not zero(i):
                        pe.wait_ge(h_ready, (i - 1) * C + j + 1)
                    nc.tensor.matmul(ps_h[j][:, :], wt1[:, j * P:(j + 1) * P], xTh[:, p, :], start=True, stop=False)
                    nc.tensor.matmul(ps_h[j][:, :], wt1[:, j * P:(j + 1) * P], xTl[:, p, :], start=False, stop=True)\
                        .then_inc(h_made, 1)

            def outputs(i, p):
                if not (isinstance(i, int) and i < 2):
                    pe.wait_ge(out_used, i - 1)
                pe.wait_ge(h_ready, i * C + C)
                for t in range(TM):
                    for j in range(C):
                        nc.tensor.matmul(ps_out[p][:, t, :], h[:, p, j, t * P:(t + 1) * P], wt2[:, j * P:(j + 1) * P],
                                         start=(j == 0), stop=False)
                    last = nc.tensor.matmul(ps_out[p][:, t, :], ones_row[:, :], w["D_b2"][:, :],
                                            start=False, stop=True)
                last.then_inc(out_ready, 1)

            def turn(i, p, next1, next2):
                if next1:
                    hidden(i + 1, 1 - p)
                if next2:
                    turn_x(i + 2, p)
                outputs(i, p)

            turn_x(0, 0)
            pe.wait_ge(ones_set, 1)
            pe.wait_ge(total_ready, 1)
            nc.tensor.matmul(ps_sum[:, :], ones[:, :], total[:, :], start=True, stop=True).then_inc(sum_ready, 1)
            turn_x(1, 1)
            pe.wait_ge(wt_ready, 1)
            hidden(0, 0)
            pe.wait_ge(wt_ready, 2)
            each_turn(pe, turn)

        @block.scalar
        def _(act):
            act.wait_ge(w["D_ready"], W_D)

            def x_hi(i, p):
                act.wait_ge(x_turned, i + 1)
                if not (isinstance(i, int) and i < 2):
                    act.wait_ge(h_made, (i - 1) * C)
                nc.scalar.copy(xTh[:, p, :], ps_x[:, :]).then_inc(xTh_ready, 1)

            def gelu(i, p):
                if not (isinstance(i, int) and i < 2):
                    act.wait_ge(out_ready, i - 1)
                for j in range(C):
                    act.wait_ge(h_made, i * C + j + 1)
                    nc.scalar.activation(h[:, p, j, :], ps_h[j][:, :], ACT.Gelu, bias=w["D_b1"][:, j:j + 1])\
                        .then_inc(h_ready, 1)

            def turn(i, p, next1, next2):
                if next1:
                    gelu(i + 1, 1 - p)
                if next2:
                    x_hi(i + 2, p)

            x_hi(0, 0)
            x_hi(1, 1)
            gelu(0, 0)
            each_turn(act, turn)

        @block.vector
        def _(dve):
            dve.wait_ge(w["D_ready"], W_D)
            for j in range(2):
                last = nc.vector.tensor_reduce(total[:, j:j + 1], w[f"D_W{j + 1}"][:, :], AX_X, ALU.add,
                                               apply_absolute_value=True)
            last.then_inc(total_ready, 1)
            dve.wait_ge(sum_ready, 1)
            n = 0

            def step(ins):
                nonlocal n
                n += 1
                ins.then_inc(tern_step, 1)
                dve.wait_ge(tern_step, n)

            def x_lo(i, p):
                dve.wait_ge(xTh_ready, i + 1)
                nc.vector.tensor_tensor(xTl[:, p, :], ps_x[:, :], xTh[:, p, :], ALU.subtract).then_inc(xTl_ready, 1)

            def finish(i, p):
                dve.wait_ge(out_ready, i + 1)
                if not zero(i):
                    dve.wait_ge(final_ready, i)
                nc.vector.tensor_tensor(rows[:, :, :], ps_out[p][:, :, :], x_all[:, ds(i * TM, TM), :], ALU.add)\
                    .then_inc(out_used, 1)
                dve.wait_ge(out_used, i + 1)
                row_variance(dve, nc, rows, stats, mv, TM, mv_ready, i + 1, var_ready)
                if not (isinstance(i, int) and i < 2):
                    dve.wait_ge(stored[p], (i - p) * 8)
                dve.wait_ge(rstd_ready, i + 1)
                row_normalise(nc, rows, mv, rstd, TM, lambda t: final[:, p, t, :]).then_inc(final_ready, 1)

            def turn(i, p, next1, next2):
                if next2:
                    x_lo(i + 2, p)
                finish(i, p)

            step(nc.vector.tensor_scalar(scale[:, :], ps_sum[:, :], 1.0 / (4 * D * D), 1e-8, ALU.mult, ALU.max))
            step(nc.vector.reciprocal(rscale[:, :], scale[:, :]))
            x_lo(0, 0)
            for j, wt in enumerate((wt1, wt2)):
                src, t = w[f"D_W{j + 1}"][:, :], tern[:, j, :]
                step(nc.vector.tensor_scalar(t, src, rscale[:, j:j + 1], None, ALU.mult))
                step(nc.vector.tensor_scalar(t, t, MAGIC, None, ALU.add))
                step(nc.vector.tensor_scalar(t, t, -MAGIC, None, ALU.add))
                step(nc.vector.tensor_scalar(t, t, -1.0, 1.0, ALU.max, ALU.min))
                step(nc.vector.tensor_tensor(t, t, src, ALU.subtract))
                nc.vector.tensor_tensor(wt[:, :], src, t, ALU.add).then_inc(wt_ready, 1)
                if j == 0:
                    x_lo(1, 1)
            each_turn(dve, turn)


CONSTS = 4
W_SCALE = 64.0
PIECE = 1024
PIECES = 3 * 4
W_A = 16 * 2
W_B = 16 * 7
W_C = 16
W_D = 16 * 4


def load_small_weights(eng, a, w, wa):
    eng.dma_start(w["B_gate"][:, :], a["L0_ffn_gate_W"]).then_inc(w["B_ready"], 16)
    for j, n in enumerate(("ln1_g", "ln1_b", "ln2_g", "ln2_b")):
        eng.dma_start(w["B_lnrow"][:, j, :], a["L0_ffn_" + n].partition_broadcast(P)).then_inc(w["B_ready"], 16)
    eng.dma_start(w["B_b1"][:, :], a["L0_ffn_b1"]).then_inc(w["B_ready"], 16)
    eng.dma_start(w["B_b2"][:, :], a["L0_ffn_b2"]).then_inc(w["B_ready"], 16)
    eng.dma_start(wa["C_out"][:, :, :], a["L1_attn_w_out"].rearrange("(m p) n -> p m n", p=P))\
        .then_inc(w["C_ready"], 16)
    eng.dma_start(w["D_W1"][:, :], a["L1_ffn_W1"]).then_inc(w["D_ready"], 16)
    eng.dma_start(w["D_W2"][:, :].rearrange("p (j d) -> p j d", d=D),
                  a["L1_ffn_W2"].rearrange("(j p) d -> p j d", p=P)).then_inc(w["D_ready"], 16)
    eng.dma_start(w["D_b1"][:, :], a["L1_ffn_b1"]).then_inc(w["D_ready"], 16)
    eng.dma_start(w["D_b2"][:, :], a["L1_ffn_b2"].rearrange("(a n) -> a n", a=1)).then_inc(w["D_ready"], 16)


def weight_piece(a, n, slot):
    kind, j = divmod(n, 4)
    if kind == 0:
        return slot.rearrange("p (e f) -> p e f", e=2), a["L0_ffn_W1"][2 * j:2 * j + 2].rearrange("e p f -> p e f")
    if kind == 1:
        return (slot.rearrange("p (n d) -> p n d", d=D),
                a["L0_ffn_W2"][2 * j:2 * j + 2].rearrange("e (j p) d -> p (e j) d", p=P))
    return slot, (a["L1_attn_w_qkv"][:, j * PIECE:(j + 1) * PIECE] if j < 3 else a["L1_attn_w_gate"])


def two_blocks(nc, a, out):
    with ExitStack() as stack:
        Chip.given.clear()
        c = Chip(nc, stack)
        x_all = c.sb("x_all", [P, TILES, D])
        ident = c.sb("ident", [P, P])
        ones_row = c.sb("ones_row", [1, P])
        mhalf = c.sb("mhalf", [P, 8])
        consts_ready = c.sem("consts_ready")
        consts_step = c.sem("consts_step")

        w = {"split": c.sem("w_split"), "split_small": c.sem("w_split_small"),
             "B_ready": c.sem("B_ready"), "C_ready": c.sem("C_ready"), "D_ready": c.sem("D_ready")}
        for half in "hl":
            w[half] = c.sb("w_" + half, [P, PIECES * PIECE], F16)
            for j, name in enumerate(("B_W1", "B_W2", "C_w")):
                w[name + half] = w[half][:, 4 * j * PIECE:4 * (j + 1) * PIECE]
        w["C_oh"] = c.sb("C_oh", [P, PAIRS, D], F16)
        w["C_ol"] = c.sb("C_ol", [P, PAIRS, D], F16)
        w["D_W1"] = c.sb("D_W1", [P, 4 * D])
        w["D_W2"] = c.sb("D_W2", [P, 4 * D])
        w["D_b1"] = c.sb("D_b1", [P, 4])
        w["D_b2"] = c.sb("D_b2", [1, D])

        b_stack = stack.enter_context(ExitStack())
        b_mem = Chip(nc, b_stack)
        for half in "hl":
            w["B_w" + half] = b_mem.sb("B_w" + half, [P, 3 * D], F16)
        w["B_gate"] = b_mem.sb("B_gate", [P, 8])
        w["B_b1"] = b_mem.sb("B_b1", [P, 32])
        w["B_b2"] = b_mem.sb("B_b2", [8, D])
        lnrow = w["B_lnrow"] = b_mem.sb("B_lnrow", [P, 4, D])

        a_stack = stack.enter_context(ExitStack())
        a_mem = Chip(nc, a_stack)
        wa = {"ready": a_mem.sem("A_ready"), "o": a_mem.sb("A_wo", [P, PAIRS, D]), "bo": a_mem.sb("A_bo", [1, D]),
              "C_out": a_mem.sb("C_out", [P, PAIRS, D])}

        with nc.Block() as block:

            @block.gpsimd
            def _(pool):
                nc.gpsimd.memset(ident[:, :], 0.0).then_inc(consts_step, 1)
                nc.gpsimd.memset(ones_row[:, :], 1.0).then_inc(consts_ready, 1)
                nc.gpsimd.memset(mhalf[:, :], -0.5).then_inc(consts_ready, 1)
                pool.wait_ge(consts_step, 1)
                nc.gpsimd.affine_select(out=ident[:, :], in_=ident[:, :], compare_op=ALU.not_equal, fill=1.0,
                                        base=0, pattern=[[-1, P]], channel_multiplier=1).then_inc(consts_ready, 2)

        def stage(f, *args):
            with ExitStack() as inner:
                f(nc, Chip(nc, inner), *args)

        stage(stage_a, a, x_all, w, wa, ident, mhalf, consts_ready)
        a_stack.close()
        y_all = b_mem.sb("y_all", [P, TILES, D])
        stage(stage_b_attention, x_all, y_all, w, ident, consts_ready, mhalf, lnrow)
        stage(stage_b_experts, x_all, y_all, w, ident, consts_ready, mhalf, lnrow)
        b_stack.close()
        stage(stage_c, x_all, w, ident, consts_ready, mhalf)
        stored = [c.sem(f"stored{j}") for j in range(2)]
        stage(stage_d, x_all, out, w, ident, ones_row, consts_ready, mhalf, stored)
        with nc.Block() as block:
            @block.sync
            def _(sp):
                for s in stored:
                    sp.wait_ge(s, 16 * TILES // 8)


_INS = ['L0_attn_x', 'L0_attn_Wq', 'L0_attn_Wk', 'L0_attn_Wv', 'L0_attn_Wo', 'L0_attn_bo',
        'L0_ffn_Wq', 'L0_ffn_Wk', 'L0_ffn_Wv', 'L0_ffn_gate_W', 'L0_ffn_W1', 'L0_ffn_b1', 'L0_ffn_W2', 'L0_ffn_b2',
        'L0_ffn_ln1_g', 'L0_ffn_ln1_b', 'L0_ffn_ln2_g', 'L0_ffn_ln2_b',
        'L1_attn_w_qkv', 'L1_attn_w_gate', 'L1_attn_w_out', 'L1_ffn_W1', 'L1_ffn_b1', 'L1_ffn_W2', 'L1_ffn_b2']
_OUTS = [((B, N, D), 'float32')]


def kernel(**inputs):
    import numpy as _np
    import concourse.bacc as _bacc
    from concourse import mybir as _mybir
    from concourse.bass_utils import run_bass_kernel_spmd as _run

    nc = _bacc.Bacc("TRN2", target_bir_lowering=False, num_devices=1)
    arrays, args = {}, {}
    for name in _INS:
        a = _np.asarray(inputs[name])
        if name in ('L0_ffn_Wq', 'L0_ffn_Wk', 'L0_ffn_Wv'):
            a = a.transpose(1, 0, 2)
        if name in ('L1_ffn_W1', 'L1_ffn_W2'):
            a = a.T
        if name in ('L0_ffn_b1', 'L1_ffn_b1'):
            a = a.reshape(-1, 128).T
        a = _np.ascontiguousarray(a)
        arrays[f"in_{name}_dram"] = a
        args[name] = nc.dram_tensor(f"in_{name}_dram", a.shape, _mybir.dt.from_np(a.dtype), kind="ExternalInput").ap()
    shape, dtype = _OUTS[0]
    out = nc.dram_tensor("out_0_dram", shape, _mybir.dt.from_np(_np.dtype(dtype)), kind="ExternalOutput").ap()
    two_blocks(nc, args, out)
    r = _run(nc, [arrays], core_ids=[0])
    return r.results[0]["out_0_dram"]
```
